# Optimizing a Trainium2 kernel written in Bass

```python
import numpy as np
import jax
import jax.numpy as jnp

def _softmax(x, axis=-1):
    return jax.nn.softmax(x, axis=axis)

def _gelu(x):
    return jax.nn.gelu(x, approximate=True)

def _silu(x):
    return jax.nn.silu(x)

def _sigmoid(x):
    return jax.nn.sigmoid(x)

def _layernorm(x, axis=-1, eps=1e-05):
    m = jnp.mean(x, axis=axis, keepdims=True)
    v = jnp.var(x, axis=axis, keepdims=True)
    return (x - m) / jnp.sqrt(v + eps)

def _scatter_add(tgt, idx, src, axis=0):
    return tgt.at[idx].add(src)

def _segment_sum(src, seg, n):
    return jax.ops.segment_sum(src, seg, n)
kernel_name = 'mk_prb_d2_jaxref_r8_97765e'

def setup_inputs(seed: int=0):
    np.random.seed(seed)
    _w = jnp.asarray

    def _L0_attn_setup():
        import jax, jax.numpy as jnp
        import numpy as np
        D_MODEL = 128
        N_HEADS = 16
        HEAD_DIM = D_MODEL // N_HEADS
        LORA_RANK = 16
        LORA_SCALING = 1.0 / LORA_RANK

        def lora_linear(x, w, a, b):
            return x @ w.T + LORA_SCALING * (x @ a.T @ b.T)
        key = jax.random.key(seed)
        ks = jax.random.split(key, 14)
        B, S = (4, 256)

        def w(k, shape, scale=0.02):
            return jax.random.normal(k, shape, dtype=jnp.float32) * scale
        inp = {'x': jax.random.normal(ks[0], (B, S, D_MODEL), dtype=jnp.float32), 'wq': w(ks[1], (D_MODEL, D_MODEL)), 'aq': w(ks[2], (LORA_RANK, D_MODEL)), 'bq': w(ks[3], (D_MODEL, LORA_RANK)), 'wk': w(ks[4], (D_MODEL, D_MODEL)), 'ak': w(ks[5], (LORA_RANK, D_MODEL)), 'bk': w(ks[6], (D_MODEL, LORA_RANK)), 'wv': w(ks[7], (D_MODEL, D_MODEL)), 'av': w(ks[8], (LORA_RANK, D_MODEL)), 'bv': w(ks[9], (D_MODEL, LORA_RANK)), 'wo': w(ks[10], (D_MODEL, D_MODEL)), 'ao': w(ks[11], (LORA_RANK, D_MODEL)), 'bo': w(ks[12], (D_MODEL, LORA_RANK))}
        return inp
    _L0_attn_in = _L0_attn_setup()

    def _L0_ffn_setup():
        import jax, jax.numpy as jnp
        import numpy as np
        B, S, D = (1, 256, 128)
        E, F, TOP_K = (8, 512, 2)
        key = jax.random.key(seed)
        k0, k1, k2, k3, k4 = jax.random.split(key, 5)
        s = 0.02
        x = jax.random.normal(k0, (B, S, D), jnp.float32)
        Wr = jax.random.normal(k1, (D, E), jnp.float32) * s
        W1 = jax.random.normal(k2, (E, D, F), jnp.float32) * s
        W3 = jax.random.normal(k3, (E, D, F), jnp.float32) * s
        W2 = jax.random.normal(k4, (E, F, D), jnp.float32) * s
        return {'x': x, 'Wr': Wr, 'W1': W1, 'W2': W2, 'W3': W3}
    _L0_ffn_in = _L0_ffn_setup()

    def _L1_attn_setup():
        import jax, jax.numpy as jnp
        from jax import lax
        import numpy as np

        def log_g(x):
            return jnp.where(x >= 0, jnp.log(jnp.maximum(x, 0) + 0.5), -jax.nn.softplus(-x))
        key = jax.random.key(seed)
        k1, k2, k3, k4 = jax.random.split(key, 4)
        B, T, D, E = (8, 256, 128, 256)
        x = jax.random.normal(k1, (B, T, D), dtype=jnp.float32)
        W = jax.random.normal(k2, (3 * E, D), dtype=jnp.float32) * (1.0 / np.sqrt(D))
        b = jax.random.normal(k3, (3 * E,), dtype=jnp.float32) * 0.02
        Wd = jax.random.normal(k4, (D, E), dtype=jnp.float32) * (1.0 / np.sqrt(E))
        return {'x': x, 'W': W, 'b': b, 'Wd': Wd}
    _L1_attn_in = _L1_attn_setup()

    def _L1_ffn_setup():
        import jax, jax.numpy as jnp
        import numpy as np
        TOP_K = 2
        key = jax.random.key(seed)
        ks = jax.random.split(key, 7)
        E, D, F = (8, 128, 512)
        B, S = (4, 256)
        s_in = 1.0 / np.sqrt(D)
        s_ff = 1.0 / np.sqrt(F)
        return {'x': jax.random.normal(ks[0], (B, S, D), jnp.float32), 'gate_w': jax.random.normal(ks[1], (D, E), jnp.float32) * s_in, 'gate_b': jax.random.normal(ks[2], (E,), jnp.float32) * 0.01, 'w1': jax.random.normal(ks[3], (E, D, F), jnp.float32) * s_in, 'b1': jax.random.normal(ks[4], (E, F), jnp.float32) * 0.01, 'w2': jax.random.normal(ks[5], (E, F, D), jnp.float32) * s_ff, 'b2': jax.random.normal(ks[6], (E, D), jnp.float32) * 0.01}
    _L1_ffn_in = _L1_ffn_setup()
    _d = {'L0_attn_x': _L0_attn_in['x'], 'L0_attn_wq': _L0_attn_in['wq'], 'L0_attn_aq': _L0_attn_in['aq'], 'L0_attn_bq': _L0_attn_in['bq'], 'L0_attn_wk': _L0_attn_in['wk'], 'L0_attn_ak': _L0_attn_in['ak'], 'L0_attn_bk': _L0_attn_in['bk'], 'L0_attn_wv': _L0_attn_in['wv'], 'L0_attn_av': _L0_attn_in['av'], 'L0_attn_bv': _L0_attn_in['bv'], 'L0_attn_wo': _L0_attn_in['wo'], 'L0_attn_ao': _L0_attn_in['ao'], 'L0_attn_bo': _L0_attn_in['bo'], 'L0_ffn_Wr': _L0_ffn_in['Wr'], 'L0_ffn_W1': _L0_ffn_in['W1'], 'L0_ffn_W2': _L0_ffn_in['W2'], 'L0_ffn_W3': _L0_ffn_in['W3'], 'L1_attn_W': _L1_attn_in['W'], 'L1_attn_b': _L1_attn_in['b'], 'L1_attn_Wd': _L1_attn_in['Wd'], 'L1_ffn_gate_w': _L1_ffn_in['gate_w'], 'L1_ffn_gate_b': _L1_ffn_in['gate_b'], 'L1_ffn_w1': _L1_ffn_in['w1'], 'L1_ffn_b1': _L1_ffn_in['b1'], 'L1_ffn_w2': _L1_ffn_in['w2'], 'L1_ffn_b2': _L1_ffn_in['b2']}
    _x0 = _d['L0_attn_x']
    _d['L0_attn_x'] = jax.random.normal(jax.random.fold_in(jax.random.key(seed), 1), (4, 1024, 128), dtype=_x0.dtype)
    del _x0
    return _d

def reference(L0_attn_x, L0_attn_wq, L0_attn_aq, L0_attn_bq, L0_attn_wk, L0_attn_ak, L0_attn_bk, L0_attn_wv, L0_attn_av, L0_attn_bv, L0_attn_wo, L0_attn_ao, L0_attn_bo, L0_ffn_Wr, L0_ffn_W1, L0_ffn_W2, L0_ffn_W3, L1_attn_W, L1_attn_b, L1_attn_Wd, L1_ffn_gate_w, L1_ffn_gate_b, L1_ffn_w1, L1_ffn_b1, L1_ffn_w2, L1_ffn_b2):

    def _L0_attn_ref(x, wq, aq, bq, wk, ak, bk, wv, av, bv, wo, ao, bo):
        import jax, jax.numpy as jnp
        import numpy as np
        D_MODEL = 128
        N_HEADS = 16
        HEAD_DIM = D_MODEL // N_HEADS
        LORA_RANK = 16
        LORA_SCALING = 1.0 / LORA_RANK

        def lora_linear(x, w, a, b):
            return x @ w.T + LORA_SCALING * (x @ a.T @ b.T)
        B, S, _ = x.shape

        def split_heads(t):
            return t.reshape(B, S, N_HEADS, HEAD_DIM).transpose(0, 2, 1, 3)
        q = split_heads(lora_linear(x, wq, aq, bq))
        k = split_heads(lora_linear(x, wk, ak, bk))
        v = split_heads(lora_linear(x, wv, av, bv))
        scores = jnp.einsum('bhqd,bhkd->bhqk', q, k) / jnp.sqrt(jnp.float32(HEAD_DIM))
        causal = jnp.tril(jnp.ones((S, S), dtype=bool))
        scores = jnp.where(causal, scores, -jnp.inf)
        attn = jax.nn.softmax(scores, axis=-1)
        ctx = jnp.einsum('bhqk,bhkd->bhqd', attn, v)
        ctx = ctx.transpose(0, 2, 1, 3).reshape(B, S, D_MODEL)
        return lora_linear(ctx, wo, ao, bo)

    def _L0_ffn_ref(x, Wr, W1, W2, W3):
        import jax, jax.numpy as jnp
        import numpy as np
        B, S, D = (1, 256, 128)
        E, F, TOP_K = (8, 512, 2)
        b, s, d = x.shape
        e = Wr.shape[1]
        xt = x.reshape(b * s, d)
        logits = xt @ Wr
        top_v, top_i = jax.lax.top_k(logits, TOP_K)
        probs = jax.nn.softmax(top_v, axis=-1)
        combine = jnp.sum(probs[..., None] * jax.nn.one_hot(top_i, e, dtype=xt.dtype), axis=1)
        h = jnp.einsum('td,edf->etf', xt, W1)
        g = jnp.einsum('td,edf->etf', xt, W3)
        y = jnp.einsum('etf,efd->etd', jax.nn.silu(h) * g, W2)
        out = jnp.einsum('etd,te->td', y, combine)
        return out.reshape(b, s, d)

    def _L1_attn_ref(x, W, b, Wd):
        import jax, jax.numpy as jnp
        from jax import lax
        import numpy as np

        def log_g(x):
            return jnp.where(x >= 0, jnp.log(jnp.maximum(x, 0) + 0.5), -jax.nn.softplus(-x))
        k = jnp.einsum('btd,ed->bte', x, W) + b
        k_f, k_i, k_h = jnp.split(k, 3, axis=-1)
        log_f = -jax.nn.softplus(-k_f)
        log_i = -jax.nn.softplus(-k_i)
        log_tilde_h = log_g(k_h)
        B, T, E = log_f.shape
        log_h0 = jnp.full((B, 1, E), jnp.log(jnp.asarray(0.5, dtype=x.dtype)), dtype=x.dtype)
        a_star = jnp.pad(jnp.cumsum(log_f, axis=1), ((0, 0), (1, 0), (0, 0)))
        log_values = jnp.concatenate([log_h0, log_i + log_tilde_h], axis=1)
        log_h0_plus_b_star = lax.associative_scan(jnp.logaddexp, log_values - a_star, axis=1)
        h_t = jnp.exp(a_star + log_h0_plus_b_star)[:, 1:]
        return jnp.einsum('bte,de->btd', h_t, Wd)

    def _L1_ffn_ref(x, gate_w, gate_b, w1, b1, w2, b2):
        import jax, jax.numpy as jnp
        import numpy as np
        TOP_K = 2
        B, S, D = x.shape
        E = gate_b.shape[0]
        flat = x.reshape(-1, D)
        T = flat.shape[0]
        logits = flat @ gate_w + gate_b
        probs = jax.nn.softmax(logits, axis=-1)
        top_p, top_i = jax.lax.top_k(probs, TOP_K)
        top_w = top_p / (jnp.sum(top_p, axis=-1, keepdims=True) + 1e-09)
        rows = jnp.arange(T)[:, None]
        comb = jnp.zeros((T, E), dtype=flat.dtype).at[rows, top_i].add(top_w)
        out = jnp.zeros_like(flat)
        for e in range(E):
            h = jax.nn.gelu(flat @ w1[e] + b1[e], approximate=False)
            y = h @ w2[e] + b2[e]
            out = out + comb[:, e:e + 1] * y
        return out.reshape(B, S, D)
    x = L0_attn_x
    xn = _layernorm(x, axis=-1)
    x = x + _L0_attn_ref(xn, L0_attn_wq, L0_attn_aq, L0_attn_bq, L0_attn_wk, L0_attn_ak, L0_attn_bk, L0_attn_wv, L0_attn_av, L0_attn_bv, L0_attn_wo, L0_attn_ao, L0_attn_bo) + _L0_ffn_ref(xn, L0_ffn_Wr, L0_ffn_W1, L0_ffn_W2, L0_ffn_W3)
    xn = _layernorm(x, axis=-1)
    x = x + _L1_attn_ref(xn, L1_attn_W, L1_attn_b, L1_attn_Wd) + _L1_ffn_ref(xn, L1_ffn_gate_w, L1_ffn_gate_b, L1_ffn_w1, L1_ffn_b1, L1_ffn_w2, L1_ffn_b2)
    return x

_drawn_inputs = setup_inputs


def setup_inputs(seed=0):
    import zlib

    import numpy as np

    out = dict(_drawn_inputs(seed))
    spreads = {}
    factors = {'L0_attn_wq': 8.0,
     'L0_attn_aq': 8.0,
     'L0_attn_bq': 8.0,
     'L0_attn_wk': 8.0,
     'L0_attn_ak': 8.0,
     'L0_attn_bk': 8.0,
     'L0_attn_wv': 4.101,
     'L0_attn_av': 8.0,
     'L0_attn_bv': 8.0,
     'L0_attn_wo': 4.459,
     'L0_attn_ao': 8.0,
     'L0_attn_bo': 8.0,
     'L0_ffn_Wr': 8.425,
     'L1_attn_b': 3.998,
     'L1_ffn_b1': 8.0,
     'L1_ffn_b2': 8.0,
     'L0_ffn_W1': 2.99,
     'L0_ffn_W2': 2.838,
     'L0_ffn_W3': 2.811,
     'L1_ffn_gate_b': 2.687}
    for name, (base, spread) in spreads.items():
        noise = np.random.default_rng([zlib.crc32(name.encode()), seed]).standard_normal(out[name].shape)
        drawn = base * np.exp(spread * noise) if base else spread * noise
        out[name] = jnp.asarray(drawn.astype(out[name].dtype))
    for name, factor in factors.items():
        out[name] = (out[name] * factor).astype(out[name].dtype)
    return out
```

```python
from contextlib import ExitStack

import concourse.bass as bass
import concourse.mybir as mybir
import numpy as np

F32 = mybir.dt.float32
F32R = mybir.dt.float32r
BF16 = mybir.dt.bfloat16
I32 = mybir.dt.int32
ALU = mybir.AluOpType
ACT = mybir.ActivationFunctionType
AX = mybir.AxisListType.X

P = 128
D = 128
BATCH, SEQ = 4, 1024
TOKENS = BATCH * SEQ
TT = TOKENS // P
TPB = SEQ // P
CHUNK = 512
NCH = TOKENS // CHUNK
TPC = CHUNK // P
HEADS, HD = 16, 8
GROUPS, HPG = 4, 4
NIT = GROUPS * BATCH
EXPERTS, FF, TOPK = 8, 512, 2
FC = FF // P
SLOT_TILES = TOPK * TOKENS // P + EXPERTS - 1
ROW = D + 2
SKIP = float(1 << 20)
BIG = 3.0e38
LORA_RANK = 16
RNN_E = 256
RC = RNN_E // P
EPS = 1e-5
MASKED = -1.0e30

C_ID, C_MASK, C_TRI, C_ONES, C_RMASK = 0, 128, 256, 384, 512
C_PRIO = C_RMASK + TT * EXPERTS
C_IOTA = C_PRIO + EXPERTS
C_HEAD = C_IOTA + SLOT_TILES
C_TOK2 = C_HEAD + HPG
C_PART = C_TOK2 + TT
C_END = C_PART + SLOT_TILES


def constants():
    c = np.zeros((P, C_END), np.float32)
    c[:, C_ID:C_ID + P] = np.eye(P)
    c[:, C_MASK:C_MASK + P] = np.triu(np.full((P, P), MASKED), 1)
    c[:, C_TRI:C_TRI + P] = np.triu(np.ones((P, P)), 1)
    c[:, C_ONES:C_ONES + P] = 1.0
    c[:, C_RMASK:C_PRIO] = np.tile(np.arange(TT) > 0, EXPERTS)
    c[:, C_PRIO:C_IOTA] = EXPERTS - np.arange(EXPERTS)
    c[:, C_IOTA:C_HEAD] = np.arange(SLOT_TILES)
    c[:, C_HEAD:C_TOK2] = np.arange(P)[:, None] // 32 == np.arange(HPG)[None]
    c[:, C_TOK2:C_PART] = 2 * (np.arange(TT)[None] * P + np.arange(P)[:, None])
    c[:, C_PART:] = np.arange(SLOT_TILES)[None] * P + np.arange(P)[:, None]
    return c


def program(nc, x, consts, w_cat, lora_a, lora_b, wo_t, W1, W2, W3, rnn_w, rnn_b, rnn_wd,
            gate_w, gate_b, w1, b1, w2, b2, out):
    xs = [nc.dram_tensor(f"sorted_rows_{l}", (SLOT_TILES * P, ROW), F32).ap() for l in range(2)]
    yc = [nc.dram_tensor(f"expert_rows_{l}", (TOPK * TOKENS, D), F32).ap() for l in range(2)]

    ctx = ExitStack()
    with ctx:
        base = (nc.sbuf_base + 63) // 64 * 64
        total = 212736
        ctx.enter_context(nc.sbuf_tensor("arena", [P, total // 4], F32))
        names = [0]

        def at(name, off, shape, dt=F32):
            n = int(np.prod(shape)) * (2 if dt == BF16 else 4)
            assert off + n <= total, (name, off, n)
            names[0] += 1
            return nc.alloc_sbuf_tensor_at(name, [P] + list(shape), dt, offset=base + off)

        pos_ = [0]

        def keep(name, shape, dt=F32):
            t = at(name, pos_[0], shape, dt)
            pos_[0] += (int(np.prod(shape)) * (2 if dt == BF16 else 4) + 31) // 32 * 32
            return t

        xres = keep("xres", [TT, D])
        rows = keep("rows", [TT, ROW])
        cst = keep("cst", [C_END])
        ident_b = keep("ident_b", [P], BF16)
        mask_b = keep("mask_b", [P], BF16)
        gate_wt = keep("gate_wt", [TOPK, TT])
        slot_i = keep("slot_i", [TOPK, TT], I32)
        tile_expert = keep("tile_expert", [SLOT_TILES], I32)
        wo_sb = keep("wo_sb", [D])
        bn6 = keep("bn6", [8, 6])
        mv = keep("mv", [8, 2])
        rs = keep("rs", [8])
        rt = keep("rt", [8])
        sd = keep("sd", [8])
        small = keep("small", [12, EXPERTS])
        smalli = keep("smalli", [EXPERTS], I32)
        gbias = keep("gbias", [EXPERTS])
        gw_sb = keep("gw_sb", [EXPERTS])
        gwh = keep("gwh", [EXPERTS], F32R)
        gwl = keep("gwl", [EXPERTS], F32R)
        rnn_bias = keep("rnn_bias", [3 * RC])
        rnn_bh = keep("rnn_bh", [RC])
        destf = keep("destf", [4], I32)
        negm = keep("negm", [HPG, TPB])
        negh = keep("negh", [HPG, TPB], F32R)
        mall = keep("mall", [HPG, TPB])
        mtwo = keep("mtwo", [HPG, TPB // 2, 2])
        recip = keep("recip", [2, TPC, HPG])
        Z = (pos_[0] + 63) // 64 * 64

        ident = cst[:, C_ID:C_ID + P]
        prio = cst[:, C_PRIO:C_PRIO + EXPERTS]

        kz = [at(f"kz{i}", Z + 16384 * i, [HPG, SEQ], F32R) for i in range(2)]
        QK = at("QK", Z + 32768, [2, NIT, TPB * HPG, HD])
        Vn = at("Vn", Z + 65536, [NIT, TPB, HPG * HD])
        qs = [at(f"qs{i}", Z + 81920 + 4096 * i, [SEQ], F32R) for i in range(2)]
        qm = [at(f"qm{i}", Z + 90112 + 4096 * i, [SEQ], F32R) for i in range(2)]
        tq = [at(f"tq{i}", Z + 98304 + 4096 * i, [TPB * HPG, 32]) for i in range(2)]
        tk = [at(f"tk{i}", Z + 106496 + 4096 * i, [TPB * HPG, 32]) for i in range(2)]
        Vs = [at(f"Vs{i}", Z + 114688 + 4096 * i, [TPB, HPG, 32]) for i in range(2)]
        pT = at("pT", Z + 122880, [8, SEQ])
        oT = at("oT", Z + 155648, [SEQ])
        xh = at("xh", Z, [TOKENS], F32R)
        xl = at("xl", Z + 16384, [TOKENS], F32R)
        NW = 3 * D + EXPERTS
        wraw = at("wraw", Z + 81920, [NW])
        wh = at("wh", Z + 81920 + 2048, [NW], F32R)
        wl = at("wl", Z + 81920 + 4096, [NW], F32R)
        wo_raw = at("wo_raw", Z + 81920 + 6144, [D])
        la = at("la", Z + 81920 + 8192, [4 * D])
        lb = at("lb", Z + 81920 + 10240, [4 * D])
        pad_rows = at("pad_rows", Z + 81920 + 12288, [ROW])
        R0 = Z + 114688
        lg = at("lg", R0, [TT, EXPERTS])
        ra = at("ra", R0 + 1024, [TT, EXPERTS])
        rb = at("rb", R0 + 2048, [TT, EXPERTS])
        ch0 = at("ch0", R0 + 3072, [TT, EXPERTS])
        ch1 = at("ch1", R0 + 4096, [TT, EXPERTS])
        cnt = at("cnt", R0 + 5120, [EXPERTS, TT])
        run = at("run", R0 + 6144, [EXPERTS, TT])
        tcmp = at("tcmp", R0 + 7168, [SLOT_TILES, EXPERTS])
        r1 = at("r1", R0 + 10240, [12, TT])

        cT = at("cT", Z + 155648, [2, CHUNK])
        cx = at("cx", Z + 138240, [TT, D])
        W1h = at("W1h", Z, [EXPERTS * FF], F32R)
        W1l = at("W1l", Z + 16384, [EXPERTS * FF], F32R)
        W3h = at("W3h", Z + 32768, [EXPERTS * FF], F32R)
        W3l = at("W3l", Z + 49152, [EXPERTS * FF], F32R)
        W2s = at("W2s", Z + 81920, [EXPERTS * FC * D])
        wst = [at(f"wst{i}", Z + 98304 + 8192 * i, [4 * FF]) for i in range(2)]

        class TileBufs:
            def __init__(self, l, o):
                self.xg = at(f"xg{l}", o, [8, ROW])
                o += 8 * ROW * 4
                self.gh = at(f"gh{l}", o, [2, D], F32R)
                self.gl = at(f"gl{l}", o + 1024, [2, D], F32R)
                self.s1 = at(f"s1{l}", o + 2048, [2, FF])
                self.act = at(f"act{l}", o + 2048 + 4096, [2, FF])
                self.aT = at(f"aT{l}", o + 2048 + 8192, [2, FF])
                self.yo = at(f"yo{l}", o + 2048 + 12288, [4, D])
                self.end = o + 2048 + 12288 + 2048

        tb = [TileBufs(0, Z + 114688), TileBufs(1, Z)]
        yback = [at("yback0", Z + 135424, [TT, TOPK, D]), at("yback1", Z + 32768, [TT, TOPK, D])]
        hT = at("hT", Z + 32768, [RC, TOKENS])
        rw = at("rw", Z + 65536, [3 * RNN_E])
        rwh = at("rwh", Z + 65536 + 3072, [3 * RNN_E], F32R)
        rwl = at("rwl", Z + 65536 + 6144, [3 * RNN_E], F32R)
        rwd = at("rwd", Z + 65536 + 9216, [RC, D])
        gf = at("gf", Z + 75776, [2, CHUNK])
        gi = at("gi", Z + 75776 + 4096, [2, CHUNK])
        gs = at("gs", Z + 75776 + 8192, [2, CHUNK])
        gv = at("gv", Z + 75776 + 12288, [2, CHUNK])
        gg = at("gg", Z + 75776 + 16384, [2, CHUNK])
        V1h = at("V1h", Z + 98304, [EXPERTS * FF], F32R)
        V1l = at("V1l", Z + 98304 + 16384, [EXPERTS * FF], F32R)
        V2s = at("V2s", Z + 131072, [EXPERTS * FC * D])
        vraw = at("vraw", Z + 147456, [EXPERTS * FF])
        b1s = at("b1s", Z + 147456, [EXPERTS * FF])
        b2s = at("b2s", Z + 163840, [EXPERTS * D])

        psum = ctx.enter_context(nc.psum_tensor("psum", [P, 8, 512], F32))

        sems = {}

        def sem(name):
            if name not in sems:
                sems[name] = ctx.enter_context(nc.semaphore(name))
            return sems[name]

        chained = {}

        def chain(eng, name):
            s = sem(name)

            def done(ins):
                chained[name] = chained.get(name, 0) + 1
                ins.then_inc(s, 1)
                eng.wait_ge(s, chained[name])
            return done

        block = ctx.enter_context(nc.Block())

        def ring_units(n):
            prev, nxt, nxt2 = n >= 1, n + 1 < NIT, n + 2 < NIT
            a = [("A", j, i, 0) for i in range(4) for j in range(HPG)]
            a += [("A", j, i, c) for i in range(4, TPB) for j in range(HPG) for c in range(2)]
            units = []
            for u in range(4 * TPB):
                if nxt:
                    for w in a[len(a) * u // 28:len(a) * (u + 1) // 28]:
                        units.append((u, w))
                if u == 4 and nxt:
                    units.append((u, ("k", 1)))
                if u in (6, 7) and prev:
                    units.append((u, ("o", u - 6)))
                if u == 18 and nxt2:
                    units.append((u, ("k", 0)))
                if u in (20, 22) and nxt2:
                    units.append((u, ("q", (u - 20) // 2)))
                if u in (29, 30) and nxt:
                    units.append((u, ("m", u - 29)))
            return units

        by_vector = ("A", "o")
        FRONT = [(0, ("k", 0)), (0, ("q", 0)), (0, ("q", 1))]
        BACK = [(0, ("o", 0)), (0, ("o", 1))]

        def ring_before(n):
            units = list(FRONT)
            for k in range(-1, n):
                units += ring_units(k)
            v = sum(1 for _, w in units if w[0] in by_vector)
            return len(units), v, len(units) - v

        class Count:
            def __init__(self, n, turn):
                self.all, self.vec, self.sca = ring_before(n)
                self.hist = []
                if n > -1:
                    last = (FRONT + [w for k in range(-1, n) for w in ring_units(k)])[-2:]
                    v, s = self.vec, self.sca
                    h = []
                    for _, w in reversed(last):
                        h.append((w[0] in by_vector, v if w[0] in by_vector else s))
                        if w[0] in by_vector:
                            v -= 1
                        else:
                            s -= 1
                    self.hist = h[::-1]
                elif n == -1:
                    self.hist = [(False, 2), (False, 3)]

            def add(self, w):
                if w[0] in by_vector:
                    self.vec += 1
                    self.hist.append((True, self.vec))
                else:
                    self.sca += 1
                    self.hist.append((False, self.sca))
                self.all += 1

        STEADY = ring_units(2)
        PER_ALL = len(STEADY)
        PER_VEC = sum(1 for _, w in STEADY if w[0] in by_vector)
        PER_SCA = PER_ALL - PER_VEC
        assert PER_ALL % 2 == 0 and len(ring_units(1)) == PER_ALL and len(ring_units(NIT - 3)) == PER_ALL

        def upto(n, name):
            s = ring_before(n)[2]
            for _, w in ring_units(n):
                if w[0] not in by_vector:
                    s += 1
                    if w == name:
                        return s
            raise ValueError(name)

        def all_upto(n, name):
            a = ring_before(n)[0]
            for _, w in ring_units(n):
                a += 1
                if w == name:
                    return a
            raise ValueError(name)

        def attention_iterations(eng, body):
            for n in (-1, 0, 1):
                body(n, None)
            with eng.Fori(0, NIT - 5, 2) as turn:
                body(2, turn)
                body(3, turn)
            for n in (NIT - 2, NIT - 1):
                body(n, None)

        def wait(eng, name, count, per, turn):
            if turn is None:
                if count > 0:
                    eng.wait_ge(sem(name), count)
            else:
                assert count > 0
                eng.wait_ge(sem(name), turn * per + count)

        def a_columns(i, c):
            if i < 4:
                return 0, max(256, P * (i + 1))
            half = 64 * (i + 1)
            return c * half, half

        def b_columns(jt):
            n = SEQ - P * jt
            if n > 512:
                return [(P * jt, n // 2, 0), (P * jt + n // 2, n // 2, 1)]
            return [(min(P * jt, SEQ - 256), max(n, 256), 0)]

        def mixture_loads(sp, l):
            sp.wait_ge(sem(f"rows_sorted{l}"), 16 * TOPK * TT)
            if l == 1:
                sp.wait_ge(sem("rnn_mm"), RC * NCH)
            for s in range(8):
                sp.dma_start(tb[l].xg[:, s, :], xs[l][s * P:(s + 1) * P, :]).then_inc(sem(f"row_in{l}_{s}"), 16)
            steady = (SLOT_TILES - 8) // 8 * 8
            with sp.Fori(0, steady - 7, 8) as s0:
                for c in range(8):
                    sp.wait_ge(sem(f"dest_ready{l}"), s0 + (c + 1))
                    sp.dma_start(tb[l].xg[:, c, :], xs[l][bass.ds((s0 + (8 + c)) * P, P), :]).then_inc(
                        sem(f"row_in{l}_{c}"), 16)
            for s in range(steady + 8, SLOT_TILES):
                sp.wait_ge(sem(f"dest_ready{l}"), s - 7)
                sp.dma_start(tb[l].xg[:, s % 8, :], xs[l][s * P:(s + 1) * P, :]).then_inc(
                    sem(f"row_in{l}_{s % 8}"), 16)

        def rows_back(sp, l):
            for c in range(4):
                sp.wait_ge(sem(f"row_out{l}_{c}"), 16 * len(range(c, SLOT_TILES, 4)))
            v = yc[l].rearrange("(i p k) d -> p i k d", p=P, k=TOPK)
            for c in range(4):
                sp.dma_start(yback[l][:, 8 * c:8 * c + 8], v[:, 8 * c:8 * c + 8]).then_inc(sem(f"back{l}_{c}"), 16)

        @block.sync
        def _(sp):
            sp.dma_start(cst[:], consts).then_inc(sem("const_in"), 16)
            xv = x.rearrange("b (i p) d -> p (b i) d", p=P)
            for c in range(4):
                sp.dma_start(xres[:, 8 * c:8 * c + 8], xv[:, 8 * c:8 * c + 8]).then_inc(sem(f"x_in{c}"), 16)
            sp.wait_ge(sem("pad_ready"), 2)
            for l in range(2):
                sp.dma_start(xs[l].rearrange("(s p) r -> p s r", p=P),
                             pad_rows[:].unsqueeze(1).to_broadcast([P, SLOT_TILES, ROW])).then_inc(
                                 sem("pads_in"), 16)
            sp.wait_ge(sem("pv_done"), TPB * NIT)
            sp.wait_ge(sem("ring_vec"), ring_before(NIT)[1])
            sp.dma_start(W2s[:].rearrange("p (e c d) -> p e c d", e=EXPERTS, c=FC),
                         W2.rearrange("e (c p) d -> p e c d", p=P)).then_inc(sem("w2_in0"), 16)
            for n in range(4):
                src = (W1, W3)[n // 2].rearrange("e d f -> d e f")[:, 4 * (n % 2):4 * (n % 2) + 4, :]
                if n >= 2:
                    sp.wait_ge(sem("w_split0"), n - 1)
                sp.dma_start(wst[n % 2][:].rearrange("p (e f) -> p e f", e=4), src).then_inc(sem(f"w_in0_{n}"), 16)
            mixture_loads(sp, 0)
            rows_back(sp, 0)
            sp.wait_ge(sem("combined0"), 4)
            sp.dma_start(rw[:], rnn_w).then_inc(sem("rnn_in"), 16)
            sp.dma_start(rwd[:], rnn_wd.rearrange("(c p) d -> p c d", p=P)).then_inc(sem("rnn_in"), 16)
            sp.dma_start(rnn_bias[:], rnn_b).then_inc(sem("rnn_in"), 16)
            sp.dma_start(vraw[:].rearrange("p (e f) -> p e f", e=EXPERTS),
                         w1.rearrange("e d f -> d e f")).then_inc(sem("v_in"), 16)
            sp.dma_start(V2s[:].rearrange("p (e c d) -> p e c d", e=EXPERTS, c=FC),
                         w2.rearrange("e (c p) d -> p e c d", p=P)).then_inc(sem("v2_in"), 16)
            sp.dma_start(b2s[:], b2.rearrange("e d -> (e d)").partition_broadcast(P)).then_inc(sem("v2_in"), 16)
            sp.wait_ge(sem("v_split"), 1)
            sp.dma_start(b1s[:], b1.rearrange("e f -> (e f)").partition_broadcast(P)).then_inc(sem("v2_in"), 16)
            mixture_loads(sp, 1)
            rows_back(sp, 1)
            ov = out.rearrange("b (i p) d -> p (b i) d", p=P)
            for c in range(4):
                sp.wait_ge(sem("combined1"), c + 1)
                sp.dma_start(ov[:, 8 * c:8 * c + 8], xres[:, 8 * c:8 * c + 8]).then_inc(sem("out_done"), 16)
            sp.wait_ge(sem("out_done"), 64)

        def qkv_out(copy, T):
            b, t = divmod(T, TPB)
            src = psum[:, 2 + T % 4, 0:NW]
            for a in range(2):
                dst = QK[:, a, b::BATCH, t * HPG:(t + 1) * HPG, :].rearrange("p g j d -> p g (j d)")
                copy(dst, src[:, a * D:(a + 1) * D].rearrange("p (g r) -> p g r", g=GROUPS))
            copy(Vn[:, b::BATCH, t, :], src[:, 2 * D:3 * D].rearrange("p (g r) -> p g r", g=GROUPS))
            return copy(lg[:, T, :], src[:, 3 * D:NW])

        def norm_vector(v, l, done):
            for c in range(4):
                if l == 0:
                    v.wait_ge(sem(f"x_in{c}"), 16)
                for i in range(8):
                    last = nc.vector.bn_stats(bn6[:, i, :], xres[:, 8 * c + i, :])
                done(last)
                for i in range(8):
                    last = nc.vector.bn_aggr(mv[:, i, :], bn6[:, i, :])
                done(last)
                nc.vector.tensor_scalar(rt[:], mv[:, :, 1], EPS, None, ALU.add).then_inc(sem(f"var_ready{l}"), 1)
                v.wait_ge(sem(f"sd_ready{l}"), c + 1)
                done(nc.vector.reciprocal(rs[:], sd[:]))
                done(nc.vector.tensor_tensor(sd[:], rs[:], rs[:], ALU.mult))
                done(nc.vector.tensor_tensor(sd[:], sd[:], rt[:], ALU.mult))
                done(nc.vector.tensor_scalar(sd[:], sd[:], -0.5, 1.5, ALU.mult, ALU.add))
                done(nc.vector.tensor_tensor(rs[:], rs[:], sd[:], ALU.mult))
                for i in range(8):
                    last = nc.vector.tensor_scalar(rows[:, 8 * c + i, 0:D], xres[:, 8 * c + i, :],
                                                   mv[:, i, 0:1], rs[:, i:i + 1], ALU.subtract, ALU.mult)
                last.then_inc(sem(f"xn_ready{l}"), 1)
                v.wait_ge(sem(f"xn_ready{l}"), c + 1)

        def lo_vector(v, l):
            for c in range(NCH):
                v.wait_ge(sem(f"xh_ready{l}"), c + 1)
                nc.vector.tensor_tensor(xl[:, c * CHUNK:(c + 1) * CHUNK], psum[:, c % 2, :],
                                        xh[:, c * CHUNK:(c + 1) * CHUNK].bitcast(F32),
                                        ALU.subtract).then_inc(sem(f"xl_ready{l}"), 1)

        def router_vector(v, l, done):
            def bc(t):
                return t.unsqueeze(2).to_broadcast([P, TT, EXPERTS])
            prio_b = prio.unsqueeze(1).to_broadcast([P, TT, EXPERTS])
            top0, top1, w, q0, q1, z = (r1[:, i, :] for i in range(6))
            if l == 1:
                done(nc.vector.tensor_tensor(lg[:], lg[:], gbias[:].unsqueeze(1).to_broadcast([P, TT, EXPERTS]),
                                             ALU.add))
            done(nc.vector.tensor_reduce(top0, lg[:], AX, ALU.max))
            done(nc.vector.tensor_tensor(ra[:], lg[:], bc(top0), ALU.is_equal))
            done(nc.vector.tensor_tensor(rb[:], ra[:], prio_b, ALU.mult))
            done(nc.vector.tensor_reduce(w, rb[:], AX, ALU.max))
            done(nc.vector.tensor_tensor(ch0[:], prio_b, bc(w), ALU.is_equal))
            done(nc.vector.scalar_tensor_tensor(ra[:], ch0[:], -BIG, lg[:], ALU.mult, ALU.add))
            done(nc.vector.tensor_reduce(top1, ra[:], AX, ALU.max))
            done(nc.vector.tensor_tensor(rb[:], ra[:], bc(top1), ALU.is_equal))
            done(nc.vector.tensor_tensor(ra[:], rb[:], prio_b, ALU.mult))
            done(nc.vector.tensor_reduce(w, ra[:], AX, ALU.max))
            done(nc.vector.tensor_tensor(ch1[:], prio_b, bc(w), ALU.is_equal))
            nc.vector.tensor_tensor(q0, top1, top0, ALU.subtract).then_inc(sem(f"gate_diff{l}"), 1)
            if l == 1:
                nc.vector.tensor_tensor(lg[:], lg[:], bc(top0), ALU.subtract).then_inc(sem(f"gate_diff{l}"), 1)
            done(nc.vector.tensor_tensor(cnt[:].rearrange("p e i -> p i e"), ch0[:], ch1[:], ALU.add))
            done(nc.vector.tensor_tensor_scan(run[:].rearrange("p e i -> p (e i)"),
                                              cst[:, C_RMASK:C_PRIO], cnt[:].rearrange("p e i -> p (e i)"),
                                              0.0, ALU.mult, ALU.add))
            nc.vector.tensor_copy(small[:, 0, :], run[:, :, TT - 1]).then_inc(sem(f"count_ready{l}"), 1)
            v.wait_ge(sem(f"count_sums{l}"), 1)
            done(nc.vector.tensor_copy(small[:, 1, :], psum[:, 7, 0:EXPERTS]))
            done(nc.vector.tensor_scalar(smalli[:], psum[:, 7, EXPERTS:2 * EXPERTS], float(P - 1), None, ALU.add))
            done(nc.vector.tensor_scalar(smalli[:], smalli[:], 7, None, ALU.logical_shift_right))
            done(nc.vector.tensor_copy(small[:, 2, :], smalli[:]))
            done(nc.vector.tensor_tensor_scan(small[:, 3, :], cst[:, C_ONES:C_ONES + EXPERTS], small[:, 2, :],
                                              0.0, ALU.mult, ALU.add))
            done(nc.vector.tensor_tensor(small[:, 4, :], small[:, 3, :], small[:, 2, :], ALU.subtract))
            done(nc.vector.tensor_scalar(small[:, 4, :], small[:, 4, :], float(P), -1.0, ALU.mult, ALU.add))
            done(nc.vector.tensor_tensor(small[:, 4, :], small[:, 4, :], small[:, 1, :], ALU.add))
            done(nc.vector.tensor_tensor(run[:], run[:], small[:, 4, :].unsqueeze(2).to_broadcast([P, EXPERTS, TT]),
                                         ALU.add))
            run_v = run[:].rearrange("p e i -> p i e")
            for k, ch in enumerate((ch0, ch1)):
                done(nc.vector.tensor_tensor(ra[:], run_v, ch[:], ALU.mult))
                done(nc.vector.tensor_reduce(r1[:, 6 + k, :], ra[:], AX, ALU.add))
            iota = cst[:, C_IOTA:C_HEAD].unsqueeze(2).to_broadcast([P, SLOT_TILES, EXPERTS])
            ends = small[:, 3, :].unsqueeze(1).to_broadcast([P, SLOT_TILES, EXPERTS])
            done(nc.vector.tensor_tensor(tcmp[:], iota, ends, ALU.is_ge))
            ended = cnt[:].rearrange("p e i -> p (e i)")[:, 0:SLOT_TILES]
            done(nc.vector.tensor_reduce(ended, tcmp[:], AX, ALU.add))
            done(nc.vector.tensor_scalar(tile_expert[:], ended, float(EXPERTS - 1), None, ALU.min))
            done(nc.vector.tensor_copy(slot_i[:], r1[:, 6:8, :]))
            done(nc.vector.tensor_copy(rows[:, :, D], cst[:, C_TOK2:C_PART]))
            nc.vector.tensor_copy(rows[:, :, D + 1], r1[:, 6, :]).then_inc(sem(f"slots_ready{l}"), 1)
            if l == 0:
                v.wait_ge(sem("gate_exp0"), 1)
                done(nc.vector.tensor_scalar(z, q1, 1.0, None, ALU.add))
                done(nc.vector.reciprocal(gate_wt[:, 0, :], z))
                done(nc.vector.tensor_tensor(gate_wt[:, 1, :], q1, gate_wt[:, 0, :], ALU.mult))
            else:
                v.wait_ge(sem("gate_exp1"), 2)
                done(nc.vector.tensor_reduce(z, lg[:], AX, ALU.add))
                done(nc.vector.reciprocal(q0, z))
                done(nc.vector.tensor_tensor(q1, q1, q0, ALU.mult))
                done(nc.vector.tensor_tensor(z, q0, q1, ALU.add))
                done(nc.vector.tensor_scalar(z, z, 1e-9, None, ALU.add))
                done(nc.vector.reciprocal(w, z))
                done(nc.vector.tensor_tensor(gate_wt[:, 0, :], q0, w, ALU.mult))
                done(nc.vector.tensor_tensor(gate_wt[:, 1, :], q1, w, ALU.mult))

        LOOP_FROM, LOOP_TURNS = 8, (SLOT_TILES - 8) // 8

        def mixture_steps(eng, step):
            for s in range(LOOP_FROM):
                step(s, None, s)
            with eng.Fori(0, 8 * LOOP_TURNS - 7, 8) as dyn:
                for c in range(8):
                    step(LOOP_FROM + c, dyn, c)
            for s in range(LOOP_FROM + 8 * LOOP_TURNS, SLOT_TILES + 2):
                step(s, None, s)

        def mixture_vector(v, l):
            b = tb[l]

            def step(s, dyn, c):
                def w(name, count):
                    v.wait_ge(sem(name), count if dyn is None else dyn + count)
                if 1 <= s <= SLOT_TILES:
                    t = (c - 1) % 2
                    if l == 0:
                        w("silu_ready0", s)
                        w("h_ready0", 2 * s) if dyn is None else v.wait_ge(sem("h_ready0"), dyn * 2 + 2 * s)
                        if s >= 3:
                            w("aT_in0", s - 2)
                        nc.vector.tensor_tensor(b.act[:, t, :], b.s1[:, t, :], psum[:, 3 + t, :],
                                                ALU.mult).then_inc(sem("act_ready0"), 1)
                    else:
                        e = v.value_load(tile_expert[0:1, s - 1:s] if dyn is None else
                                         tile_expert[0:1, bass.ds(dyn + (s - 1), 1)],
                                         min_val=0, max_val=EXPERTS - 1)
                        w("h_ready1", s)
                        if s >= 3:
                            w("act_ready1", s - 2)
                        nc.vector.tensor_tensor(b.s1[:, t, :], psum[:, 1 + t, :], b1s[:, bass.ds(e * FF, FF)],
                                                ALU.add).then_inc(sem("pre_ready1"), 1)
                if s < SLOT_TILES:
                    w(f"gh_ready{l}", s + 1)
                    nc.vector.tensor_tensor(b.gl[:, c % 2, :], psum[:, 0, 0:P], b.gh[:, c % 2, :].bitcast(F32),
                                            ALU.subtract).then_inc(sem(f"gl_ready{l}"), 1)
                    if s >= 4:
                        v.wait_ge(sem(f"row_out{l}_{c % 4}"), 16 * (s // 4)) if dyn is None else \
                            v.wait_ge(sem(f"row_out{l}_{c % 4}"), dyn * 4 + 16 * (s // 4))
                    slot_id = cst[:, C_PART + s:C_PART + s + 1] if dyn is None else \
                        cst[:, bass.ds(dyn + (C_PART + s), 1)]
                    nc.vector.tensor_scalar(destf[:, c % 4:c % 4 + 1], slot_id, b.xg[:, c % 8, D + 1:D + 2],
                                            b.xg[:, c % 8, D:D + 1], ALU.not_equal, ALU.add).then_inc(
                                                sem(f"dest_ready{l}"), 1)
                if l == 1 and s >= 2:
                    e = v.value_load(tile_expert[0:1, s - 2:s - 1] if dyn is None else
                                     tile_expert[0:1, bass.ds(dyn + (s - 2), 1)], min_val=0, max_val=EXPERTS - 1)
                    w("y_ready1", s - 1)
                    if s >= 6:
                        v.wait_ge(sem(f"row_out1_{(c - 2) % 4}"), 16 * ((s - 2) // 4)) if dyn is None else \
                            v.wait_ge(sem(f"row_out1_{(c - 2) % 4}"), dyn * 4 + 16 * ((s - 2) // 4))
                    nc.vector.tensor_tensor(b.yo[:, (c - 2) % 4, :], psum[:, 7, 0:D], b2s[:, bass.ds(e * D, D)],
                                            ALU.add).then_inc(sem("yo_ready1"), 1)
            mixture_steps(v, step)

        def combine_vector(v, l, done):
            for c in range(4):
                v.wait_ge(sem(f"back{l}_{c}"), 16)
                for i in range(8 * c, 8 * c + 8):
                    last = nc.vector.scalar_tensor_tensor(xres[:, i, :], yback[l][:, i, 0, :],
                                                          gate_wt[:, 0, i:i + 1], xres[:, i, :], ALU.mult, ALU.add)
                done(last)
                for i in range(8 * c, 8 * c + 8):
                    last = nc.vector.scalar_tensor_tensor(xres[:, i, :], yback[l][:, i, 1, :],
                                                          gate_wt[:, 1, i:i + 1], xres[:, i, :], ALU.mult, ALU.add)
                last.then_inc(sem(f"combined{l}"), 1)
            v.wait_ge(sem(f"combined{l}"), 4)

        @block.vector
        def _(v):
            done = chain(v, "vector_step")
            nc.vector.memset(pad_rows[:, 0:D], 0.0).then_inc(sem("pad_ready"), 1)
            v.wait_ge(sem("pad_ready"), 1)
            nc.vector.memset(pad_rows[:, D:ROW], SKIP).then_inc(sem("pad_ready"), 1)
            v.wait_ge(sem("const_in"), 16)
            nc.vector.tensor_copy(ident_b[:], ident)
            nc.vector.tensor_copy(mask_b[:], cst[:, C_MASK:C_MASK + P]).then_inc(sem("bf_consts"), 1)
            norm_vector(v, 0, done)
            v.wait_ge(sem("lora_prod"), 1)
            done(nc.vector.scalar_tensor_tensor(wraw[:, 0:3 * D], psum[:, 6, 0:3 * D], 1.0 / LORA_RANK,
                                                wraw[:, 0:3 * D], ALU.mult, ALU.add))
            nc.vector.scalar_tensor_tensor(wo_sb[:], psum[:, 6, 3 * D:4 * D], 1.0 / LORA_RANK,
                                           wo_raw[:], ALU.mult, ALU.add).then_inc(sem("w_ready"), 1)
            v.wait_ge(sem("wh_ready"), 1)
            nc.vector.tensor_tensor(wl[:], wraw[:], wh[:].bitcast(F32), ALU.subtract).then_inc(sem("wl_ready"), 1)
            lo_vector(v, 0)
            for T in range(1, TT, 2):
                v.wait_ge(sem("qkv_done"), T + 1)
                last = qkv_out(nc.vector.tensor_copy, T)
                last.then_inc(sem("qkv_vec"), 1)
            v.wait_ge(sem("qkv_sca"), TT // 2)
            v.wait_ge(sem("qkv_vec"), TT // 2)
            router_vector(v, 0, done)
            for i in range(2):
                nc.vector.memset(tq[i][:], 0.0)
                done(nc.vector.memset(tk[i][:], 0.0))
                nc.vector.memset(tk[i][:, :, 24:26], 1.0)
                done(nc.vector.memset(Vs[i][:], 0.0))
                last = nc.vector.memset(Vs[i][:, :, :, HD:HD + 1], 1.0)
            last.then_inc(sem("stacks_zeroed"), 1)

            def body(n, turn):
                cn = Count(n, turn)
                for u, w in ring_units(n):
                    bank = cn.all % 2
                    idx = cn.all + 1
                    cn.add(w)
                    if w[0] not in by_vector:
                        continue
                    wait(v, "ring_full", idx, PER_ALL, turn)
                    if w[0] == "A":
                        _, j, i, c = w
                        width = a_columns(i, c)[1] if i else P
                        dst = mall[:, j, i:i + 1] if i < 4 else mtwo[:, j, i - 4, c:c + 1]
                        nc.vector.reduce_max(dst, psum[:, bank, 0:width], AX).then_inc(sem("ring_vec"), 1)
                    else:
                        output_unit(v, n - 1, turn, w[1], bank)
                if n + 1 < NIT:
                    par = (n + 1) % 2
                    wait(v, "ring_vec", cn.vec, PER_VEC, turn)
                    step_a(v, nc.vector.tensor_reduce(mall[:, :, 4:TPB], mtwo[:], AX, ALU.max), n, turn, 1)
                    step_a(v, nc.vector.tensor_scalar(negm[:], mall[:], -1.0, None, ALU.mult), n, turn, 2)
                    step_a(v, nc.vector.tensor_copy(negh[:], negm[:]), n, turn, 3)
                    cols = tq[par][:].rearrange("p (t j) r -> p j t r", j=HPG)
                    nc.vector.tensor_copy(cols[:, :, :, 24], negh[:].bitcast(F32))
                    nc.vector.tensor_tensor(cols[:, :, :, 25], negm[:], negh[:].bitcast(F32),
                                            ALU.subtract).then_inc(sem("m_ready"), 1)

            def step_a(v, ins, n, turn, k):
                ins.then_inc(sem("max_step"), 1)
                wait(v, "max_step", 3 * (n + 1) + k, 3, turn)

            def output_unit(v, n, turn, half, bank):
                src = psum[:, bank, :].rearrange("p (t j r) -> p t j r", t=TPC, j=HPG)
                nc.vector.reciprocal(recip[:, half], src[:, :, :, HD]).then_inc(sem("recip_step"), 1)
                wait(v, "recip_step", 2 * n + half + 1, 2, turn)
                off = (2 * n + half) * CHUNK // 4
                if turn is None:
                    dst = Vn[:, n, half * TPC:(half + 1) * TPC, :]
                else:
                    flat = Vn[:].rearrange("p n t r -> p (n t r)")
                    dst = flat[:, bass.ds(turn * (TPB * HPG * HD) + off, TPC * HPG * HD)].rearrange(
                        "p (t r) -> p t r", t=TPC)
                nc.vector.tensor_tensor(dst.rearrange("p t (j d) -> p t j d", j=HPG), src[:, :, :, 0:HD],
                                        recip[:, half].unsqueeze(3).to_broadcast([P, TPC, HPG, HD]),
                                        ALU.mult).then_inc(sem("ring_vec"), 1)

            attention_iterations(v, body)
            r_all, r_vec, _ = ring_before(NIT)
            for half in range(2):
                v.wait_ge(sem("ring_full"), r_all + half + 1)
                output_unit(v, NIT - 1, None, half, (r_all + half) % 2)
            v.wait_ge(sem("ring_vec"), r_vec + 2)
            v.wait_ge(sem("pv_done"), TPB * NIT)
            for c in range(NCH):
                b, i = divmod(TPC * c, TPB)
                nc.vector.tensor_copy(cx[:, TPC * c:TPC * (c + 1), :].rearrange("p t (g r) -> p t g r", g=GROUPS),
                                      Vn[:, b::BATCH, i:i + TPC, :].rearrange("p g t r -> p t g r")).then_inc(
                                          sem("cx_ready"), 1)
            for n in range(4):
                v.wait_ge(sem("w_hi0"), n + 1)
                h, lo = ((W1h, W1l), (W3h, W3l))[n // 2]
                r = slice(4 * FF * (n % 2), 4 * FF * (n % 2 + 1))
                nc.vector.tensor_tensor(lo[:, r], wst[n % 2][:], h[:, r].bitcast(F32),
                                        ALU.subtract).then_inc(sem("w_split0"), 1)
            for c in range(NCH):
                v.wait_ge(sem("proj_done"), c + 1)
                nc.vector.tensor_tensor(xres[:, TPC * c:TPC * (c + 1), :], xres[:, TPC * c:TPC * (c + 1), :],
                                        psum[:, 4 + c % 2, :].rearrange("p (t d) -> p t d", t=TPC),
                                        ALU.add).then_inc(sem("proj_added"), 1)
            mixture_vector(v, 0)
            v.wait_ge(sem("proj_added"), NCH)
            combine_vector(v, 0, done)
            norm_vector(v, 1, done)
            v.wait_ge(sem("gw_in"), 32)
            lo_vector(v, 1)
            v.wait_ge(sem("gwh_ready"), 1)
            nc.vector.tensor_tensor(gwl[:], gw_sb[:], gwh[:].bitcast(F32), ALU.subtract).then_inc(sem("gwl_ready"), 1)
            v.wait_ge(sem("rnn_hi"), 1)
            nc.vector.tensor_tensor(rwl[:], rw[:], rwh[:].bitcast(F32), ALU.subtract).then_inc(sem("rnn_lo"), 1)
            nc.vector.tensor_scalar(rnn_bh[:], rnn_bias[:, 2 * RC:3 * RC], 0.5, None, ALU.add).then_inc(
                sem("rnn_bh_ready"), 1)
            v.wait_ge(sem("logits1"), 1)
            done(nc.vector.tensor_copy(lg[:].rearrange("p i e -> p (i e)"), psum[:, 6, 0:TT * EXPERTS]))
            router_vector(v, 1, done)
            v.wait_ge(sem("v_hi"), 1)
            nc.vector.tensor_tensor(V1l[:], vraw[:], V1h[:].bitcast(F32), ALU.subtract).then_inc(sem("v_split"), 1)
            v.wait_ge(sem("rnn_bh_ready"), 1)
            for m in range(RC * NCH):
                c, k = m // RC, m % RC
                v.wait_ge(sem("sig_ready"), 3 * (m + 1))
                nc.vector.scalar_tensor_tensor(gg[:, m % 2, :], psum[:, 3 * (m % 2) + 2, :], rnn_bh[:, k:k + 1],
                                               gs[:, m % 2, :], ALU.add, ALU.max).then_inc(sem("g_ready"), 1)
                v.wait_ge(sem("g_ready"), m + 1)
                done(nc.vector.tensor_tensor(gv[:, m % 2, :], gg[:, m % 2, :], gi[:, m % 2, :], ALU.mult))
                start = c * CHUNK
                first = 0.5 if start % SEQ == 0 else hT[:, k, start - 1:start]
                if start % SEQ:
                    v.wait_ge(sem("scan_done"), m - RC + 1)
                nc.vector.tensor_tensor_scan(hT[:, k, start:start + CHUNK], gf[:, m % 2, :], gv[:, m % 2, :],
                                             first, ALU.mult, ALU.add).then_inc(sem("scan_done"), 1)
            for c in range(NCH):
                v.wait_ge(sem("rnn_out"), c + 1)
                nc.vector.tensor_tensor(xres[:, TPC * c:TPC * (c + 1), :], xres[:, TPC * c:TPC * (c + 1), :],
                                        psum[:, 6 + c % 2, :].rearrange("p (t d) -> p t d", t=TPC),
                                        ALU.add).then_inc(sem("rnn_added"), 1)
            mixture_vector(v, 1)
            v.wait_ge(sem("rnn_added"), NCH)
            combine_vector(v, 1, done)

        def hi_scalar(a, l):
            for c in range(NCH):
                a.wait_ge(sem(f"xT_done{l}"), c + 1)
                nc.scalar.copy(xh[:, c * CHUNK:(c + 1) * CHUNK], psum[:, c % 2, :]).then_inc(sem(f"xh_ready{l}"), 1)

        def norm_scalar(a, l):
            for c in range(4):
                a.wait_ge(sem(f"var_ready{l}"), c + 1)
                nc.scalar.activation(sd[:], rt[:], ACT.Sqrt).then_inc(sem(f"sd_ready{l}"), 1)

        def mixture_scalar(a, l):
            b = tb[l]

            def step(s, dyn, c):
                def w(name, count, per=1):
                    a.wait_ge(sem(name), count if dyn is None else dyn * per + count)
                if s >= 2:
                    w(f"aT_in{l}", s - 1)
                    if s >= 4:
                        w(f"y_ready{l}", s - 3)
                    nc.scalar.copy(b.aT[:, c % 2, :], psum[:, 5 + c % 2, :]).then_inc(sem(f"aT_ready{l}"), 1)
                if 1 <= s <= SLOT_TILES:
                    t = (c - 1) % 2
                    if l == 0:
                        w("h_ready0", 2 * s - 1, 2)
                        if s >= 3:
                            w("act_ready0", s - 2)
                        nc.scalar.activation(b.s1[:, t, :], psum[:, 1 + t, :], ACT.Silu).then_inc(
                            sem("silu_ready0"), 1)
                    else:
                        w("pre_ready1", s)
                        nc.scalar.activation(b.act[:, t, :], b.s1[:, t, :], ACT.Gelu).then_inc(sem("act_ready1"), 1)
                if s < SLOT_TILES:
                    w(f"gT_done{l}", s + 1)
                    if s >= 2:
                        w(f"h_ready{l}", (2 if l == 0 else 1) * (s - 1), 2 if l == 0 else 1)
                    nc.scalar.copy(b.gh[:, c % 2, :], psum[:, 0, 0:P]).then_inc(sem(f"gh_ready{l}"), 1)
                if s >= 2 and l == 0:
                    w("y_ready0", s - 1)
                    if s >= 6:
                        a.wait_ge(sem(f"row_out0_{(c - 2) % 4}"), 16 * ((s - 2) // 4)) if dyn is None else \
                            a.wait_ge(sem(f"row_out0_{(c - 2) % 4}"), dyn * 4 + 16 * ((s - 2) // 4))
                    nc.scalar.copy(b.yo[:, (c - 2) % 4, :], psum[:, 7, 0:D]).then_inc(sem("yo_ready0"), 1)
            mixture_steps(a, step)

        @block.scalar
        def _(a):
            a.dma_start(wraw[:], w_cat).then_inc(sem("w_in"), 16)
            a.dma_start(la[0:LORA_RANK, :], lora_a).then_inc(sem("w_in"), 16)
            a.dma_start(lb[0:LORA_RANK, :], lora_b).then_inc(sem("w_in"), 16)
            a.dma_start(wo_raw[:], wo_t).then_inc(sem("w_in"), 16)
            a.dma_start(gw_sb[:], gate_w).then_inc(sem("gw_in"), 16)
            a.dma_start(gbias[:], gate_b.partition_broadcast(P)).then_inc(sem("gw_in"), 16)
            norm_scalar(a, 0)
            a.wait_ge(sem("w_ready"), 1)
            nc.scalar.copy(wh[:], wraw[:]).then_inc(sem("wh_ready"), 1)
            hi_scalar(a, 0)
            for T in range(0, TT, 2):
                a.wait_ge(sem("qkv_done"), T + 1)
                qkv_out(nc.scalar.copy, T).then_inc(sem("qkv_sca"), 1)
            a.wait_ge(sem("gate_diff0"), 1)
            nc.scalar.activation(r1[:, 4, :], r1[:, 3, :], ACT.Exp).then_inc(sem("gate_exp0"), 1)

            def heads(n, turn, a_):
                if turn is None:
                    return QK[:, a_, n, :, :]
                flat = QK[:].rearrange("p a n x d -> p (a n x d)")
                size = TPB * HPG * HD
                return flat[:, bass.ds(turn * size + (a_ * NIT + n) * size, size)].rearrange(
                    "p (x d) -> p x d", d=HD)

            def build_hi(n, turn):
                for a_, t in ((0, tq), (1, tk)):
                    nc.scalar.copy(t[n % 2][:, :, 0:HD].bitcast(F32R), heads(n, turn, a_)).then_inc(
                        sem("tok_hi"), 1)

            def stack_unit(n, turn, w, bank, idx):
                wait(a, "ring_full", idx, PER_ALL, turn)
                kind, half = w[0], w[1]
                r = slice(half * CHUNK, (half + 1) * CHUNK)
                if kind == "k":
                    m = n + 2 if half == 0 else n + 1
                    if m >= 2:
                        wait(a, "b_full", 4 * TPB * (m - 2) + (16 if half == 0 else 4 * TPB), 4 * TPB, turn)
                    for j in range(HPG):
                        last = nc.scalar.activation(kz[m % 2][:, j, r], psum[:, bank, :], ACT.Copy,
                                                    scale=cst[:, C_HEAD + j:C_HEAD + j + 1])
                elif kind == "q":
                    last = nc.scalar.copy(qs[n % 2][:, r], psum[:, bank, :])
                else:
                    if n >= 1:
                        wait(a, "b_full", 4 * TPB * n, 4 * TPB, turn)
                    last = nc.scalar.copy(qm[(n + 1) % 2][:, r], psum[:, bank, :])
                last.then_inc(sem("ring_sca"), 1)

            a.wait_ge(sem("stacks_zeroed"), 1)
            build_hi(0, None)
            for k, (_, w) in enumerate(FRONT):
                stack_unit(-2, None, w, k % 2, k + 1)

            def body(n, turn):
                cn = Count(n, turn)
                mine = {}
                for u, w in ring_units(n):
                    if w[0] not in by_vector:
                        mine.setdefault(u, []).append((w, cn.all % 2, cn.all + 1))
                    cn.add(w)
                for u in range(4 * TPB):
                    if n >= 0:
                        jt, j = divmod(u, HPG)
                        wait(a, "b_full", 4 * TPB * n + u + 1, 4 * TPB, turn)
                        if n > 0 or jt >= 2:
                            wait(a, "pv_done", TPB * n + jt - 1, TPB, turn)
                        cols = b_columns(jt)
                        width = SEQ - P * jt
                        slot = (jt % 2) * HPG + j
                        bank = 2 + 2 * (u % 2)
                        if len(cols) == 2:
                            src = psum[:, bank:bank + 2, 0:width // 2]
                            dst = pT[:, slot, 0:width].rearrange("p (c q) -> p c q", c=2)
                        else:
                            skip = P * jt - cols[0][0]
                            src = psum[:, bank, skip:skip + width]
                            dst = pT[:, slot, 0:width]
                        nc.scalar.activation(dst, src, ACT.Exp, scale=HD ** -0.5).then_inc(sem("exp_done"), 1)
                    if u == 2 and n >= 1:
                        evacuate_o(n - 1, turn, n)
                    if u == 8 and n + 2 < NIT:
                        if n >= 0:
                            wait(a, "ring_full", all_upto(n - 1, ("m", 1)), PER_ALL, turn)
                        build_hi(n + 2, turn)
                    for w, bank, idx in mine.get(u, ()):
                        stack_unit(n, turn, w, bank, idx)

            def evacuate_o(n, turn, now):
                wait(a, "pv_done", TPB * (n + 1), TPB, turn)
                if n >= 1:
                    wait(a, "ring_full", all_upto(n, ("o", 1)), PER_ALL, turn)
                nc.scalar.copy(oT[:].rearrange("p (c q) -> p c q", c=2), psum[:, 6:8, :]).then_inc(
                    sem("o_taken"), 1)

            attention_iterations(a, body)
            evacuate_o(NIT - 1, None, NIT)
            for n in range(4):
                a.wait_ge(sem(f"w_in0_{n}"), 16)
                if n == 0:
                    a.wait_ge(sem("b_full"), 4 * TPB * NIT)
                h = (W1h, W3h)[n // 2]
                nc.scalar.copy(h[:, 4 * FF * (n % 2):4 * FF * (n % 2 + 1)], wst[n % 2][:]).then_inc(sem("w_hi0"), 1)
            for c in range(NCH):
                a.wait_ge(sem("cT_done"), c + 1)
                if c >= 2:
                    a.wait_ge(sem("proj_done"), c - 1)
                nc.scalar.copy(cT[:, c % 2, :], psum[:, 2 + c % 2, :]).then_inc(sem("cT_ready"), 1)
            mixture_scalar(a, 0)
            norm_scalar(a, 1)
            hi_scalar(a, 1)
            a.wait_ge(sem("gw_in"), 32)
            nc.scalar.copy(gwh[:], gw_sb[:]).then_inc(sem("gwh_ready"), 1)
            a.wait_ge(sem("rnn_in"), 48)
            nc.scalar.copy(rwh[:], rw[:]).then_inc(sem("rnn_hi"), 1)
            a.wait_ge(sem("v_in"), 16)
            nc.scalar.copy(V1h[:], vraw[:]).then_inc(sem("v_hi"), 1)
            a.wait_ge(sem("gate_diff1"), 2)
            nc.scalar.activation(r1[:, 4, :], r1[:, 3, :], ACT.Exp).then_inc(sem("gate_exp1"), 1)
            nc.scalar.activation(lg[:], lg[:], ACT.Exp).then_inc(sem("gate_exp1"), 1)
            for m in range(RC * NCH):
                k = m % RC
                a.wait_ge(sem("rnn_mm"), m + 1)
                if m >= 2:
                    a.wait_ge(sem("scan_done"), m - 1)
                for g, dst in ((0, gf), (1, gi), (2, gs)):
                    nc.scalar.activation(dst[:, m % 2, :], psum[:, 3 * (m % 2) + g, :], ACT.Sigmoid,
                                         bias=rnn_bias[:, g * RC + k:g * RC + k + 1]).then_inc(sem("sig_ready"), 1)
            mixture_scalar(a, 1)

        def split_product(dst, lh, ll, rh, rl, extra_last=False):
            nc.tensor.matmul(dst, lh, rh, start=True, stop=False)
            nc.tensor.matmul(dst, ll, rh, start=False, stop=False)
            return nc.tensor.matmul(dst, lh, rl, start=False, stop=True)

        def transposes_tensor(pe, l):
            for c in range(NCH):
                pe.wait_ge(sem(f"xn_ready{l}"), c // 2 + 1)
                if c >= 2:
                    pe.wait_ge(sem(f"xl_ready{l}"), c - 1)
                for t in range(TPC):
                    last = nc.tensor.transpose(psum[:, c % 2, t * P:(t + 1) * P], rows[:, TPC * c + t, 0:D], ident)
                last.then_inc(sem(f"xT_done{l}"), 1)

        def counts_tensor(pe, l):
            pe.wait_ge(sem(f"count_ready{l}"), 1)
            nc.tensor.matmul(psum[:, 7, 0:EXPERTS], cst[:, C_TRI:C_TRI + P], small[:, 0, :], start=True, stop=True)
            nc.tensor.matmul(psum[:, 7, EXPERTS:2 * EXPERTS], cst[:, C_ONES:C_ONES + P], small[:, 0, :],
                             start=True, stop=True).then_inc(sem(f"count_sums{l}"), 1)

        def mixture_tensor(pe, l):
            b = tb[l]
            W2x = W2s if l == 0 else V2s

            def expert(t, dyn):
                return pe.value_load(tile_expert[0:1, t:t + 1] if dyn is None else
                                     tile_expert[0:1, bass.ds(dyn + t, 1)], min_val=0, max_val=EXPERTS - 1)

            def step(s, dyn, c):
                def w(name, count, per=1):
                    pe.wait_ge(sem(name), count if dyn is None else dyn * per + count)
                if s >= 2:
                    t = c % 2
                    w(f"act_ready{l}", s - 1)
                    if s >= 4:
                        w(f"aT_ready{l}", s - 3)
                    for k in range(FC):
                        last = nc.tensor.transpose(psum[:, 5 + t, k * P:(k + 1) * P],
                                                   b.act[:, t, k * P:(k + 1) * P], ident)
                    last.then_inc(sem(f"aT_in{l}"), 1)
                if 1 <= s <= SLOT_TILES:
                    t = (c - 1) % 2
                    e = expert(s - 1, dyn)
                    w(f"gl_ready{l}", s)
                    cols = bass.ds(e * FF, FF)
                    if s >= 3:
                        w("silu_ready0" if l == 0 else "pre_ready1", s - 2)
                    pairs = ((W1h, W1l, 1), (W3h, W3l, 3)) if l == 0 else ((V1h, V1l, 1),)
                    for h, lo, bank in pairs:
                        if bank == 3 and s >= 3:
                            w("act_ready0", s - 2)
                        split_product(psum[:, bank + t, :], b.gh[:, t, :], b.gl[:, t, :], h[:, cols],
                                      lo[:, cols]).then_inc(sem(f"h_ready{l}"), 1)
                if s < SLOT_TILES:
                    pe.wait_ge(sem(f"row_in{l}_{c % 8}"), 16 * (s // 8 + 1)) if dyn is None else \
                        pe.wait_ge(sem(f"row_in{l}_{c % 8}"), dyn * 2 + 16 * (s // 8 + 1))
                    if s >= 1:
                        w(f"gl_ready{l}", s)
                    nc.tensor.transpose(psum[:, 0, 0:P], b.xg[:, c % 8, 0:D], ident).then_inc(sem(f"gT_done{l}"), 1)
                if s >= 2:
                    t = c % 2
                    e = expert(s - 2, dyn)
                    w(f"aT_ready{l}", s - 1)
                    if s >= 3:
                        w(f"yo_ready{l}", s - 2)
                    for k in range(FC):
                        last = nc.tensor.matmul(psum[:, 7, 0:D], b.aT[:, t, k * P:(k + 1) * P],
                                                W2x[:, bass.ds(e * (FC * D) + k * D, D)],
                                                start=(k == 0), stop=(k == FC - 1))
                    last.then_inc(sem(f"y_ready{l}"), 1)
            mixture_steps(pe, step)

        @block.tensor
        def _(pe):
            pe.wait_ge(sem("const_in"), 16)
            pe.wait_ge(sem("w_in"), 64)
            for k in range(4):
                last = nc.tensor.matmul(psum[:, 6, k * D:(k + 1) * D], la[0:LORA_RANK, k * D:(k + 1) * D],
                                        lb[0:LORA_RANK, k * D:(k + 1) * D], start=True, stop=True)
            last.then_inc(sem("lora_prod"), 1)
            transposes_tensor(pe, 0)
            pe.wait_ge(sem("wl_ready"), 1)
            for T in range(TT):
                if T % TPC == 0:
                    pe.wait_ge(sem("xl_ready0"), T // TPC + 1)
                if T >= 4:
                    pe.wait_ge(sem("qkv_sca" if T % 2 == 0 else "qkv_vec"), T // 2 - 1)
                t = slice(T * P, (T + 1) * P)
                split_product(psum[:, 2 + T % 4, 0:NW], xh[:, t], xl[:, t], wh[:], wl[:]).then_inc(
                    sem("qkv_done"), 1)
            counts_tensor(pe, 0)

            def ring_fill(n, turn, w, cn):
                bank = cn.all % 2
                if len(cn.hist) >= 2:
                    vec, count = cn.hist[-2]
                    if vec:
                        wait(pe, "ring_vec", count, PER_VEC, turn)
                    else:
                        wait(pe, "ring_sca", count, PER_SCA, turn)
                cn.add(w)
                if w[0] == "A":
                    _, j, i, c = w
                    m = n + 1
                    if (j, c) == (0, 0) and i in (0, 4):
                        if i == 0:
                            count = upto(m - 2, ("q", 1)) if m - 2 >= -1 else len(FRONT)
                            wait(pe, "ring_sca", count, PER_SCA, turn)
                        else:
                            wait(pe, "ring_sca", upto(n, ("k", 1)), PER_SCA, turn)
                    k0, width = a_columns(i, c)
                    diag = i < 4 or c == 1
                    last = nc.tensor.matmul(psum[:, bank, 0:width], qs[m % 2][:, i * P:(i + 1) * P],
                                            kz[m % 2][:, j, k0:k0 + width], start=True, stop=not diag)
                    if diag:
                        d0 = P * i - k0
                        last = nc.tensor.matmul(psum[:, bank, d0:d0 + P], ident_b[:], mask_b[:],
                                                start=False, stop=True)
                    return last
                half = w[1]
                if w[0] == "o":
                    if half == 0:
                        wait(pe, "o_taken", n, 1, turn)
                    src = oT[:]
                elif w[0] == "k":
                    m = n + 2 if half == 0 else n + 1
                    wait(pe, "tok_ready", m + 1, 1, turn)
                    src = tk[m % 2][:].rearrange("p x r -> p (x r)")
                elif w[0] == "q":
                    wait(pe, "tok_ready", n + 3, 1, turn)
                    src = tq[n % 2][:].rearrange("p x r -> p (x r)")
                else:
                    wait(pe, "m_ready", n + 2, 1, turn)
                    src = tq[(n + 1) % 2][:].rearrange("p x r -> p (x r)")
                for t in range(TPC):
                    c0 = (half * TPC + t) * P
                    last = nc.tensor.transpose(psum[:, bank, t * P:(t + 1) * P], src[:, c0:c0 + P], ident)
                return last

            def pv(n, turn, jt):
                wait(pe, "diag_done", 4 * TPB * n + HPG * (jt + 1), 4 * TPB, turn)
                if jt == 0:
                    wait(pe, "v_ready", n + 1, 1, turn)
                    if n >= 1:
                        wait(pe, "o_taken", n, 1, turn)
                q0 = P * jt
                for bank in range(2):
                    lo, hi = max(q0, 512 * bank), 512 * (bank + 1)
                    if lo >= hi:
                        continue
                    for j in range(HPG):
                        last = nc.tensor.matmul(psum[32 * j:32 * j + 32, 6 + bank, lo - 512 * bank:512],
                                                Vs[n % 2][:, jt, j, :],
                                                pT[:, (jt % 2) * HPG + j, lo - q0:hi - q0],
                                                start=(jt == 0), stop=(jt == (3 if bank == 0 else TPB - 1)))
                last.then_inc(sem("pv_done"), 1)

            def body(n, turn):
                cn = Count(n, turn)
                fills = {}
                for u, w in ring_units(n):
                    fills.setdefault(u, []).append(w)
                for u in range(4 * TPB):
                    if n >= 0:
                        jt, j = divmod(u, HPG)
                        if u == 0:
                            wait(pe, "ring_sca", upto(n - 1, ("m", 1)), PER_SCA, turn)
                        if not (n == 0 and u < 2):
                            wait(pe, "exp_done", 4 * TPB * n + u - 1, 4 * TPB, turn)
                        bank = 2 + 2 * (u % 2)
                        for q0, width, b in b_columns(jt):
                            last = nc.tensor.matmul(psum[:, bank + b, 0:width],
                                                    kz[n % 2][:, j, jt * P:(jt + 1) * P],
                                                    qm[n % 2][:, q0:q0 + width], start=True, stop=True)
                        last.then_inc(sem("b_full"), 1)
                    if u == 1 and n >= 1:
                        pv(n - 1, turn, TPB - 1)
                    if n >= 0 and u % 4 == 3 and u >= 7:
                        pv(n, turn, u // 4 - 1)
                    for w in fills.get(u, ()):
                        ring_fill_signal(n, turn, w, cn)

            def ring_fill_signal(n, turn, w, cn):
                last = ring_fill(n, turn, w, cn)
                last.then_inc(sem("ring_full"), 1)

            cf = Count(-1, None)
            cf.all, cf.vec, cf.sca, cf.hist = 0, 0, 0, []
            for _, w in FRONT:
                ring_fill_signal(-2, None, w, cf)
            attention_iterations(pe, body)
            pv(NIT - 1, None, TPB - 1)
            ce = Count(NIT, None)
            for _, w in BACK:
                ring_fill_signal(NIT, None, w, ce)

            pe.wait_ge(sem("exp_done"), 4 * TPB * NIT)
            for c in range(NCH + 1):
                if c < NCH:
                    if c >= 2:
                        pe.wait_ge(sem("cT_ready"), c - 1)
                    pe.wait_ge(sem("cx_ready"), c + 1)
                    for t in range(TPC):
                        last = nc.tensor.transpose(psum[:, 2 + c % 2, t * P:(t + 1) * P], cx[:, TPC * c + t, :],
                                                   ident)
                    last.then_inc(sem("cT_done"), 1)
                if c >= 1:
                    k = c - 1
                    pe.wait_ge(sem("cT_ready"), k + 1)
                    if k >= 2:
                        pe.wait_ge(sem("proj_added"), k - 1)
                    for t in range(TPC):
                        last = nc.tensor.matmul(psum[:, 4 + k % 2, t * P:(t + 1) * P],
                                                cT[:, k % 2, t * P:(t + 1) * P], wo_sb[:], start=True, stop=True)
                    last.then_inc(sem("proj_done"), 1)
            pe.wait_ge(sem("w_split0"), 4)
            pe.wait_ge(sem("w2_in0"), 16)
            pe.wait_ge(sem("proj_added"), NCH)
            mixture_tensor(pe, 0)

            transposes_tensor(pe, 1)
            pe.wait_ge(sem("gwl_ready"), 1)
            pe.wait_ge(sem("xl_ready1"), NCH)
            for T in range(TT):
                t = slice(T * P, (T + 1) * P)
                last = split_product(psum[:, 6, T * EXPERTS:(T + 1) * EXPERTS], xh[:, t], xl[:, t], gwh[:], gwl[:])
            last.then_inc(sem("logits1"), 1)
            counts_tensor(pe, 1)
            pe.wait_ge(sem("rnn_lo"), 1)
            for m in range(RC * NCH):
                c, k = m // RC, m % RC
                if m >= 2:
                    pe.wait_ge(sem("g_ready"), m - 1)
                    pe.wait_ge(sem("sig_ready"), 3 * (m - 1))
                xr = slice(c * CHUNK, (c + 1) * CHUNK)
                for g in range(3):
                    wr = slice(g * RNN_E + k * P, g * RNN_E + (k + 1) * P)
                    last = split_product(psum[:, 3 * (m % 2) + g, :], rwh[:, wr], rwl[:, wr], xh[:, xr], xl[:, xr])
                last.then_inc(sem("rnn_mm"), 1)
            for c in range(NCH):
                pe.wait_ge(sem("scan_done"), RC * (c + 1))
                if c >= 2:
                    pe.wait_ge(sem("rnn_added"), c - 1)
                for t in range(TPC):
                    T = TPC * c + t
                    for k in range(RC):
                        last = nc.tensor.matmul(psum[:, 6 + c % 2, t * D:(t + 1) * D], hT[:, k, T * P:(T + 1) * P],
                                                rwd[:, k, :], start=(k == 0), stop=(k == RC - 1))
                last.then_inc(sem("rnn_out"), 1)
            pe.wait_ge(sem("v_split"), 1)
            pe.wait_ge(sem("v2_in"), 48)
            pe.wait_ge(sem("rnn_added"), NCH)
            mixture_tensor(pe, 1)

        def scatter_rows(g, l, first=0, end=TT):
            if first == 0:
                g.wait_ge(sem(f"slots_ready{l}"), 1)
                g.wait_ge(sem("pads_in"), 32)
            for i in range(first, end):
                for k in range(TOPK):
                    g.indirect_dma_start(xs[l], bass.IndirectOffsetOnAxis(ap=slot_i[:, k, i:i + 1], axis=0),
                                         rows[:, i, :], None).then_inc(sem(f"rows_sorted{l}"), 16)

        def mixture_gpsimd(g, l):
            b = tb[l]

            def step(s, dyn, c):
                if not 2 <= s:
                    return
                t = (c - 2) % 4
                g.wait_ge(sem(f"yo_ready{l}"), s - 1 if dyn is None else dyn + (s - 1))
                g.wait_ge(sem(f"dest_ready{l}"), s - 1 if dyn is None else dyn + (s - 1))
                if dyn is not None:
                    g.sem_inc(sem("pool_waited"), 1)
                g.indirect_dma_start(yc[l], bass.IndirectOffsetOnAxis(ap=destf[:, t:t + 1], axis=0),
                                     b.yo[:, t, :], None, bounds_check=TOPK * TOKENS - 1,
                                     oob_is_err=False).then_inc(sem(f"row_out{l}_{t}"), 16)
            mixture_steps(g, step)

        @block.gpsimd
        def _(g):
            def wait_alone(name, count, per, turn):
                wait(g, name, count, per, turn)
                if turn is not None:
                    g.sem_inc(sem("pool_waited"), 1)

            def heads(n, turn, a_):
                if turn is None:
                    return QK[:, a_, n, :, :]
                flat = QK[:].rearrange("p a n x d -> p (a n x d)")
                size = TPB * HPG * HD
                return flat[:, bass.ds(turn * size + (a_ * NIT + n) * size, size)].rearrange(
                    "p (x d) -> p x d", d=HD)

            def build(n, turn):
                par = n % 2
                wait_alone("tok_hi", 2 * n + 2, 2, turn)
                q, k = tq[par], tk[par]
                nc.gpsimd.tensor_tensor(q[:, :, 8:16], heads(n, turn, 0), q[:, :, 0:8], ALU.subtract)
                nc.gpsimd.tensor_copy(q[:, :, 16:24], q[:, :, 0:8])
                nc.gpsimd.memset(q[:, :, 24:26], 0.0)
                nc.gpsimd.tensor_copy(k[:, :, 8:16], k[:, :, 0:8])
                nc.gpsimd.tensor_tensor(k[:, :, 16:24], heads(n, turn, 1), k[:, :, 0:8],
                                        ALU.subtract).then_inc(sem("tok_ready"), 1)

            def values(n, turn):
                if n >= 2:
                    wait_alone("pv_done", TPB * (n - 1), TPB, turn)
                if turn is None:
                    src = Vn[:, n, :, :]
                else:
                    size = TPB * HPG * HD
                    src = Vn[:].rearrange("p n t r -> p (n t r)")[:, bass.ds(turn * size + n * size, size)].rearrange(
                        "p (t r) -> p t r", t=TPB)
                nc.gpsimd.tensor_copy(Vs[n % 2][:, :, :, 0:HD], src.rearrange("p t (j d) -> p t j d", j=HPG)).then_inc(
                    sem("v_ready"), 1)

            def body(n, turn):
                for u in range(4 * TPB):
                    if n >= 0:
                        jt, j = divmod(u, HPG)
                        wait_alone("exp_done", 4 * TPB * n + u + 1, 4 * TPB, turn)
                        blk = pT[:, (jt % 2) * HPG + j, 0:P]
                        nc.gpsimd.affine_select(out=blk, in_=blk, compare_op=ALU.is_ge, fill=0.0, base=0,
                                                pattern=[[1, P]], channel_multiplier=-1).then_inc(
                                                    sem("diag_done"), 1)
                    if u == 3 and n + 1 < NIT:
                        values(n + 1, turn)
                    if u == 10 and n + 2 < NIT:
                        build(n + 2, turn)
                    if turn is None and u % 4 == 2 and u >= 6:
                        if sorted_[0] < TT:
                            scatter_rows(g, 0, sorted_[0], sorted_[0] + 1)
                            sorted_[0] += 1

            sorted_ = [0]
            build(0, None)
            attention_iterations(g, body)
            scatter_rows(g, 0, sorted_[0], TT)
            mixture_gpsimd(g, 0)
            scatter_rows(g, 1)
            mixture_gpsimd(g, 1)


def kernel(**inputs):
    import concourse.bacc as bacc
    from concourse import mybir as mb
    from concourse.bass_utils import run_bass_kernel_spmd

    f = {k: np.asarray(v) for k, v in inputs.items()}

    def cat(*xs):
        return np.ascontiguousarray(np.concatenate(xs, axis=1))

    A = "L0_attn_"
    arrays = {
        "x": f[A + "x"], "consts": constants(),
        "w_cat": cat(*(f[A + "w" + n].T for n in "qkv"), f["L0_ffn_Wr"]),
        "lora_a": cat(*(f[A + "a" + n] for n in "qkvo")),
        "lora_b": cat(*(f[A + "b" + n].T for n in "qkvo")),
        "wo_t": f[A + "wo"].T,
        "W1": f["L0_ffn_W1"], "W2": f["L0_ffn_W2"], "W3": f["L0_ffn_W3"],
        "rnn_w": f["L1_attn_W"].T, "rnn_b": f["L1_attn_b"].reshape(-1, P).T, "rnn_wd": f["L1_attn_Wd"].T,
        "gate_w": f["L1_ffn_gate_w"], "gate_b": f["L1_ffn_gate_b"], "w1": f["L1_ffn_w1"], "b1": f["L1_ffn_b1"],
        "w2": f["L1_ffn_w2"], "b2": f["L1_ffn_b2"],
    }
    nc = bacc.Bacc("TRN2", target_bir_lowering=False, num_devices=1)
    feed, args = {}, []
    for name, a in arrays.items():
        a = np.ascontiguousarray(a)
        feed[f"in_{name}"] = a
        args.append(nc.dram_tensor(f"in_{name}", a.shape, mb.dt.from_np(a.dtype), kind="ExternalInput").ap())
    args.append(nc.dram_tensor("out_x", f[A + "x"].shape, mb.dt.from_np(f[A + "x"].dtype),
                               kind="ExternalOutput").ap())
    program(nc, *args)
    r = run_bass_kernel_spmd(nc, [feed], core_ids=[0])
    return r.results[0]["out_x"]
```

```python
from contextlib import ExitStack

import concourse.bass as bass
import concourse.mybir as mybir
import numpy as np

F32 = mybir.dt.float32
F32R = mybir.dt.float32r
BF16 = mybir.dt.bfloat16
I32 = mybir.dt.int32
ALU = mybir.AluOpType
ACT = mybir.ActivationFunctionType
AX = mybir.AxisListType.X

P = 128
D = 128
BATCH, SEQ = 4, 1024
TOKENS = BATCH * SEQ
TT = TOKENS // P
TPB = SEQ // P
CHUNK = 512
NCH = TOKENS // CHUNK
TPC = CHUNK // P
HEADS, HD = 16, 8
GROUPS, HPG = 4, 4
NIT = GROUPS * BATCH
EXPERTS, FF, TOPK = 8, 512, 2
FC = FF // P
SLOT_TILES = TOPK * TOKENS // P + EXPERTS - 1
ROW = D + 2
SKIP = float(1 << 20)
BIG = 3.0e38
LORA_RANK = 16
OUTS = 8
RNN_E = 256
RC = RNN_E // P
EPS = 1e-5
MASKED = -1.0e30

C_ID, C_MASK, C_TRI, C_ONES, C_RMASK = 0, 128, 256, 384, 512
C_PRIO = C_RMASK + TT * EXPERTS
C_IOTA = C_PRIO + EXPERTS
C_HEAD = C_IOTA + SLOT_TILES
C_TOK2 = C_HEAD + HPG
C_PART = C_TOK2 + TT
C_END = C_PART + SLOT_TILES


def constants():
    c = np.zeros((P, C_END), np.float32)
    c[:, C_ID:C_ID + P] = np.eye(P)
    c[:, C_MASK:C_MASK + P] = np.triu(np.full((P, P), MASKED), 1)
    c[:, C_TRI:C_TRI + P] = np.triu(np.ones((P, P)), 1)
    c[:, C_ONES:C_ONES + P] = 1.0
    c[:, C_RMASK:C_PRIO] = np.tile(np.arange(TT) > 0, EXPERTS)
    c[:, C_PRIO:C_IOTA] = EXPERTS - np.arange(EXPERTS)
    c[:, C_IOTA:C_HEAD] = np.arange(SLOT_TILES)
    c[:, C_HEAD:C_TOK2] = np.arange(P)[:, None] // 32 == np.arange(HPG)[None]
    c[:, C_TOK2:C_PART] = 2 * (np.arange(TT)[None] * P + np.arange(P)[:, None])
    c[:, C_PART:] = np.arange(SLOT_TILES)[None] * P + np.arange(P)[:, None]
    return c


def program(nc, x, consts, w_cat, lora_a, lora_b, wo_t, W1, W2, W3, rnn_w, rnn_b, rnn_wd,
            gate_w, gate_b, w1, b1, w2, b2, out):
    xs = [nc.dram_tensor(f"sorted_rows_{l}", (SLOT_TILES * P, ROW), F32).ap() for l in range(2)]
    bias_rows = nc.dram_tensor("bias_rows", (3, EXPERTS * (FF + D)), BF16).ap()
    yc = [nc.dram_tensor(f"expert_rows_{l}", (TOPK * TOKENS, D), F32).ap() for l in range(2)]

    ctx = ExitStack()
    with ctx:
        base = (nc.sbuf_base + 63) // 64 * 64
        total = 212736
        ctx.enter_context(nc.sbuf_tensor("arena", [P, total // 4], F32))
        names = [0]

        def at(name, off, shape, dt=F32):
            n = int(np.prod(shape)) * (2 if dt == BF16 else 4)
            assert off + n <= total, (name, off, n)
            names[0] += 1
            return nc.alloc_sbuf_tensor_at(name, [P] + list(shape), dt, offset=base + off)

        pos_ = [0]

        def keep(name, shape, dt=F32):
            t = at(name, pos_[0], shape, dt)
            pos_[0] += (int(np.prod(shape)) * (2 if dt == BF16 else 4) + 31) // 32 * 32
            return t

        xres = keep("xres", [TT, D])
        rows = keep("rows", [TT, ROW])
        cst = keep("cst", [C_END])
        ident_b = keep("ident_b", [P], BF16)
        mask_b = keep("mask_b", [P], BF16)
        ones_b = keep("ones_b", [P], BF16)
        gate_wt = keep("gate_wt", [TOPK, TT])
        slot_i = keep("slot_i", [TOPK, TT], I32)
        tile_expert = keep("tile_expert", [SLOT_TILES], I32)
        wo_sb = keep("wo_sb", [D])
        bn6 = keep("bn6", [8, 6])
        mv = keep("mv", [8, 2])
        rs = keep("rs", [8])
        rt = keep("rt", [8])
        sd = keep("sd", [8])
        small = keep("small", [12, EXPERTS])
        smalli = keep("smalli", [EXPERTS], I32)
        gbias = keep("gbias", [EXPERTS])
        gw_sb = keep("gw_sb", [EXPERTS])
        gwh = keep("gwh", [EXPERTS], F32R)
        gwl = keep("gwl", [EXPERTS], F32R)
        rnn_bias = keep("rnn_bias", [3 * RC])
        rnn_bh = keep("rnn_bh", [RC])
        destf = keep("destf", [OUTS], I32)
        negm = keep("negm", [HPG, TPB])
        negh = keep("negh", [HPG, TPB], F32R)
        mall = keep("mall", [HPG, TPB])
        mtwo = keep("mtwo", [HPG, TPB // 2, 2])
        recip = keep("recip", [2, TPC, HPG])
        Z = (pos_[0] + 63) // 64 * 64

        ident = cst[:, C_ID:C_ID + P]
        prio = cst[:, C_PRIO:C_PRIO + EXPERTS]

        kz = [at(f"kz{i}", Z + 16384 * i, [HPG, SEQ], F32R) for i in range(2)]
        QK = at("QK", Z + 32768, [2, NIT, TPB * HPG, HD])
        Vn = at("Vn", Z + 65536, [NIT, TPB, HPG * HD])
        qs = [at(f"qs{i}", Z + 81920 + 4096 * i, [SEQ], F32R) for i in range(2)]
        qm = [at(f"qm{i}", Z + 90112 + 4096 * i, [SEQ], F32R) for i in range(2)]
        tq = [at(f"tq{i}", Z + 98304 + 4096 * i, [TPB * HPG, 32]) for i in range(2)]
        tk = [at(f"tk{i}", Z + 106496 + 4096 * i, [TPB * HPG, 32]) for i in range(2)]
        Vs = [at(f"Vs{i}", Z + 114688 + 4096 * i, [TPB, HPG, 32]) for i in range(2)]
        pT = at("pT", Z + 122880, [4 * HPG, CHUNK])
        oT = at("oT", Z + 155648, [SEQ])
        xh = at("xh", Z, [TOKENS], F32R)
        xl = at("xl", Z + 16384, [TOKENS], F32R)
        NW = 3 * D + EXPERTS
        wraw = at("wraw", Z + 81920, [NW])
        wh = at("wh", Z + 81920 + 2048, [NW], F32R)
        wl = at("wl", Z + 81920 + 4096, [NW], F32R)
        wo_raw = at("wo_raw", Z + 81920 + 6144, [D])
        la = at("la", Z + 81920 + 8192, [4 * D])
        lb = at("lb", Z + 81920 + 10240, [4 * D])
        pad_rows = at("pad_rows", Z + 81920 + 12288, [ROW])
        R0 = Z + 114688
        lg = at("lg", R0, [TT, EXPERTS])
        ra = at("ra", R0 + 1024, [TT, EXPERTS])
        rb = at("rb", R0 + 2048, [TT, EXPERTS])
        ch0 = at("ch0", R0 + 3072, [TT, EXPERTS])
        ch1 = at("ch1", R0 + 4096, [TT, EXPERTS])
        cnt = at("cnt", R0 + 5120, [EXPERTS, TT])
        run = at("run", R0 + 6144, [EXPERTS, TT])
        tcmp = at("tcmp", R0 + 7168, [SLOT_TILES, EXPERTS])
        r1 = at("r1", R0 + 10240, [12, TT])

        cT = at("cT", Z + 155648, [2, CHUNK])
        cx = at("cx", Z + 138240, [TT, D])
        W1h = at("W1h", Z + 32768, [EXPERTS * FF], F32R)
        W1l = at("W1l", Z + 49152, [EXPERTS * FF], F32R)
        W3h = at("W3h", Z, [EXPERTS * FF], F32R)
        W3l = at("W3l", Z + 16384, [EXPERTS * FF], F32R)
        W2s = at("W2s", Z + 81920, [EXPERTS * FC * D])
        wst = [at(f"wst{i}", Z + 98304 + 8192 * i, [4 * FF]) for i in range(2)]

        class TileBufs:
            def __init__(self, l, o):
                self.xg = at(f"xg{l}", o, [8, ROW])
                o += 8 * ROW * 4
                self.gh = at(f"gh{l}", o, [2, D], F32R)
                self.gl = at(f"gl{l}", o + 1024, [2, D], F32R)
                self.s1 = at(f"s1{l}", o + 2048, [2, FF])
                self.act = at(f"act{l}", o + 2048 + 4096, [2, FF])
                self.aT = at(f"aT{l}", o + 2048 + 8192, [2, FF])
                self.yo = at(f"yo{l}", o + 2048 + 12288, [OUTS, D])

        tb = [TileBufs(0, Z + 114688), TileBufs(1, Z)]
        yback = [at("yback0", Z + 32768, [TT, TOPK, D]), at("yback1", Z + 32768, [TT, TOPK, D])]
        hT = at("hT", Z + 32768, [RC, TOKENS])
        rw = at("rw", Z + 65536, [3 * RNN_E])
        rwh = at("rwh", Z + 65536 + 3072, [3 * RNN_E], F32R)
        rwl = at("rwl", Z + 65536 + 6144, [3 * RNN_E], F32R)
        rwd = at("rwd", Z + 65536 + 9216, [RC, D])
        gf = at("gf", Z + 75776, [2, CHUNK])
        gi = at("gi", Z + 75776 + 4096, [2, CHUNK])
        gs = at("gs", Z + 75776 + 8192, [2, CHUNK])
        gv = at("gv", Z + 75776 + 12288, [2, CHUNK])
        gg = at("gg", Z + 75776 + 16384, [2, CHUNK])
        V1h = at("V1h", Z + 96256, [EXPERTS * FF], F32R)
        V1l = at("V1l", Z + 96256 + 16384, [EXPERTS * FF], F32R)
        V2s = at("V2s", Z + 96256 + 32768, [EXPERTS * FC * D])
        vraw = at("vraw", Z + 96256 + 49152, [EXPERTS * FF])
        BZ = EXPERTS * (FF + D)
        bz = at("bz", total - 2 * BZ, [BZ], BF16)
        NB1 = FF + D
        S0 = Z + 130048
        bias_c = at("bias_c", S0, [NB1])
        bias_r = at("bias_r", S0 + 4 * NB1, [2, NB1])
        bias_p = at("bias_p", S0 + 12 * NB1, [3, NB1], BF16)

        psum = ctx.enter_context(nc.psum_tensor("psum", [P, 8, 512], F32))

        sems = {}

        def sem(name):
            if name not in sems:
                sems[name] = ctx.enter_context(nc.semaphore(name))
            return sems[name]

        chained = {}

        def chain(eng, name):
            s = sem(name)

            def done(ins):
                chained[name] = chained.get(name, 0) + 1
                ins.then_inc(s, 1)
                eng.wait_ge(s, chained[name])
            return done

        block = ctx.enter_context(nc.Block())

        RING, SCORES, OUT = 4, 3, 7
        GROUPED = [(0, jt) for jt in range(TPB // 2)] + [(1, jt) for jt in range(TPB)]
        NG_ = len(GROUPED)
        NB = HPG * NG_
        DIAG = [g for g, (h, jt) in enumerate(GROUPED) if P * jt >= CHUNK * h]
        A_END = 42

        def a_columns(i, c):
            if i < 4:
                return 0, max(256, P * (i + 1))
            half = 64 * (i + 1)
            return c * half, half

        def b_columns(g):
            h, jt = GROUPED[g]
            q0 = max(P * jt, CHUNK * h)
            width = CHUNK * (h + 1) - q0
            return q0, width, max(256 - width, 0)

        def ring_units(n):
            nxt, nxt2 = n + 1 < NIT, n + 2 < NIT
            a = [("A", j, i, 0) for i in range(2) for j in range(0, HPG, 2)]
            a += [("A", j, i, 0) for i in range(2, 4) for j in range(HPG)]
            a += [("A", j, i, c) for i in range(4, TPB) for j in range(HPG) for c in range(2)]
            cost_b = [b_columns(u // HPG)[1] + 64 for u in range(A_END)]
            cost_a = [a_columns(w[2], w[3])[1] * (2 if w[2] < 2 else 1) + 64 for w in a]
            units, given = [], 0
            for u in range(NB):
                if nxt:
                    due = sum(cost_a) * sum(cost_b[:u + 1]) / sum(cost_b)
                    while given < len(a) and sum(cost_a[:given + 1]) <= due + 1:
                        units.append((u, a[given]))
                        given += 1
                if u == 5 and nxt:
                    units.append((u, ("k", 1)))
                if u == 9 and n >= 1:
                    units.append((u, ("o", 1)))
                if u == 27 and n >= 0:
                    units.append((u, ("o", 0)))
                if u == 34 and nxt2:
                    units.append((u, ("k", 0)))
                if u in (36, 38) and nxt2:
                    units.append((u, ("q", (u - 36) // 2)))
                if u in (45, 46) and nxt:
                    units.append((u, ("m", u - 45)))
            return units

        by_vector = ("A", "o")
        FRONT = [(0, ("k", 0)), (0, ("q", 0)), (0, ("q", 1))]
        BACK = [(0, ("o", 1))]

        def ring_before(n):
            units = list(FRONT)
            for k in range(-1, n):
                units += ring_units(k)
            v = sum(1 for _, w in units if w[0] in by_vector)
            return len(units), v, len(units) - v

        class Count:
            def __init__(self, n, turn):
                self.all, self.vec, self.sca = ring_before(n)
                self.hist = []
                v = c = 0
                for _, w in FRONT + [w for k in range(-1, n) for w in ring_units(k)]:
                    if w[0] in by_vector:
                        v += 1
                    else:
                        c += 1
                    self.hist.append((w[0] in by_vector, v if w[0] in by_vector else c))

            def add(self, w):
                if w[0] in by_vector:
                    self.vec += 1
                    self.hist.append((True, self.vec))
                else:
                    self.sca += 1
                    self.hist.append((False, self.sca))
                self.all += 1

        STEADY = ring_units(2)
        PER_ALL = len(STEADY)
        PER_VEC = sum(1 for _, w in STEADY if w[0] in by_vector)
        PER_SCA = PER_ALL - PER_VEC
        assert 2 * PER_ALL % RING == 0 and NB % SCORES == 0 and NG_ % 4 == 0 and len(ring_units(1)) == PER_ALL and len(ring_units(NIT - 3)) == PER_ALL

        def upto(n, name):
            s = ring_before(n)[2]
            for _, w in ring_units(n):
                if w[0] not in by_vector:
                    s += 1
                    if w == name:
                        return s
            raise ValueError(name)

        def all_upto(n, name):
            a = ring_before(n)[0]
            for _, w in ring_units(n):
                a += 1
                if w == name:
                    return a
            raise ValueError(name)

        def attention_iterations(eng, body):
            for n in (-1, 0, 1):
                body(n, None)
            with eng.Fori(0, NIT - 5, 2) as turn:
                body(2, turn)
                body(3, turn)
            for n in (NIT - 2, NIT - 1):
                body(n, None)

        def wait(eng, name, count, per, turn):
            if turn is None:
                if count > 0:
                    eng.wait_ge(sem(name), count)
            else:
                assert count > 0
                eng.wait_ge(sem(name), turn * per + count)

        def mixture_loads(sp, l):
            sp.wait_ge(sem(f"rows_sorted{l}"), 16 * TOPK * TT)
            if l == 1:
                sp.wait_ge(sem("rnn_mm"), RC * NCH)
            for s in range(8):
                sp.dma_start(tb[l].xg[:, s, :], xs[l][s * P:(s + 1) * P, :]).then_inc(sem(f"row_in{l}_{s}"), 16)
            steady = (SLOT_TILES - 8) // 8 * 8
            with sp.Fori(0, steady - 7, 8) as s0:
                for c in range(8):
                    sp.wait_ge(sem(f"dest_ready{l}"), s0 + (c + 1))
                    sp.dma_start(tb[l].xg[:, c, :], xs[l][bass.ds((s0 + (8 + c)) * P, P), :]).then_inc(
                        sem(f"row_in{l}_{c}"), 16)
            for s in range(steady + 8, SLOT_TILES):
                sp.wait_ge(sem(f"dest_ready{l}"), s - 7)
                sp.dma_start(tb[l].xg[:, s % 8, :], xs[l][s * P:(s + 1) * P, :]).then_inc(
                    sem(f"row_in{l}_{s % 8}"), 16)

        def rows_back(sp, l):
            for c in range(OUTS):
                sp.wait_ge(sem(f"row_out{l}_{c}"), 16 * len(range(c, SLOT_TILES, OUTS)))
            v = yc[l].rearrange("(i p k) d -> p i k d", p=P, k=TOPK)
            for c in range(4):
                sp.dma_start(yback[l][:, 8 * c:8 * c + 8], v[:, 8 * c:8 * c + 8]).then_inc(sem(f"back{l}_{c}"), 16)

        @block.sync
        def _(sp):
            sp.dma_start(cst[:], consts).then_inc(sem("const_in"), 16)
            xv = x.rearrange("b (i p) d -> p (b i) d", p=P)
            for c in range(4):
                sp.dma_start(xres[:, 8 * c:8 * c + 8], xv[:, 8 * c:8 * c + 8]).then_inc(sem(f"x_in{c}"), 16)
            sp.wait_ge(sem("pad_ready"), 2)
            for l in range(2):
                sp.dma_start(xs[l].rearrange("(s p) r -> p s r", p=P),
                             pad_rows[:].unsqueeze(1).to_broadcast([P, SLOT_TILES, ROW])).then_inc(
                                 sem("pads_in"), 16)
            sp.wait_ge(sem("bias_split"), 5)
            sp.wait_ge(sem("bz_zeroed"), 1)
            for first, width in ((0, FF), (FF, D)):
                sp.dma_start(bias_rows[:, EXPERTS * first:EXPERTS * (first + width)].rearrange(
                    "k (e f) -> e k f", e=EXPERTS), bias_p[0:EXPERTS, :, first:first + width]).then_inc(
                        sem("bias_rows_out"), 16)
            sp.wait_ge(sem("bias_rows_out"), 32)
            sp.dma_start(bz[0:3, :], bias_rows).then_inc(sem("bz_in"), 16)
            sp.wait_ge(sem("ring_full"), all_upto(NIT - 2, ("m", 1)))
            for n in range(4):
                src = (W1, W3)[n // 2].rearrange("e d f -> d e f")[:, 4 * (n % 2):4 * (n % 2) + 4, :]
                if n >= 2:
                    sp.wait_ge(sem("w_split0"), n - 1)
                sp.dma_start(wst[n % 2][:].rearrange("p (e f) -> p e f", e=4), src).then_inc(sem(f"w_in0_{n}"), 16)
            sp.wait_ge(sem("b_full"), NB * NIT)
            sp.dma_start(W2s[:].rearrange("p (e c d) -> p e c d", e=EXPERTS, c=FC),
                         W2.rearrange("e (c p) d -> p e c d", p=P)).then_inc(sem("w2_in0"), 16)
            sp.wait_ge(sem("pv_done"), NG_ * NIT)
            mixture_loads(sp, 0)
            rows_back(sp, 0)
            sp.wait_ge(sem("y_ready0"), SLOT_TILES)
            sp.dma_start(rw[:], rnn_w).then_inc(sem("rnn_in"), 16)
            sp.dma_start(rwd[:], rnn_wd.rearrange("(c p) d -> p c d", p=P)).then_inc(sem("rnn_in"), 16)
            sp.dma_start(rnn_bias[:], rnn_b).then_inc(sem("rnn_in"), 16)
            sp.dma_start(vraw[:].rearrange("p (e f) -> p e f", e=EXPERTS),
                         w1.rearrange("e d f -> d e f")).then_inc(sem("v_in"), 16)
            sp.dma_start(V2s[:].rearrange("p (e c d) -> p e c d", e=EXPERTS, c=FC),
                         w2.rearrange("e (c p) d -> p e c d", p=P)).then_inc(sem("v2_in"), 16)
            mixture_loads(sp, 1)
            rows_back(sp, 1)
            ov = out.rearrange("b (i p) d -> p (b i) d", p=P)
            for c in range(4):
                sp.wait_ge(sem("combined1"), c + 1)
                sp.dma_start(ov[:, 8 * c:8 * c + 8], xres[:, 8 * c:8 * c + 8]).then_inc(sem("out_done"), 16)
            sp.wait_ge(sem("out_done"), 64)

        def qkv_out(copy, T):
            b, t = divmod(T, TPB)
            src = psum[:, 2 + T % 4, 0:NW]
            for a in range(2):
                dst = QK[:, a, b::BATCH, t * HPG:(t + 1) * HPG, :].rearrange("p g j d -> p g (j d)")
                copy(dst, src[:, a * D:(a + 1) * D].rearrange("p (g r) -> p g r", g=GROUPS))
            copy(Vn[:, b::BATCH, t, :], src[:, 2 * D:3 * D].rearrange("p (g r) -> p g r", g=GROUPS))
            return copy(lg[:, T, :], src[:, 3 * D:NW])

        def norm_vector(v, l, done):
            for c in range(4):
                if l == 0:
                    v.wait_ge(sem(f"x_in{c}"), 16)
                for i in range(8):
                    last = nc.vector.bn_stats(bn6[:, i, :], xres[:, 8 * c + i, :])
                done(last)
                for i in range(8):
                    last = nc.vector.bn_aggr(mv[:, i, :], bn6[:, i, :])
                done(last)
                nc.vector.tensor_scalar(rt[:], mv[:, :, 1], EPS, None, ALU.add).then_inc(sem(f"var_ready{l}"), 1)
                v.wait_ge(sem(f"sd_ready{l}"), c + 1)
                done(nc.vector.reciprocal(rs[:], sd[:]))
                done(nc.vector.tensor_tensor(sd[:], rs[:], rs[:], ALU.mult))
                done(nc.vector.tensor_tensor(sd[:], sd[:], rt[:], ALU.mult))
                done(nc.vector.tensor_scalar(sd[:], sd[:], -0.5, 1.5, ALU.mult, ALU.add))
                done(nc.vector.tensor_tensor(rs[:], rs[:], sd[:], ALU.mult))
                for i in range(8):
                    last = nc.vector.tensor_scalar(rows[:, 8 * c + i, 0:D], xres[:, 8 * c + i, :],
                                                   mv[:, i, 0:1], rs[:, i:i + 1], ALU.subtract, ALU.mult)
                last.then_inc(sem(f"xn_ready{l}"), 1)
                v.wait_ge(sem(f"xn_ready{l}"), c + 1)

        def lo_vector(v, l):
            for c in range(NCH):
                v.wait_ge(sem(f"xh_ready{l}"), c + 1)
                nc.vector.tensor_tensor(xl[:, c * CHUNK:(c + 1) * CHUNK], psum[:, c % 2, :],
                                        xh[:, c * CHUNK:(c + 1) * CHUNK].bitcast(F32),
                                        ALU.subtract).then_inc(sem(f"xl_ready{l}"), 1)

        def router_vector(v, l, done):
            def bc(t):
                return t.unsqueeze(2).to_broadcast([P, TT, EXPERTS])
            prio_b = prio.unsqueeze(1).to_broadcast([P, TT, EXPERTS])
            top0, top1, w, q0, q1, z = (r1[:, i, :] for i in range(6))
            if l == 1:
                done(nc.vector.tensor_tensor(lg[:], lg[:], gbias[:].unsqueeze(1).to_broadcast([P, TT, EXPERTS]),
                                             ALU.add))
            done(nc.vector.tensor_reduce(top0, lg[:], AX, ALU.max))
            done(nc.vector.tensor_tensor(ra[:], lg[:], bc(top0), ALU.is_equal))
            done(nc.vector.tensor_tensor(rb[:], ra[:], prio_b, ALU.mult))
            done(nc.vector.tensor_reduce(w, rb[:], AX, ALU.max))
            done(nc.vector.tensor_tensor(ch0[:], prio_b, bc(w), ALU.is_equal))
            done(nc.vector.scalar_tensor_tensor(ra[:], ch0[:], -BIG, lg[:], ALU.mult, ALU.add))
            done(nc.vector.tensor_reduce(top1, ra[:], AX, ALU.max))
            done(nc.vector.tensor_tensor(rb[:], ra[:], bc(top1), ALU.is_equal))
            done(nc.vector.tensor_tensor(ra[:], rb[:], prio_b, ALU.mult))
            done(nc.vector.tensor_reduce(w, ra[:], AX, ALU.max))
            done(nc.vector.tensor_tensor(ch1[:], prio_b, bc(w), ALU.is_equal))
            nc.vector.tensor_tensor(q0, top1, top0, ALU.subtract).then_inc(sem(f"gate_diff{l}"), 1)
            if l == 1:
                nc.vector.tensor_tensor(lg[:], lg[:], bc(top0), ALU.subtract).then_inc(sem(f"gate_diff{l}"), 1)
            done(nc.vector.tensor_tensor(cnt[:].rearrange("p e i -> p i e"), ch0[:], ch1[:], ALU.add))
            done(nc.vector.tensor_tensor_scan(run[:].rearrange("p e i -> p (e i)"),
                                              cst[:, C_RMASK:C_PRIO], cnt[:].rearrange("p e i -> p (e i)"),
                                              0.0, ALU.mult, ALU.add))
            nc.vector.tensor_copy(small[:, 0, :], run[:, :, TT - 1]).then_inc(sem(f"count_ready{l}"), 1)
            v.wait_ge(sem(f"count_sums{l}"), 1)
            done(nc.vector.tensor_copy(small[:, 1, :], psum[:, 7, 0:EXPERTS]))
            done(nc.vector.tensor_scalar(smalli[:], psum[:, 7, EXPERTS:2 * EXPERTS], float(P - 1), None, ALU.add))
            done(nc.vector.tensor_scalar(smalli[:], smalli[:], 7, None, ALU.logical_shift_right))
            done(nc.vector.tensor_copy(small[:, 2, :], smalli[:]))
            done(nc.vector.tensor_tensor_scan(small[:, 3, :], cst[:, C_ONES:C_ONES + EXPERTS], small[:, 2, :],
                                              0.0, ALU.mult, ALU.add))
            done(nc.vector.tensor_tensor(small[:, 4, :], small[:, 3, :], small[:, 2, :], ALU.subtract))
            done(nc.vector.tensor_scalar(small[:, 4, :], small[:, 4, :], float(P), -1.0, ALU.mult, ALU.add))
            done(nc.vector.tensor_tensor(small[:, 4, :], small[:, 4, :], small[:, 1, :], ALU.add))
            done(nc.vector.tensor_tensor(run[:], run[:], small[:, 4, :].unsqueeze(2).to_broadcast([P, EXPERTS, TT]),
                                         ALU.add))
            run_v = run[:].rearrange("p e i -> p i e")
            for k, ch in enumerate((ch0, ch1)):
                done(nc.vector.tensor_tensor(ra[:], run_v, ch[:], ALU.mult))
                done(nc.vector.tensor_reduce(r1[:, 6 + k, :], ra[:], AX, ALU.add))
            iota = cst[:, C_IOTA:C_HEAD].unsqueeze(2).to_broadcast([P, SLOT_TILES, EXPERTS])
            ends = small[:, 3, :].unsqueeze(1).to_broadcast([P, SLOT_TILES, EXPERTS])
            done(nc.vector.tensor_tensor(tcmp[:], iota, ends, ALU.is_ge))
            ended = cnt[:].rearrange("p e i -> p (e i)")[:, 0:SLOT_TILES]
            done(nc.vector.tensor_reduce(ended, tcmp[:], AX, ALU.add))
            done(nc.vector.tensor_scalar(tile_expert[:], ended, float(EXPERTS - 1), None, ALU.min))
            done(nc.vector.tensor_copy(slot_i[:], r1[:, 6:8, :]))
            done(nc.vector.tensor_copy(rows[:, :, D], cst[:, C_TOK2:C_PART]))
            nc.vector.tensor_copy(rows[:, :, D + 1], r1[:, 6, :]).then_inc(sem(f"slots_ready{l}"), 1)
            if l == 0:
                v.wait_ge(sem("gate_exp0"), 1)
                done(nc.vector.tensor_scalar(z, q1, 1.0, None, ALU.add))
                done(nc.vector.reciprocal(gate_wt[:, 0, :], z))
                done(nc.vector.tensor_tensor(gate_wt[:, 1, :], q1, gate_wt[:, 0, :], ALU.mult))
            else:
                v.wait_ge(sem("gate_exp1"), 2)
                done(nc.vector.tensor_reduce(z, lg[:], AX, ALU.add))
                done(nc.vector.reciprocal(q0, z))
                done(nc.vector.tensor_tensor(q1, q1, q0, ALU.mult))
                done(nc.vector.tensor_tensor(z, q0, q1, ALU.add))
                done(nc.vector.tensor_scalar(z, z, 1e-9, None, ALU.add))
                done(nc.vector.reciprocal(w, z))
                done(nc.vector.tensor_tensor(gate_wt[:, 0, :], q0, w, ALU.mult))
                done(nc.vector.tensor_tensor(gate_wt[:, 1, :], q1, w, ALU.mult))

        LOOP_FROM = 16
        LOOP_TURNS = (SLOT_TILES - LOOP_FROM) // 8

        def mixture_steps(eng, step):
            for s in range(LOOP_FROM):
                step(s, None, s % 8)
            with eng.Fori(0, 8 * LOOP_TURNS - 7, 8) as dyn:
                for c in range(8):
                    step(LOOP_FROM + c, dyn, c)
            for s in range(LOOP_FROM + 8 * LOOP_TURNS, SLOT_TILES + 3):
                step(s, None, s % 8)

        def mixture_vector(v, l):
            b = tb[l]

            def step(s, dyn, c):
                def w(name, count, per=1):
                    v.wait_ge(sem(name), count if dyn is None else dyn * per + count)
                if s < SLOT_TILES:
                    w(f"gh_ready{l}", s + 1)
                    nc.vector.tensor_tensor(b.gl[:, c % 2, :], psum[:, 0, 0:P], b.gh[:, c % 2, :].bitcast(F32),
                                            ALU.subtract).then_inc(sem(f"gl_ready{l}"), 1)
                if l == 0 and 1 <= s <= SLOT_TILES:
                    t = (c - 1) % 2
                    w("silu_ready0", s)
                    w("h_ready0", 2 * s, 2)
                    if s >= 3:
                        w("aT_in0", s - 2)
                    nc.vector.tensor_tensor(b.act[:, t, :], b.s1[:, t, :], psum[:, 3 + t, :],
                                            ALU.mult).then_inc(sem("act_ready0"), 1)
                if s < SLOT_TILES:
                    if s >= OUTS:
                        v.wait_ge(sem(f"row_out{l}_{c}"), 16 * (s // OUTS)) if dyn is None else \
                            v.wait_ge(sem(f"row_out{l}_{c}"), dyn * 2 + 16 * (s // OUTS))
                    slot_id = cst[:, C_PART + s:C_PART + s + 1] if dyn is None else \
                        cst[:, bass.ds(dyn + (C_PART + s), 1)]
                    nc.vector.tensor_scalar(destf[:, c:c + 1], slot_id, b.xg[:, c % 8, D + 1:D + 2],
                                            b.xg[:, c % 8, D:D + 1], ALU.not_equal, ALU.add).then_inc(
                                                sem(f"dest_ready{l}"), 1)
            mixture_steps(v, step)

        def combine_vector(v, l, done):
            for c in range(4):
                v.wait_ge(sem(f"back{l}_{c}"), 16)
                for i in range(8 * c, 8 * c + 8):
                    last = nc.vector.scalar_tensor_tensor(xres[:, i, :], yback[l][:, i, 0, :],
                                                          gate_wt[:, 0, i:i + 1], xres[:, i, :], ALU.mult, ALU.add)
                done(last)
                for i in range(8 * c, 8 * c + 8):
                    last = nc.vector.scalar_tensor_tensor(xres[:, i, :], yback[l][:, i, 1, :],
                                                          gate_wt[:, 1, i:i + 1], xres[:, i, :], ALU.mult, ALU.add)
                last.then_inc(sem(f"combined{l}"), 1)
            v.wait_ge(sem(f"combined{l}"), 4)

        @block.vector
        def _(v):
            done = chain(v, "vector_step")
            nc.vector.memset(pad_rows[:, 0:D], 0.0).then_inc(sem("pad_ready"), 1)
            v.wait_ge(sem("pad_ready"), 1)
            nc.vector.memset(pad_rows[:, D:ROW], SKIP).then_inc(sem("pad_ready"), 1)
            v.wait_ge(sem("const_in"), 16)
            nc.vector.tensor_copy(ident_b[:], ident)
            nc.vector.tensor_copy(ones_b[:], cst[:, C_ONES:C_ONES + P])
            nc.vector.tensor_copy(mask_b[:], cst[:, C_MASK:C_MASK + P]).then_inc(sem("bf_consts"), 1)
            norm_vector(v, 0, done)
            v.wait_ge(sem("lora_prod"), 1)
            done(nc.vector.scalar_tensor_tensor(wraw[:, 0:3 * D], psum[:, 6, 0:3 * D], 1.0 / LORA_RANK,
                                                wraw[:, 0:3 * D], ALU.mult, ALU.add))
            nc.vector.scalar_tensor_tensor(wo_sb[:], psum[:, 6, 3 * D:4 * D], 1.0 / LORA_RANK,
                                           wo_raw[:], ALU.mult, ALU.add).then_inc(sem("w_ready"), 1)
            v.wait_ge(sem("wh_ready"), 1)
            nc.vector.tensor_tensor(wl[:], wraw[:], wh[:].bitcast(F32), ALU.subtract).then_inc(sem("wl_ready"), 1)
            lo_vector(v, 0)
            for T in range(1, TT, 2):
                v.wait_ge(sem("qkv_done"), T + 1)
                last = qkv_out(nc.vector.tensor_copy, T)
                last.then_inc(sem("qkv_vec"), 1)
            v.wait_ge(sem("qkv_sca"), TT // 2)
            v.wait_ge(sem("qkv_vec"), TT // 2)
            router_vector(v, 0, done)
            for i in range(2):
                nc.vector.memset(tq[i][:], 0.0)
                done(nc.vector.memset(tk[i][:], 0.0))
                nc.vector.memset(tk[i][:, :, 24:26], 1.0)
                done(nc.vector.memset(Vs[i][:], 0.0))
                last = nc.vector.memset(Vs[i][:, :, :, HD:HD + 1], 1.0)
            last.then_inc(sem("stacks_zeroed"), 1)

            def body(n, turn):
                cn = Count(n, turn)
                for u, w in ring_units(n):
                    bank = cn.all % RING
                    idx = cn.all + 1
                    cn.add(w)
                    if w[0] not in by_vector:
                        continue
                    wait(v, "ring_full", idx, PER_ALL, turn)
                    if w[0] == "A":
                        _, j, i, c = w
                        if i < 2:
                            src = psum[:, bank, :].rearrange("p (j k) -> p j k", j=2)[:, :, 0:P * (i + 1)]
                            dst = mall[:, j:j + 2, i]
                        else:
                            src = psum[:, bank, 0:a_columns(i, c)[1]]
                            dst = mall[:, j, i:i + 1] if i < 4 else mtwo[:, j, i - 4, c:c + 1]
                        nc.vector.reduce_max(dst, src, AX).then_inc(sem("ring_vec"), 1)
                    else:
                        output_unit(v, n - w[1], turn, w[1], bank)
                        if n == NIT - 1:
                            (weights_hi_lo if w[1] == 1 else weights_hi)()
                if n + 1 < NIT:
                    par = (n + 1) % 2
                    wait(v, "ring_vec", cn.vec, PER_VEC, turn)
                    step_a(v, nc.vector.tensor_reduce(mall[:, :, 4:TPB], mtwo[:], AX, ALU.max), n, turn, 1)
                    step_a(v, nc.vector.tensor_scalar(negm[:], mall[:], -1.0, None, ALU.mult), n, turn, 2)
                    step_a(v, nc.vector.tensor_copy(negh[:], negm[:]), n, turn, 3)
                    cols = tq[par][:].rearrange("p (t j) r -> p j t r", j=HPG)
                    nc.vector.tensor_copy(cols[:, :, :, 24], negh[:].bitcast(F32))
                    nc.vector.tensor_tensor(cols[:, :, :, 25], negm[:], negh[:].bitcast(F32),
                                            ALU.subtract).then_inc(sem("m_ready"), 1)

            def mixture0_part(t, n):
                return t[:, 4 * FF * (n % 2):4 * FF * (n % 2 + 1)]

            def weights_hi_lo():
                for n in range(2):
                    v.wait_ge(sem(f"w_in0_{n}"), 16)
                    nc.vector.tensor_copy(mixture0_part(W1h, n), wst[n][:]).then_inc(sem("w_hi0"), 1)
                for n in range(2):
                    v.wait_ge(sem("w_hi0"), n + 1)
                    nc.vector.tensor_tensor(mixture0_part(W1l, n), wst[n][:], mixture0_part(W1h, n).bitcast(F32),
                                            ALU.subtract).then_inc(sem("w_split0"), 1)

            def weights_hi():
                v.wait_ge(sem("b_full"), NB * (NIT - 1))
                for n in (2, 3):
                    v.wait_ge(sem(f"w_in0_{n}"), 16)
                    nc.vector.tensor_copy(mixture0_part(W3h, n), wst[n % 2][:]).then_inc(sem("w_hi0"), 1)

            def step_a(v, ins, n, turn, k):
                ins.then_inc(sem("max_step"), 1)
                wait(v, "max_step", 3 * (n + 1) + k, 3, turn)

            def output_unit(v, n, turn, half, bank):
                src = psum[:, bank, :].rearrange("p (t j r) -> p t j r", t=TPC, j=HPG)
                nc.vector.reciprocal(recip[:, half], src[:, :, :, HD]).then_inc(sem("recip_step"), 1)
                wait(v, "recip_step", 2 * n + half + 1, 2, turn)
                off = (2 * n + half) * CHUNK // 4
                if turn is None:
                    dst = Vn[:, n, half * TPC:(half + 1) * TPC, :]
                else:
                    flat = Vn[:].rearrange("p n t r -> p (n t r)")
                    dst = flat[:, bass.ds(turn * (TPB * HPG * HD) + off, TPC * HPG * HD)].rearrange(
                        "p (t r) -> p t r", t=TPC)
                nc.vector.tensor_tensor(dst.rearrange("p t (j d) -> p t j d", j=HPG), src[:, :, :, 0:HD],
                                        recip[:, half].unsqueeze(3).to_broadcast([P, TPC, HPG, HD]),
                                        ALU.mult).then_inc(sem("ring_vec"), 1)

            attention_iterations(v, body)
            r_all, r_vec, _ = ring_before(NIT)
            v.wait_ge(sem("ring_full"), r_all + 1)
            output_unit(v, NIT - 1, None, 1, r_all % RING)
            v.wait_ge(sem("ring_vec"), r_vec + 1)
            v.wait_ge(sem("pv_done"), NG_ * NIT)
            for c in range(NCH):
                b, i = divmod(TPC * c, TPB)
                nc.vector.tensor_copy(cx[:, TPC * c:TPC * (c + 1), :].rearrange("p t (g r) -> p t g r", g=GROUPS),
                                      Vn[:, b::BATCH, i:i + TPC, :].rearrange("p g t r -> p t g r")).then_inc(
                                          sem("cx_ready"), 1)
            v.wait_ge(sem("b_full"), NB * NIT)
            for n in (2, 3):
                v.wait_ge(sem("w_hi0"), n + 1)
                nc.vector.tensor_tensor(mixture0_part(W3l, n), wst[n % 2][:], mixture0_part(W3h, n).bitcast(F32),
                                        ALU.subtract).then_inc(sem("w_split0"), 1)
            for c in range(NCH):
                v.wait_ge(sem("proj_done"), c + 1)
                nc.vector.tensor_tensor(xres[:, TPC * c:TPC * (c + 1), :], xres[:, TPC * c:TPC * (c + 1), :],
                                        psum[:, 4 + c % 2, :].rearrange("p (t d) -> p t d", t=TPC),
                                        ALU.add).then_inc(sem("proj_added"), 1)
            mixture_vector(v, 0)
            v.wait_ge(sem("proj_added"), NCH)
            combine_vector(v, 0, done)
            norm_vector(v, 1, done)
            v.wait_ge(sem("gw_in"), 32)
            lo_vector(v, 1)
            v.wait_ge(sem("gwh_ready"), 1)
            nc.vector.tensor_tensor(gwl[:], gw_sb[:], gwh[:].bitcast(F32), ALU.subtract).then_inc(sem("gwl_ready"), 1)
            v.wait_ge(sem("rnn_hi"), 1)
            nc.vector.tensor_tensor(rwl[:], rw[:], rwh[:].bitcast(F32), ALU.subtract).then_inc(sem("rnn_lo"), 1)
            nc.vector.tensor_scalar(rnn_bh[:], rnn_bias[:, 2 * RC:3 * RC], 0.5, None, ALU.add).then_inc(
                sem("rnn_bh_ready"), 1)
            v.wait_ge(sem("logits1"), 1)
            done(nc.vector.tensor_copy(lg[:].rearrange("p i e -> p (i e)"), psum[:, 6, 0:TT * EXPERTS]))
            router_vector(v, 1, done)
            v.wait_ge(sem("v_hi"), 1)
            nc.vector.tensor_tensor(V1l[:], vraw[:], V1h[:].bitcast(F32), ALU.subtract).then_inc(sem("v_split"), 1)
            v.wait_ge(sem("rnn_bh_ready"), 1)
            for m in range(RC * NCH):
                c, k = m // RC, m % RC
                v.wait_ge(sem("sig_ready"), 3 * (m + 1))
                nc.vector.scalar_tensor_tensor(gg[:, m % 2, :], psum[:, 3 * (m % 2) + 2, :], rnn_bh[:, k:k + 1],
                                               gs[:, m % 2, :], ALU.add, ALU.max).then_inc(sem("g_ready"), 1)
                v.wait_ge(sem("g_ready"), m + 1)
                done(nc.vector.tensor_tensor(gv[:, m % 2, :], gg[:, m % 2, :], gi[:, m % 2, :], ALU.mult))
                start = c * CHUNK
                first = 0.5 if start % SEQ == 0 else hT[:, k, start - 1:start]
                if start % SEQ:
                    v.wait_ge(sem("scan_done"), m - RC + 1)
                nc.vector.tensor_tensor_scan(hT[:, k, start:start + CHUNK], gf[:, m % 2, :], gv[:, m % 2, :],
                                             first, ALU.mult, ALU.add).then_inc(sem("scan_done"), 1)
            for c in range(NCH):
                v.wait_ge(sem("rnn_out"), c + 1)
                nc.vector.tensor_tensor(xres[:, TPC * c:TPC * (c + 1), :], xres[:, TPC * c:TPC * (c + 1), :],
                                        psum[:, 6 + c % 2, :].rearrange("p (t d) -> p t d", t=TPC),
                                        ALU.add).then_inc(sem("rnn_added"), 1)
            mixture_vector(v, 1)
            v.wait_ge(sem("rnn_added"), NCH)
            combine_vector(v, 1, done)

        def hi_scalar(a, l):
            for c in range(NCH):
                a.wait_ge(sem(f"xT_done{l}"), c + 1)
                nc.scalar.copy(xh[:, c * CHUNK:(c + 1) * CHUNK], psum[:, c % 2, :]).then_inc(sem(f"xh_ready{l}"), 1)

        def norm_scalar(a, l):
            for c in range(4):
                a.wait_ge(sem(f"var_ready{l}"), c + 1)
                nc.scalar.activation(sd[:], rt[:], ACT.Sqrt).then_inc(sem(f"sd_ready{l}"), 1)

        def mixture_scalar(a, l):
            b = tb[l]

            def step(s, dyn, c):
                def w(name, count, per=1):
                    a.wait_ge(sem(name), count if dyn is None else dyn * per + count)
                if s < SLOT_TILES:
                    w(f"gT_done{l}", s + 1)
                    if s >= 2:
                        w(f"h_ready{l}", (2 if l == 0 else 1) * (s - 1), 2 if l == 0 else 1)
                    nc.scalar.copy(b.gh[:, c % 2, :], psum[:, 0, 0:P]).then_inc(sem(f"gh_ready{l}"), 1)
                if 1 <= s <= SLOT_TILES:
                    t = (c - 1) % 2
                    if l == 0:
                        w("h_ready0", 2 * s - 1, 2)
                        if s >= 3:
                            w("act_ready0", s - 2)
                        nc.scalar.activation(b.s1[:, t, :], psum[:, 1 + t, :], ACT.Silu).then_inc(
                            sem("silu_ready0"), 1)
                    else:
                        w("h_ready1", s)
                        if s >= 3:
                            w("aT_in1", s - 2)
                        nc.scalar.activation(b.act[:, t, :], psum[:, 1 + t, :], ACT.Gelu).then_inc(sem("act_ready1"), 1)
                if 2 <= s < SLOT_TILES + 2:
                    w(f"aT_in{l}", s - 1)
                    if s >= 4:
                        w(f"y_ready{l}", s - 3)
                    nc.scalar.copy(b.aT[:, c % 2, :], psum[:, 5 + c % 2, :]).then_inc(sem(f"aT_ready{l}"), 1)
                if s >= 3:
                    w(f"y_ready{l}", s - 2)
                    if s - 3 >= OUTS:
                        a.wait_ge(sem(f"row_out{l}_{(c - 3) % OUTS}"), 16 * ((s - 3) // OUTS)) if dyn is None else \
                            a.wait_ge(sem(f"row_out{l}_{(c - 3) % OUTS}"), dyn * 2 + 16 * ((s - 3) // OUTS))
                    nc.scalar.copy(b.yo[:, (c - 3) % OUTS, :], psum[:, 7, 0:D]).then_inc(sem(f"yo_ready{l}"), 1)
            mixture_steps(a, step)

        @block.scalar
        def _(a):
            a.dma_start(wraw[:], w_cat).then_inc(sem("w_in"), 16)
            a.dma_start(la[0:LORA_RANK, :], lora_a).then_inc(sem("w_in"), 16)
            a.dma_start(lb[0:LORA_RANK, :], lora_b).then_inc(sem("w_in"), 16)
            a.dma_start(wo_raw[:], wo_t).then_inc(sem("w_in"), 16)
            a.dma_start(gw_sb[:], gate_w).then_inc(sem("gw_in"), 16)
            a.dma_start(gbias[:], gate_b.partition_broadcast(P)).then_inc(sem("gw_in"), 16)
            a.dma_start(bias_c[0:EXPERTS, 0:FF], b1).then_inc(sem("bias_in"), 16)
            a.dma_start(bias_c[0:EXPERTS, FF:NB1], b2).then_inc(sem("bias_in"), 16)
            norm_scalar(a, 0)
            a.wait_ge(sem("w_ready"), 1)
            nc.scalar.copy(wh[:], wraw[:]).then_inc(sem("wh_ready"), 1)
            hi_scalar(a, 0)
            for T in range(0, TT, 2):
                a.wait_ge(sem("qkv_done"), T + 1)
                qkv_out(nc.scalar.copy, T).then_inc(sem("qkv_sca"), 1)
            a.wait_ge(sem("gate_diff0"), 1)
            nc.scalar.activation(r1[:, 4, :], r1[:, 3, :], ACT.Exp).then_inc(sem("gate_exp0"), 1)

            def heads(n, turn, a_):
                if turn is None:
                    return QK[:, a_, n, :, :]
                flat = QK[:].rearrange("p a n x d -> p (a n x d)")
                size = TPB * HPG * HD
                return flat[:, bass.ds(turn * size + (a_ * NIT + n) * size, size)].rearrange(
                    "p (x d) -> p x d", d=HD)

            def build_hi(n, turn):
                for a_, t in ((0, tq), (1, tk)):
                    nc.scalar.copy(t[n % 2][:, :, 0:HD].bitcast(F32R), heads(n, turn, a_)).then_inc(
                        sem("tok_hi"), 1)

            def stack_unit(n, turn, w, bank, idx):
                wait(a, "ring_full", idx, PER_ALL, turn)
                kind, half = w[0], w[1]
                r = slice(half * CHUNK, (half + 1) * CHUNK)
                if kind == "k":
                    m = n + 2 if half == 0 else n + 1
                    if m >= 2:
                        wait(a, "b_full", NB * (m - 2) + (32 if half == 0 else NB), NB, turn)
                    for j in range(HPG):
                        last = nc.scalar.activation(kz[m % 2][:, j, r], psum[:, bank, :], ACT.Copy,
                                                    scale=cst[:, C_HEAD + j:C_HEAD + j + 1])
                elif kind == "q":
                    last = nc.scalar.copy(qs[n % 2][:, r], psum[:, bank, :])
                else:
                    if n >= 1:
                        wait(a, "b_full", NB * n, NB, turn)
                    last = nc.scalar.copy(qm[(n + 1) % 2][:, r], psum[:, bank, :])
                last.then_inc(sem("ring_sca"), 1)

            a.wait_ge(sem("stacks_zeroed"), 1)
            build_hi(0, None)
            a.wait_ge(sem("bz_in"), 16)
            for k, (_, w) in enumerate(FRONT):
                stack_unit(-2, None, w, k % RING, k + 1)

            def body(n, turn):
                cn = Count(n, turn)
                mine = {}
                for u, w in ring_units(n):
                    if w[0] not in by_vector:
                        mine.setdefault(u, []).append((w, cn.all % RING, cn.all + 1))
                    cn.add(w)
                for u in range(NB):
                    if n >= 0:
                        g, j = divmod(u, HPG)
                        wait(a, "b_full", NB * n + u + 1, NB, turn)
                        if n > 0 or g >= 4:
                            wait(a, "pv_done", NG_ * n + g - 3, NG_, turn)
                        _, width, skip = b_columns(g)
                        bank = 4 + (NB * n + u) % SCORES
                        nc.scalar.activation(pT[:, (g % 4) * HPG + j, 0:width], psum[:, bank, skip:skip + width],
                                             ACT.Exp, scale=HD ** -0.5).then_inc(sem("exp_done"), 1)
                    if u == 3 and n >= 1:
                        take_outputs(n - 1, turn, 1)
                    if u == 20 and n >= 0:
                        take_outputs(n, turn, 0)
                    if u == 12 and n + 2 < NIT:
                        if n >= 0:
                            wait(a, "ring_full", all_upto(n - 1, ("m", 1)), PER_ALL, turn)
                        build_hi(n + 2, turn)
                    for w, bank, idx in mine.get(u, ()):
                        stack_unit(n, turn, w, bank, idx)

            def take_outputs(n, turn, half):
                wait(a, "pv_done", NG_ * n + (4 if half == 0 else NG_), NG_, turn)
                if n >= 1:
                    wait(a, "ring_full", all_upto(n - 1 + half, ("o", half)), PER_ALL, turn)
                nc.scalar.copy(oT[:, half * CHUNK:(half + 1) * CHUNK], psum[:, OUT, :]).then_inc(
                    sem("o_taken"), 1)

            attention_iterations(a, body)
            take_outputs(NIT - 1, None, 1)
            for c in range(NCH):
                a.wait_ge(sem("cT_done"), c + 1)
                if c >= 2:
                    a.wait_ge(sem("proj_done"), c - 1)
                nc.scalar.copy(cT[:, c % 2, :], psum[:, 2 + c % 2, :]).then_inc(sem("cT_ready"), 1)
            mixture_scalar(a, 0)
            norm_scalar(a, 1)
            hi_scalar(a, 1)
            a.wait_ge(sem("gw_in"), 32)
            nc.scalar.copy(gwh[:], gw_sb[:]).then_inc(sem("gwh_ready"), 1)
            a.wait_ge(sem("rnn_in"), 48)
            nc.scalar.copy(rwh[:], rw[:]).then_inc(sem("rnn_hi"), 1)
            a.wait_ge(sem("v_in"), 16)
            nc.scalar.copy(V1h[:], vraw[:]).then_inc(sem("v_hi"), 1)
            a.wait_ge(sem("gate_diff1"), 2)
            nc.scalar.activation(r1[:, 4, :], r1[:, 3, :], ACT.Exp).then_inc(sem("gate_exp1"), 1)
            nc.scalar.activation(lg[:], lg[:], ACT.Exp).then_inc(sem("gate_exp1"), 1)
            for m in range(RC * NCH):
                k = m % RC
                a.wait_ge(sem("rnn_mm"), m + 1)
                if m >= 2:
                    a.wait_ge(sem("scan_done"), m - 1)
                for g, dst in ((0, gf), (1, gi), (2, gs)):
                    nc.scalar.activation(dst[:, m % 2, :], psum[:, 3 * (m % 2) + g, :], ACT.Sigmoid,
                                         bias=rnn_bias[:, g * RC + k:g * RC + k + 1]).then_inc(sem("sig_ready"), 1)
            mixture_scalar(a, 1)

        def split_product(dst, lh, ll, rh, rl, first=True):
            nc.tensor.matmul(dst, lh, rh, start=first, stop=False)
            nc.tensor.matmul(dst, ll, rh, start=False, stop=False)
            return nc.tensor.matmul(dst, lh, rl, start=False, stop=True)

        def transposes_tensor(pe, l):
            for c in range(NCH):
                pe.wait_ge(sem(f"xn_ready{l}"), c // 2 + 1)
                if c >= 2:
                    pe.wait_ge(sem(f"xl_ready{l}"), c - 1)
                for t in range(TPC):
                    last = nc.tensor.transpose(psum[:, c % 2, t * P:(t + 1) * P], rows[:, TPC * c + t, 0:D], ident)
                last.then_inc(sem(f"xT_done{l}"), 1)

        def counts_tensor(pe, l):
            pe.wait_ge(sem(f"count_ready{l}"), 1)
            nc.tensor.matmul(psum[:, 7, 0:EXPERTS], cst[:, C_TRI:C_TRI + P], small[:, 0, :], start=True, stop=True)
            nc.tensor.matmul(psum[:, 7, EXPERTS:2 * EXPERTS], cst[:, C_ONES:C_ONES + P], small[:, 0, :],
                             start=True, stop=True).then_inc(sem(f"count_sums{l}"), 1)

        def mixture_tensor(pe, l):
            b = tb[l]
            W2x = W2s if l == 0 else V2s

            held = {}

            def expert(t, dyn):
                if dyn is None:
                    first, end = t // 8 * 8, min(t // 8 * 8 + 8, SLOT_TILES)
                    if held.get("rows") != "static":
                        held.clear()
                    held["rows"] = "static"
                    where = tile_expert[0:1, first:end]
                else:
                    first, end = LOOP_FROM - 4, LOOP_FROM + 7
                    if held.get("rows") != "loop":
                        held.clear()
                    held["rows"] = "loop"
                    where = tile_expert[0:1, bass.ds(dyn + first, end - first)]
                if t not in held:
                    _, values = nc.values_load_multi_w_load_instructions(
                        where, engines=[mybir.EngineType.PE], min_val=0, max_val=EXPERTS - 1,
                        skip_runtime_bounds_check_because="tile_expert is clamped to the experts on the chip")
                    held.update({first + k: x for k, x in enumerate(values)})
                return held[t]

            def step(s, dyn, c):
                def w(name, count, per=1):
                    pe.wait_ge(sem(name), count if dyn is None else dyn * per + count)
                if s < SLOT_TILES:
                    pe.wait_ge(sem(f"row_in{l}_{c % 8}"), 16 * (s // 8 + 1)) if dyn is None else \
                        pe.wait_ge(sem(f"row_in{l}_{c % 8}"), dyn * 2 + 16 * (s // 8 + 1))
                    if s >= 1:
                        w(f"gl_ready{l}", s)
                    nc.tensor.transpose(psum[:, 0, 0:P], b.xg[:, c % 8, 0:D], ident).then_inc(sem(f"gT_done{l}"), 1)
                if 1 <= s <= SLOT_TILES:
                    t = (c - 1) % 2
                    w(f"gl_ready{l}", s)
                    cols = bass.ds(expert(s - 1, dyn) * FF, FF)
                    if s >= 3:
                        w("silu_ready0" if l == 0 else "act_ready1", s - 2)
                    pairs = ((W1h, W1l, 1), (W3h, W3l, 3)) if l == 0 else ((V1h, V1l, 1),)
                    for h, lo, bank in pairs:
                        if bank == 3 and s >= 3:
                            w("act_ready0", s - 2)
                        if l == 1:
                            nc.tensor.matmul(psum[:, bank + t, :], ones_b[:], bz[:, cols], start=True, stop=False)
                        split_product(psum[:, bank + t, :], b.gh[:, t, :], b.gl[:, t, :], h[:, cols],
                                      lo[:, cols], first=(l == 0)).then_inc(sem(f"h_ready{l}"), 1)
                if 2 <= s < SLOT_TILES + 2:
                    t = c % 2
                    w(f"act_ready{l}", s - 1)
                    if s >= 4:
                        w(f"aT_ready{l}", s - 3)
                    for k in range(FC):
                        last = nc.tensor.transpose(psum[:, 5 + t, k * P:(k + 1) * P],
                                                   b.act[:, t, k * P:(k + 1) * P], ident)
                    last.then_inc(sem(f"aT_in{l}"), 1)
                if s >= 3:
                    t = (c - 3) % 2
                    e = expert(s - 3, dyn)
                    w(f"aT_ready{l}", s - 2)
                    if s >= 4:
                        w(f"yo_ready{l}", s - 3)
                    if l == 1:
                        nc.tensor.matmul(psum[:, 7, 0:D], ones_b[:], bz[:, bass.ds(e * D + EXPERTS * FF, D)],
                                         start=True, stop=False)
                    for k in range(FC):
                        last = nc.tensor.matmul(psum[:, 7, 0:D], b.aT[:, t, k * P:(k + 1) * P],
                                                W2x[:, bass.ds(e * (FC * D) + k * D, D)],
                                                start=(k == 0 and l == 0), stop=(k == FC - 1))
                    last.then_inc(sem(f"y_ready{l}"), 1)
            mixture_steps(pe, step)

        @block.tensor
        def _(pe):
            pe.wait_ge(sem("const_in"), 16)
            pe.wait_ge(sem("w_in"), 64)
            for k in range(4):
                last = nc.tensor.matmul(psum[:, 6, k * D:(k + 1) * D], la[0:LORA_RANK, k * D:(k + 1) * D],
                                        lb[0:LORA_RANK, k * D:(k + 1) * D], start=True, stop=True)
            last.then_inc(sem("lora_prod"), 1)
            transposes_tensor(pe, 0)
            pe.wait_ge(sem("wl_ready"), 1)
            for T in range(TT):
                if T % TPC == 0:
                    pe.wait_ge(sem("xl_ready0"), T // TPC + 1)
                if T >= 4:
                    pe.wait_ge(sem("qkv_sca" if T % 2 == 0 else "qkv_vec"), T // 2 - 1)
                t = slice(T * P, (T + 1) * P)
                split_product(psum[:, 2 + T % 4, 0:NW], xh[:, t], xl[:, t], wh[:], wl[:]).then_inc(
                    sem("qkv_done"), 1)
            counts_tensor(pe, 0)

            def ring_fill(n, turn, w, cn):
                bank = cn.all % RING
                if len(cn.hist) >= RING:
                    vec, count = cn.hist[-RING]
                    if vec:
                        wait(pe, "ring_vec", count, PER_VEC, turn)
                    else:
                        wait(pe, "ring_sca", count, PER_SCA, turn)
                cn.add(w)
                if w[0] == "A":
                    _, j, i, c = w
                    m = n + 1
                    if (j, c) == (0, 0) and i in (0, 4):
                        if i == 0:
                            count = upto(m - 2, ("q", 1)) if m - 2 >= -1 else len(FRONT)
                            wait(pe, "ring_sca", count, PER_SCA, turn)
                        else:
                            wait(pe, "ring_sca", upto(n, ("k", 1)), PER_SCA, turn)
                    k0, width = a_columns(i, c)
                    diag = i < 4 or c == 1
                    for jj in range(2 if i < 2 else 1):
                        o = 256 * jj
                        last = nc.tensor.matmul(psum[:, bank, o:o + width], qs[m % 2][:, i * P:(i + 1) * P],
                                                kz[m % 2][:, j + jj, k0:k0 + width], start=True, stop=not diag)
                        if diag:
                            d0 = o + P * i - k0
                            last = nc.tensor.matmul(psum[:, bank, d0:d0 + P], ident_b[:], mask_b[:],
                                                    start=False, stop=True)
                    return last
                half = w[1]
                if w[0] == "o":
                    wait(pe, "o_taken", 2 * n + 1 - half, 2, turn)
                    src = oT[:]
                elif w[0] == "k":
                    m = n + 2 if half == 0 else n + 1
                    wait(pe, "tok_ready", m + 1, 1, turn)
                    src = tk[m % 2][:].rearrange("p x r -> p (x r)")
                elif w[0] == "q":
                    wait(pe, "tok_ready", n + 3, 1, turn)
                    src = tq[n % 2][:].rearrange("p x r -> p (x r)")
                else:
                    wait(pe, "m_ready", n + 2, 1, turn)
                    src = tq[(n + 1) % 2][:].rearrange("p x r -> p (x r)")
                for t in range(TPC):
                    c0 = (half * TPC + t) * P
                    last = nc.tensor.transpose(psum[:, bank, t * P:(t + 1) * P], src[:, c0:c0 + P], ident)
                return last

            def pv(n, turn, g):
                h, jt = GROUPED[g]
                if g in DIAG:
                    wait(pe, "diag_done", HPG * (len(DIAG) * n + DIAG.index(g) + 1), HPG * len(DIAG), turn)
                else:
                    wait(pe, "exp_done", NB * n + HPG * (g + 1), NB, turn)
                if g == 0:
                    wait(pe, "v_ready", n + 1, 1, turn)
                if jt == 0 and (n >= 1 or h == 1):
                    wait(pe, "o_taken", 2 * n + h, 2, turn)
                q0, width, _ = b_columns(g)
                o = q0 - CHUNK * h
                for j in range(HPG):
                    last = nc.tensor.matmul(psum[32 * j:32 * j + 32, OUT, o:CHUNK], Vs[n % 2][:, jt, j, :],
                                            pT[:, (g % 4) * HPG + j, 0:width],
                                            start=(jt == 0), stop=(g in (3, NG_ - 1)))
                last.then_inc(sem("pv_done"), 1)

            def body(n, turn):
                cn = Count(n, turn)
                fills = {}
                for u, w in ring_units(n):
                    fills.setdefault(u, []).append(w)
                for u in range(NB):
                    if n >= 0:
                        g, j = divmod(u, HPG)
                        if u == 0:
                            wait(pe, "ring_sca", upto(n - 1, ("m", 1)), PER_SCA, turn)
                        if not (n == 0 and u < SCORES):
                            wait(pe, "exp_done", NB * n + u + 1 - SCORES, NB, turn)
                        jt = GROUPED[g][1]
                        q0, width, skip = b_columns(g)
                        nc.tensor.matmul(psum[:, 4 + (NB * n + u) % SCORES, 0:width + skip],
                                         kz[n % 2][:, j, jt * P:(jt + 1) * P],
                                         qm[n % 2][:, q0 - skip:q0 + width],
                                         start=True, stop=True).then_inc(sem("b_full"), 1)
                    if u == 1 and n >= 1:
                        pv(n - 1, turn, NG_ - 1)
                    if n >= 0 and u % HPG == HPG - 1 and u > HPG:
                        pv(n, turn, u // HPG - 1)
                    for w in fills.get(u, ()):
                        ring_fill_signal(n, turn, w, cn)

            def ring_fill_signal(n, turn, w, cn):
                last = ring_fill(n, turn, w, cn)
                last.then_inc(sem("ring_full"), 1)

            cf = Count(-1, None)
            cf.all, cf.vec, cf.sca, cf.hist = 0, 0, 0, []
            for _, w in FRONT:
                ring_fill_signal(-2, None, w, cf)
            attention_iterations(pe, body)
            pv(NIT - 1, None, NG_ - 1)
            ce = Count(NIT, None)
            for _, w in BACK:
                ring_fill_signal(NIT, None, w, ce)

            pe.wait_ge(sem("exp_done"), NB * NIT)
            for c in range(NCH + 1):
                if c < NCH:
                    if c >= 2:
                        pe.wait_ge(sem("cT_ready"), c - 1)
                    pe.wait_ge(sem("cx_ready"), c + 1)
                    for t in range(TPC):
                        last = nc.tensor.transpose(psum[:, 2 + c % 2, t * P:(t + 1) * P], cx[:, TPC * c + t, :],
                                                   ident)
                    last.then_inc(sem("cT_done"), 1)
                if c >= 1:
                    k = c - 1
                    pe.wait_ge(sem("cT_ready"), k + 1)
                    if k >= 2:
                        pe.wait_ge(sem("proj_added"), k - 1)
                    for t in range(TPC):
                        last = nc.tensor.matmul(psum[:, 4 + k % 2, t * P:(t + 1) * P],
                                                cT[:, k % 2, t * P:(t + 1) * P], wo_sb[:], start=True, stop=True)
                    last.then_inc(sem("proj_done"), 1)
            pe.wait_ge(sem("w_split0"), 4)
            pe.wait_ge(sem("w2_in0"), 16)
            pe.wait_ge(sem("proj_added"), NCH)
            mixture_tensor(pe, 0)

            transposes_tensor(pe, 1)
            pe.wait_ge(sem("gwl_ready"), 1)
            pe.wait_ge(sem("xl_ready1"), NCH)
            for T in range(TT):
                t = slice(T * P, (T + 1) * P)
                last = split_product(psum[:, 6, T * EXPERTS:(T + 1) * EXPERTS], xh[:, t], xl[:, t], gwh[:], gwl[:])
            last.then_inc(sem("logits1"), 1)
            counts_tensor(pe, 1)
            pe.wait_ge(sem("rnn_lo"), 1)
            for m in range(RC * NCH):
                c, k = m // RC, m % RC
                if m >= 2:
                    pe.wait_ge(sem("g_ready"), m - 1)
                    pe.wait_ge(sem("sig_ready"), 3 * (m - 1))
                xr = slice(c * CHUNK, (c + 1) * CHUNK)
                for g in range(3):
                    wr = slice(g * RNN_E + k * P, g * RNN_E + (k + 1) * P)
                    last = split_product(psum[:, 3 * (m % 2) + g, :], rwh[:, wr], rwl[:, wr], xh[:, xr], xl[:, xr])
                last.then_inc(sem("rnn_mm"), 1)
            for c in range(NCH):
                pe.wait_ge(sem("scan_done"), RC * (c + 1))
                if c >= 2:
                    pe.wait_ge(sem("rnn_added"), c - 1)
                for t in range(TPC):
                    T = TPC * c + t
                    for k in range(RC):
                        last = nc.tensor.matmul(psum[:, 6 + c % 2, t * D:(t + 1) * D], hT[:, k, T * P:(T + 1) * P],
                                                rwd[:, k, :], start=(k == 0), stop=(k == RC - 1))
                last.then_inc(sem("rnn_out"), 1)
            pe.wait_ge(sem("v_split"), 1)
            pe.wait_ge(sem("v2_in"), 16)
            pe.wait_ge(sem("bz_in"), 16)
            pe.wait_ge(sem("rnn_added"), NCH)
            mixture_tensor(pe, 1)

        def scatter_rows(g, l, first=0, end=TT):
            if first == 0:
                g.wait_ge(sem(f"slots_ready{l}"), 1)
                g.wait_ge(sem("pads_in"), 32)
            for i in range(first, end):
                for k in range(TOPK):
                    g.indirect_dma_start(xs[l], bass.IndirectOffsetOnAxis(ap=slot_i[:, k, i:i + 1], axis=0),
                                         rows[:, i, :], None).then_inc(sem(f"rows_sorted{l}"), 16)

        def mixture_gpsimd(g, l):
            b = tb[l]

            def step(s, dyn, c):
                if s < 3:
                    return
                t = (c - 3) % OUTS
                g.wait_ge(sem(f"yo_ready{l}"), s - 2 if dyn is None else dyn + (s - 2))
                g.wait_ge(sem(f"dest_ready{l}"), s - 2 if dyn is None else dyn + (s - 2))
                if dyn is not None:
                    g.sem_inc(sem("pool_waited"), 1)
                g.indirect_dma_start(yc[l], bass.IndirectOffsetOnAxis(ap=destf[:, t:t + 1], axis=0),
                                     b.yo[:, t, :], None, bounds_check=TOPK * TOKENS - 1,
                                     oob_is_err=False).then_inc(sem(f"row_out{l}_{t}"), 16)
            mixture_steps(g, step)

        @block.gpsimd
        def _(g_):
            def wait_alone(name, count, per, turn):
                wait(g_, name, count, per, turn)
                if turn is not None:
                    g_.sem_inc(sem("pool_waited"), 1)

            def heads(n, turn, a_):
                if turn is None:
                    return QK[:, a_, n, :, :]
                flat = QK[:].rearrange("p a n x d -> p (a n x d)")
                size = TPB * HPG * HD
                return flat[:, bass.ds(turn * size + (a_ * NIT + n) * size, size)].rearrange(
                    "p (x d) -> p x d", d=HD)

            def build(n, turn):
                par = n % 2
                wait_alone("tok_hi", 2 * n + 2, 2, turn)
                q, k = tq[par], tk[par]
                nc.gpsimd.tensor_tensor(q[:, :, 8:16], heads(n, turn, 0), q[:, :, 0:8], ALU.subtract)
                nc.gpsimd.tensor_copy(q[:, :, 16:24], q[:, :, 0:8])
                nc.gpsimd.memset(q[:, :, 24:26], 0.0)
                nc.gpsimd.tensor_copy(k[:, :, 8:16], k[:, :, 0:8])
                nc.gpsimd.tensor_tensor(k[:, :, 16:24], heads(n, turn, 1), k[:, :, 0:8],
                                        ALU.subtract).then_inc(sem("tok_ready"), 1)

            def values(n, turn):
                if n >= 2:
                    wait_alone("pv_done", NG_ * (n - 1), NG_, turn)
                if turn is None:
                    src = Vn[:, n, :, :]
                else:
                    size = TPB * HPG * HD
                    src = Vn[:].rearrange("p n t r -> p (n t r)")[:, bass.ds(turn * size + n * size, size)].rearrange(
                        "p (t r) -> p t r", t=TPB)
                nc.gpsimd.tensor_copy(Vs[n % 2][:, :, :, 0:HD], src.rearrange("p t (j d) -> p t j d", j=HPG)).then_inc(
                    sem("v_ready"), 1)

            def body(n, turn):
                for u in range(NB):
                    g, j = divmod(u, HPG)
                    if n >= 0 and g in DIAG:
                        wait_alone("exp_done", NB * n + u + 1, NB, turn)
                        blk = pT[:, (g % 4) * HPG + j, 0:P]
                        nc.gpsimd.affine_select(out=blk, in_=blk, compare_op=ALU.is_ge, fill=0.0, base=0,
                                                pattern=[[1, P]], channel_multiplier=-1).then_inc(
                                                    sem("diag_done"), 1)
                    if u == 5 and n + 1 < NIT:
                        values(n + 1, turn)
                    if u == 16 and n + 2 < NIT:
                        build(n + 2, turn)
                    if turn is None and u % 4 == 2 and u >= 6:
                        if sorted_[0] < TT:
                            scatter_rows(g_, 0, sorted_[0], sorted_[0] + 1)
                            sorted_[0] += 1

            nc.gpsimd.memset(bz[:], 0.0).then_inc(sem("bz_zeroed"), 1)
            g_.wait_ge(sem("bias_in"), 32)
            e8 = slice(0, EXPERTS)
            steps = [(bias_p[e8, 0, :], bias_c[e8, :], None), (bias_r[e8, 0, :], bias_c[e8, :], bias_p[e8, 0, :]),
                     (bias_p[e8, 1, :], bias_r[e8, 0, :], None),
                     (bias_r[e8, 1, :], bias_r[e8, 0, :], bias_p[e8, 1, :]),
                     (bias_p[e8, 2, :], bias_r[e8, 1, :], None)]
            for k, (dst, src, part) in enumerate(steps):
                if k:
                    g_.wait_ge(sem("bias_split"), k)
                ins = nc.gpsimd.tensor_copy(dst, src) if part is None else \
                    nc.gpsimd.tensor_tensor(dst, src, part, ALU.subtract)
                ins.then_inc(sem("bias_split"), 1)
            sorted_ = [0]
            build(0, None)
            attention_iterations(g_, body)
            scatter_rows(g_, 0, sorted_[0], TT)
            mixture_gpsimd(g_, 0)
            scatter_rows(g_, 1)
            mixture_gpsimd(g_, 1)


def kernel(**inputs):
    import concourse.bacc as bacc
    from concourse import mybir as mb
    from concourse.bass_utils import run_bass_kernel_spmd

    f = {k: np.asarray(v) for k, v in inputs.items()}

    def cat(*xs):
        return np.ascontiguousarray(np.concatenate(xs, axis=1))

    A = "L0_attn_"
    arrays = {
        "x": f[A + "x"], "consts": constants(),
        "w_cat": cat(*(f[A + "w" + n].T for n in "qkv"), f["L0_ffn_Wr"]),
        "lora_a": cat(*(f[A + "a" + n] for n in "qkvo")),
        "lora_b": cat(*(f[A + "b" + n].T for n in "qkvo")),
        "wo_t": f[A + "wo"].T,
        "W1": f["L0_ffn_W1"], "W2": f["L0_ffn_W2"], "W3": f["L0_ffn_W3"],
        "rnn_w": f["L1_attn_W"].T, "rnn_b": f["L1_attn_b"].reshape(-1, P).T, "rnn_wd": f["L1_attn_Wd"].T,
        "gate_w": f["L1_ffn_gate_w"], "gate_b": f["L1_ffn_gate_b"], "w1": f["L1_ffn_w1"], "b1": f["L1_ffn_b1"],
        "w2": f["L1_ffn_w2"], "b2": f["L1_ffn_b2"],
    }
    nc = bacc.Bacc("TRN2", target_bir_lowering=False, num_devices=1)
    feed, args = {}, []
    for name, a in arrays.items():
        a = np.ascontiguousarray(a)
        feed[f"in_{name}"] = a
        args.append(nc.dram_tensor(f"in_{name}", a.shape, mb.dt.from_np(a.dtype), kind="ExternalInput").ap())
    args.append(nc.dram_tensor("out_x", f[A + "x"].shape, mb.dt.from_np(f[A + "x"].dtype),
                               kind="ExternalOutput").ap())
    program(nc, *args)
    r = run_bass_kernel_spmd(nc, [feed], core_ids=[0])
    return r.results[0]["out_x"]
```

```python
from contextlib import ExitStack

import concourse.bass as bass
import concourse.mybir as mybir
import numpy as np

F32 = mybir.dt.float32
F32R = mybir.dt.float32r
BF16 = mybir.dt.bfloat16
I32 = mybir.dt.int32
ALU = mybir.AluOpType
ACT = mybir.ActivationFunctionType
AX = mybir.AxisListType.X

P = 128
D = 128
BATCH, SEQ = 4, 1024
TOKENS = BATCH * SEQ
TT = TOKENS // P
TPB = SEQ // P
CHUNK = 512
NCH = TOKENS // CHUNK
TPC = CHUNK // P
NT = 2 * TPC
NN = TT // NT
HEADS, HD = 16, 8
GROUPS, HPG = 4, 4
NIT = GROUPS * BATCH
EXPERTS, FF, TOPK = 8, 512, 2
FC = FF // P
SLOT_TILES = TOPK * TOKENS // P + EXPERTS - 1
ROW = D + 2
SKIP = float(1 << 20)
BIG = 3.0e38
LORA_RANK = 16
OUTS = 8
RNN_E = 256
RC = RNN_E // P
EPS = 1e-5
MASKED = -1.0e30

C_ID, C_MASK, C_TRI, C_ONES, C_RMASK = 0, 128, 256, 384, 512
C_PRIO = C_RMASK + TT * EXPERTS
C_IOTA = C_PRIO + EXPERTS
C_HEAD = C_IOTA + SLOT_TILES
C_TOK2 = C_HEAD + HPG
C_PART = C_TOK2 + TT
C_END = C_PART + SLOT_TILES


def constants():
    c = np.zeros((P, C_END), np.float32)
    c[:, C_ID:C_ID + P] = np.eye(P)
    c[:, C_MASK:C_MASK + P] = np.triu(np.full((P, P), MASKED), 1)
    c[:, C_TRI:C_TRI + P] = np.triu(np.ones((P, P)), 1)
    c[:, C_ONES:C_ONES + P] = 1.0
    c[:, C_RMASK:C_PRIO] = np.tile(np.arange(TT) > 0, EXPERTS)
    c[:, C_PRIO:C_IOTA] = EXPERTS - np.arange(EXPERTS)
    c[:, C_IOTA:C_HEAD] = np.arange(SLOT_TILES)
    c[:, C_HEAD:C_TOK2] = np.arange(P)[:, None] // 32 == np.arange(HPG)[None]
    c[:, C_TOK2:C_PART] = 2 * (np.arange(TT)[None] * P + np.arange(P)[:, None])
    c[:, C_PART:] = np.arange(SLOT_TILES)[None] * P + np.arange(P)[:, None]
    return c


def program(nc, x, consts, w_cat, lora_a, lora_b, wo_t, W1, W2, W3, rnn_w, rnn_b, rnn_wd,
            gate_w, gate_b, w1, b1, w2, b2, out):
    xs = [nc.dram_tensor(f"sorted_rows_{l}", (SLOT_TILES * P, ROW), F32).ap() for l in range(2)]
    bias_rows = nc.dram_tensor("bias_rows", (3, EXPERTS * (FF + D)), BF16).ap()
    yc = [nc.dram_tensor(f"expert_rows_{l}", (TOPK * TOKENS, D), F32).ap() for l in range(2)]

    ctx = ExitStack()
    with ctx:
        base = (nc.sbuf_base + 63) // 64 * 64
        total = 212736
        ctx.enter_context(nc.sbuf_tensor("arena", [P, total // 4], F32))
        names = [0]

        def at(name, off, shape, dt=F32):
            n = int(np.prod(shape)) * (2 if dt == BF16 else 4)
            assert off + n <= total, (name, off, n)
            names[0] += 1
            return nc.alloc_sbuf_tensor_at(name, [P] + list(shape), dt, offset=base + off)

        pos_ = [0]

        def keep(name, shape, dt=F32):
            t = at(name, pos_[0], shape, dt)
            pos_[0] += (int(np.prod(shape)) * (2 if dt == BF16 else 4) + 31) // 32 * 32
            return t

        xres = keep("xres", [TT, D])
        rows = keep("rows", [TT, ROW])
        cst = keep("cst", [C_END])
        ident_b = keep("ident_b", [P], BF16)
        mask_b = keep("mask_b", [P], BF16)
        ones_b = keep("ones_b", [P], BF16)
        gate_wt = keep("gate_wt", [TOPK, TT])
        slot_i = keep("slot_i", [TOPK, TT], I32)
        tile_expert = keep("tile_expert", [SLOT_TILES], I32)
        wo_sb = keep("wo_sb", [D])
        bn6 = keep("bn6", [NT, 6])
        mv = keep("mv", [2, NT, 2])
        rs = keep("rs", [2, NT])
        rt = keep("rt", [2, NT])
        sd = keep("sd", [2, NT])
        nm = keep("nm", [2, NT])
        small = keep("small", [12, EXPERTS])
        smalli = keep("smalli", [EXPERTS], I32)
        gbias = keep("gbias", [EXPERTS])
        gw_sb = keep("gw_sb", [EXPERTS])
        gwh = keep("gwh", [EXPERTS], F32R)
        gwl = keep("gwl", [EXPERTS], F32R)
        rnn_bias = keep("rnn_bias", [3 * RC])
        rnn_bh = keep("rnn_bh", [RC])
        destf = keep("destf", [OUTS], I32)
        negm = keep("negm", [HPG, TPB])
        negh = keep("negh", [HPG, TPB], F32R)
        mall = keep("mall", [HPG, TPB])
        mpart = keep("mpart", [HPG, TPB, TPB])
        recip = keep("recip", [2, TPC, HPG])
        Z = (pos_[0] + 63) // 64 * 64

        ident = cst[:, C_ID:C_ID + P]
        prio = cst[:, C_PRIO:C_PRIO + EXPERTS]

        kz = [at(f"kz{i}", Z + 16384 * i, [HPG, SEQ], F32R) for i in range(2)]
        QK = at("QK", Z + 32768, [2, NIT, TPB * HPG, HD])
        Vn = at("Vn", Z + 65536, [NIT, TPB, HPG * HD])
        qs = [at(f"qs{i}", Z + 81920 + 4096 * i, [SEQ], F32R) for i in range(2)]
        qm = [at(f"qm{i}", Z + 90112 + 4096 * i, [SEQ], F32R) for i in range(2)]
        tq = [at(f"tq{i}", Z + 98304 + 4096 * i, [TPB * HPG, 32]) for i in range(2)]
        tk = [at(f"tk{i}", Z + 106496 + 4096 * i, [TPB * HPG, 32]) for i in range(2)]
        Vs = [at(f"Vs{i}", Z + 114688 + 4096 * i, [TPB, HPG, 32]) for i in range(2)]
        pT = at("pT", Z + 122880, [4 * HPG, CHUNK])
        oT = at("oT", Z + 155648, [SEQ])
        xh = at("xh", Z, [TOKENS], F32R)
        xl = at("xl", Z + 16384, [TOKENS], F32R)
        NW = 3 * D + EXPERTS
        wraw = at("wraw", Z + 81920, [NW])
        wh = at("wh", Z + 81920 + 2048, [NW], F32R)
        wl = at("wl", Z + 81920 + 4096, [NW], F32R)
        wo_raw = at("wo_raw", Z + 81920 + 6144, [D])
        la = at("la", Z + 81920 + 8192, [4 * D])
        lb = at("lb", Z + 81920 + 10240, [4 * D])
        pad_rows = at("pad_rows", Z + 81920 + 12288, [ROW])

        class Routing:
            def __init__(self, l, o):
                self.lg = at(f"lg{l}", o, [TT, EXPERTS])
                self.ra = at(f"ra{l}", o + 1024, [TT, EXPERTS])
                self.rb = at(f"rb{l}", o + 2048, [TT, EXPERTS])
                self.ch0 = at(f"ch0{l}", o + 3072, [TT, EXPERTS])
                self.ch1 = at(f"ch1{l}", o + 4096, [TT, EXPERTS])
                self.cnt = at(f"cnt{l}", o + 5120, [EXPERTS, TT])
                self.run = at(f"run{l}", o + 6144, [EXPERTS, TT])
                self.tcmp = at(f"tcmp{l}", o + 7168, [SLOT_TILES, EXPERTS])
                self.r1 = at(f"r1{l}", o + 10240, [12, TT])

        rout = [Routing(0, Z + 135168), Routing(1, Z + 114688)]

        cT = at("cT", Z + 155648, [2, CHUNK])
        cx = at("cx", Z + 138240, [TT, D])
        W1h = at("W1h", Z + 32768, [EXPERTS * FF], F32R)
        W1l = at("W1l", Z + 49152, [EXPERTS * FF], F32R)
        W3h = at("W3h", Z, [EXPERTS * FF], F32R)
        W3l = at("W3l", Z + 16384, [EXPERTS * FF], F32R)
        W2s = at("W2s", Z + 81920, [EXPERTS * FC * D])
        wst = [at(f"wst{i}", Z + 98304 + 8192 * i, [4 * FF]) for i in range(2)]

        class TileBufs:
            def __init__(self, l, o):
                self.xg = at(f"xg{l}", o, [8, ROW])
                o += 8 * ROW * 4
                self.gh = at(f"gh{l}", o, [2, D], F32R)
                self.gl = at(f"gl{l}", o + 1024, [2, D], F32R)
                self.s1 = at(f"s1{l}", o + 2048, [2, FF])
                self.act = at(f"act{l}", o + 2048 + 4096, [2, FF])
                self.aT = at(f"aT{l}", o + 2048 + 8192, [2, FF])
                self.yo = at(f"yo{l}", o + 2048 + 12288, [OUTS, D])

        tb = [TileBufs(0, Z + 114688), TileBufs(1, Z)]
        yback = [at("yback0", Z + 32768, [TT, TOPK, D]), at("yback1", Z + 32768, [TT, TOPK, D])]
        hT = at("hT", Z + 32768, [RC, TOKENS])
        rw = at("rw", Z + 72704 + 8192, [3 * RNN_E])
        rwh = at("rwh", Z + 65536, [3 * RNN_E], F32R)
        rwl = at("rwl", Z + 65536 + 3072, [3 * RNN_E], F32R)
        rwd = at("rwd", Z + 65536 + 6144, [RC, D])
        gf = at("gf", Z + 72704, [2, CHUNK])
        gi = at("gi", Z + 72704 + 4096, [2, CHUNK])
        gs = at("gs", Z + 72704 + 8192, [2, CHUNK])
        gv = at("gv", Z + 72704 + 12288, [2, CHUNK])
        gg = at("gg", Z + 72704 + 16384, [2, CHUNK])
        lgT = at("lgT", Z + 72704, [4, CHUNK])
        V1h = at("V1h", Z + 93184, [EXPERTS * FF], F32R)
        V1l = at("V1l", Z + 93184 + 16384, [EXPERTS * FF], F32R)
        V2s = at("V2s", Z + 93184 + 32768, [EXPERTS * FC * D])
        vraw = at("vraw", Z + 93184 + 49152, [EXPERTS * FF])
        BZ = EXPERTS * (FF + D)
        bz = at("bz", total - 2 * BZ, [BZ], BF16)
        NB1 = FF + D
        S0 = Z + 122880
        bias_c = at("bias_c", S0, [NB1])
        bias_r = at("bias_r", S0 + 4 * NB1, [2, NB1])
        bias_p = at("bias_p", S0 + 12 * NB1, [3, NB1], BF16)

        psum = ctx.enter_context(nc.psum_tensor("psum", [P, 8, 512], F32))

        sems = {}

        def sem(name):
            if name not in sems:
                sems[name] = ctx.enter_context(nc.semaphore(name))
            return sems[name]

        chained = {}

        def chain(eng, name):
            s = sem(name)

            def done(ins):
                chained[name] = chained.get(name, 0) + 1
                ins.then_inc(s, 1)
                eng.wait_ge(s, chained[name])
            return done

        block = ctx.enter_context(nc.Block())

        RING, SCORES, OUT = 4, 3, 7
        GROUPED = [(0, jt) for jt in range(TPB // 2)] + [(1, jt) for jt in range(TPB)]
        NGROUPED = len(GROUPED)
        NB = HPG * NGROUPED
        DIAG = [g for g, (h, jt) in enumerate(GROUPED) if P * jt >= CHUNK * h]
        A_END = 37

        def b_columns(g):
            h, jt = GROUPED[g]
            q0 = max(P * jt, CHUNK * h)
            width = CHUNK * (h + 1) - q0
            return q0, width, max(256 - width, 0)

        def ring_units(n):
            nxt, nxt2 = n + 1 < NIT, n + 2 < NIT
            a = [("A", i, jt) for i in range(TPB) for jt in range(i + 1)]
            cost_b = [b_columns(u // HPG)[1] + 64 for u in range(A_END)]
            units, given = [], 0
            for u in range(NB):
                while nxt and given < len(a) and (given + 1) * sum(cost_b) <= len(a) * sum(cost_b[:u + 1]):
                    units.append((u, a[given]))
                    given += 1
                if u == 6 and nxt:
                    units.append((u, ("k", 1)))
                if u == 7 and n >= 1:
                    units.append((u, ("o", 1)))
                if u == 27 and n >= 0:
                    units.append((u, ("o", 0)))
                if u == 34 and nxt2:
                    units.append((u, ("k", 0)))
                if u in (36, 38) and nxt2:
                    units.append((u, ("q", (u - 36) // 2)))
                if u in (41, 44) and nxt:
                    units.append((u, ("m", int(u == 44))))
            return units

        by_vector = ("A", "o")
        FRONT = [(0, ("k", 0)), (0, ("q", 0)), (0, ("q", 1))]
        BACK = [(0, ("o", 1))]

        def ring_before(n):
            units = list(FRONT)
            for k in range(-1, n):
                units += ring_units(k)
            v = sum(1 for _, w in units if w[0] in by_vector)
            return len(units), v, len(units) - v

        class Count:
            def __init__(self, n, turn):
                self.all, self.vec, self.sca = ring_before(n)
                self.hist = []
                v = c = 0
                for _, w in FRONT + [w for k in range(-1, n) for w in ring_units(k)]:
                    if w[0] in by_vector:
                        v += 1
                    else:
                        c += 1
                    self.hist.append((w[0] in by_vector, v if w[0] in by_vector else c))

            def add(self, w):
                if w[0] in by_vector:
                    self.vec += 1
                    self.hist.append((True, self.vec))
                else:
                    self.sca += 1
                    self.hist.append((False, self.sca))
                self.all += 1

        STEADY = ring_units(2)
        PER_ALL = len(STEADY)
        PER_VEC = sum(1 for _, w in STEADY if w[0] in by_vector)
        PER_SCA = PER_ALL - PER_VEC
        assert 2 * PER_ALL % RING == 0 and NB % SCORES == 0 and NGROUPED % 4 == 0
        assert len(ring_units(1)) == PER_ALL and len(ring_units(NIT - 3)) == PER_ALL

        def upto(n, name):
            s = ring_before(n)[2]
            for _, w in ring_units(n):
                if w[0] not in by_vector:
                    s += 1
                    if w == name:
                        return s
            raise ValueError(name)

        def all_upto(n, name):
            a = ring_before(n)[0]
            for _, w in ring_units(n):
                a += 1
                if w == name:
                    return a
            raise ValueError(name)

        def attention_iterations(eng, body):
            for n in (-1, 0, 1):
                body(n, None)
            with eng.Fori(0, NIT - 5, 2) as turn:
                body(2, turn)
                body(3, turn)
            for n in (NIT - 2, NIT - 1):
                body(n, None)

        def wait(eng, name, count, per, turn):
            if turn is None:
                if count > 0:
                    eng.wait_ge(sem(name), count)
            else:
                assert count > 0
                eng.wait_ge(sem(name), turn * per + count)

        def slot_uses(l, c):
            return 16 * l * len(range(c, SLOT_TILES, OUTS))

        def mixture_loads(sp, l):
            sp.wait_ge(sem(f"rows_sorted{l}"), 16 * TOPK * TT)
            if l == 1:
                sp.wait_ge(sem("rnn_mm"), RC * NCH)
            for s in range(8):
                sp.dma_start(tb[l].xg[:, s, :], xs[l][s * P:(s + 1) * P, :]).then_inc(sem(f"row_in_{s}"), 16)
            steady = (SLOT_TILES - 8) // 8 * 8
            with sp.Fori(0, steady - 7, 8) as s0:
                for c in range(8):
                    sp.wait_ge(sem(f"dest_ready{l}"), s0 + (c + 1))
                    sp.dma_start(tb[l].xg[:, c, :], xs[l][bass.ds((s0 + (8 + c)) * P, P), :]).then_inc(
                        sem(f"row_in_{c}"), 16)
            for s in range(steady + 8, SLOT_TILES):
                sp.wait_ge(sem(f"dest_ready{l}"), s - 7)
                sp.dma_start(tb[l].xg[:, s % 8, :], xs[l][s * P:(s + 1) * P, :]).then_inc(
                    sem(f"row_in_{s % 8}"), 16)

        def rows_back(sp, l):
            for c in range(OUTS):
                sp.wait_ge(sem(f"row_out_{c}"), slot_uses(l + 1, c))
            v = yc[l].rearrange("(i p k) d -> p i k d", p=P, k=TOPK)
            for c in range(NCH):
                sp.dma_start(yback[l][:, TPC * c:TPC * (c + 1)], v[:, TPC * c:TPC * (c + 1)]).then_inc(
                    sem(f"back_{c}"), 16)

        @block.sync
        def _(sp):
            xv = x.rearrange("b (i p) d -> p (b i) d", p=P)
            for c in range(NN):
                sp.dma_start(xres[:, NT * c:NT * (c + 1)], xv[:, NT * c:NT * (c + 1)]).then_inc(sem(f"x_in{c}"), 16)
                if c == 0:
                    sp.dma_start(cst[:], consts).then_inc(sem("const_in"), 16)
            sp.wait_ge(sem("pad_ready"), 2)
            sp.wait_ge(sem("w_in"), 64)
            sp.wait_ge(sem(f"x_in{NN - 1}"), 16)
            for l in range(2):
                sp.dma_start(xs[l].rearrange("(s p) r -> p s r", p=P),
                             pad_rows[:].unsqueeze(1).to_broadcast([P, SLOT_TILES, ROW])).then_inc(
                                 sem("pads_in"), 16)
            sp.wait_ge(sem("bias_split"), 5)
            sp.wait_ge(sem("bz_zeroed"), 1)
            for first, width in ((0, FF), (FF, D)):
                sp.dma_start(bias_rows[:, EXPERTS * first:EXPERTS * (first + width)].rearrange(
                    "k (e f) -> e k f", e=EXPERTS), bias_p[0:EXPERTS, :, first:first + width]).then_inc(
                        sem("bias_rows_out"), 16)
            sp.wait_ge(sem("bias_rows_out"), 32)
            sp.dma_start(bz[0:3, :], bias_rows).then_inc(sem("bz_in"), 16)
            sp.wait_ge(sem("ring_full"), all_upto(NIT - 2, ("m", 1)))
            for n in range(4):
                src = (W1, W3)[n // 2].rearrange("e d f -> d e f")[:, 4 * (n % 2):4 * (n % 2) + 4, :]
                if n >= 2:
                    sp.wait_ge(sem("w_split0"), n - 1)
                sp.dma_start(wst[n % 2][:].rearrange("p (e f) -> p e f", e=4), src).then_inc(sem(f"w_in0_{n}"), 16)
            sp.wait_ge(sem("b_full"), NB * NIT)
            sp.dma_start(W2s[:].rearrange("p (e c d) -> p e c d", e=EXPERTS, c=FC),
                         W2.rearrange("e (c p) d -> p e c d", p=P)).then_inc(sem("w2_in0"), 16)
            sp.wait_ge(sem("pv_done"), NGROUPED * NIT)
            mixture_loads(sp, 0)
            rows_back(sp, 0)
            sp.wait_ge(sem("y_ready0"), SLOT_TILES)
            sp.dma_start(rw[:], rnn_w).then_inc(sem("rnn_in"), 16)
            sp.dma_start(rwd[:], rnn_wd.rearrange("(c p) d -> p c d", p=P)).then_inc(sem("rnn_in"), 16)
            sp.dma_start(rnn_bias[:], rnn_b).then_inc(sem("rnn_in"), 16)
            sp.dma_start(vraw[:].rearrange("p (e f) -> p e f", e=EXPERTS),
                         w1.rearrange("e d f -> d e f")).then_inc(sem("v_in"), 16)
            sp.dma_start(V2s[:].rearrange("p (e c d) -> p e c d", e=EXPERTS, c=FC),
                         w2.rearrange("e (c p) d -> p e c d", p=P)).then_inc(sem("v2_in"), 16)
            mixture_loads(sp, 1)
            rows_back(sp, 1)
            ov = out.rearrange("b (i p) d -> p (b i) d", p=P)
            for c in range(NCH):
                sp.wait_ge(sem("combined1"), c + 1)
                sp.dma_start(ov[:, TPC * c:TPC * (c + 1)], xres[:, TPC * c:TPC * (c + 1)]).then_inc(
                    sem("out_done"), 16)
            sp.wait_ge(sem("out_done"), 16 * NCH)

        def qkv_out(copy, T):
            b, t = divmod(T, TPB)
            src = psum[:, 2 + T % 4, 0:NW]
            copy(QK[:, :, b::BATCH, t * HPG:(t + 1) * HPG, :].rearrange("p a g j d -> p a g (j d)"),
                 src[:, 0:2 * D].rearrange("p (a g r) -> p a g r", a=2, g=GROUPS))
            copy(Vn[:, b::BATCH, t, :], src[:, 2 * D:3 * D].rearrange("p (g r) -> p g r", g=GROUPS))
            return copy(rout[0].lg[:, T, :], src[:, 3 * D:NW])

        def moments(v, l, c, done):
            for i in range(NT):
                last = nc.vector.bn_stats(bn6[:, i, :], xres[:, NT * c + i, :])
            done(last)
            for i in range(NT):
                last = nc.vector.bn_aggr(mv[:, c % 2, i, :], bn6[:, i, :])
            done(last)
            nc.vector.tensor_scalar(rt[:, c % 2], mv[:, c % 2, :, 1], EPS, None, ALU.add).then_inc(
                sem(f"var_ready{l}"), 1)

        def norm_vector(v, l, c, done):
            v.wait_ge(sem(f"sd_ready{l}"), c + 1)
            if c >= 2:
                v.wait_ge(sem(f"xn_sca{l}"), c - 1)
            rs_, sd_, nm_ = rs[:, c % 2], sd[:, c % 2], nm[:, c % 2]
            done(nc.vector.reciprocal(rs_, sd_))
            done(nc.vector.tensor_tensor(sd_, rs_, rs_, ALU.mult))
            done(nc.vector.tensor_tensor(sd_, sd_, rt[:, c % 2], ALU.mult))
            done(nc.vector.tensor_scalar(sd_, sd_, -0.5, 1.5, ALU.mult, ALU.add))
            done(nc.vector.tensor_tensor(rs_, rs_, sd_, ALU.mult))
            nc.vector.scalar_tensor_tensor(nm_, mv[:, c % 2, :, 0], -1.0, rs_, ALU.mult, ALU.mult).then_inc(
                sem(f"rs_ready{l}"), 1)
            for i in range(TPC):
                last = nc.vector.tensor_scalar(rows[:, NT * c + i, 0:D], xres[:, NT * c + i, :],
                                               mv[:, c % 2, i, 0:1], rs[:, c % 2, i:i + 1], ALU.subtract, ALU.mult)
            last.then_inc(sem(f"xn_vec{l}"), 1)

        def lo_vector(v, l, c):
            v.wait_ge(sem(f"xh_ready{l}"), c + 1)
            nc.vector.tensor_tensor(xl[:, c * CHUNK:(c + 1) * CHUNK], psum[:, c % 2, :],
                                    xh[:, c * CHUNK:(c + 1) * CHUNK].bitcast(F32),
                                    ALU.subtract).then_inc(sem(f"xl_ready{l}"), 1)

        def logits_at(first, end):
            half = first // (TT // 2)
            o = 2 * EXPERTS + (first - half * TT // 2) * EXPERTS
            return psum[:, 6 + half, o:o + (end - first) * EXPERTS]

        def choices_vector(v, l, first, end, done):
            n = end - first
            def bc(t):
                return t.unsqueeze(2).to_broadcast([P, n, EXPERTS])
            k, i = rout[l], slice(first, end)
            lg, ra, rb, ch0, ch1 = k.lg[:, i], k.ra[:, i], k.rb[:, i], k.ch0[:, i], k.ch1[:, i]
            top0, top1, w, q0 = (k.r1[:, x, i] for x in range(4))
            prio_b = prio.unsqueeze(1).to_broadcast([P, n, EXPERTS])
            if l == 1:
                done(nc.vector.tensor_tensor(
                    lg, logits_at(first, end).rearrange("p (i e) -> p i e", e=EXPERTS),
                    gbias[:].unsqueeze(1).to_broadcast([P, n, EXPERTS]), ALU.add))
            done(nc.vector.tensor_reduce(top0, lg, AX, ALU.max))
            done(nc.vector.tensor_tensor(ra, lg, bc(top0), ALU.is_equal))
            done(nc.vector.tensor_tensor(rb, ra, prio_b, ALU.mult))
            done(nc.vector.tensor_reduce(w, rb, AX, ALU.max))
            done(nc.vector.tensor_tensor(ch0, prio_b, bc(w), ALU.is_equal))
            done(nc.vector.scalar_tensor_tensor(ra, ch0, -BIG, lg, ALU.mult, ALU.add))
            done(nc.vector.tensor_reduce(top1, ra, AX, ALU.max))
            done(nc.vector.tensor_tensor(rb, ra, bc(top1), ALU.is_equal))
            done(nc.vector.tensor_tensor(ra, rb, prio_b, ALU.mult))
            done(nc.vector.tensor_reduce(w, ra, AX, ALU.max))
            done(nc.vector.tensor_tensor(ch1, prio_b, bc(w), ALU.is_equal))
            nc.vector.tensor_tensor(q0, top1, top0, ALU.subtract).then_inc(sem(f"gate_diff{l}"), 1)
            if l == 1:
                nc.vector.tensor_tensor(lg, lg, bc(top0), ALU.subtract).then_inc(sem(f"gate_diff{l}"), 1)

        def router_vector(v, l, done):
            k = rout[l]
            lg, ra, ch0, ch1, cnt, run, tcmp, r1 = k.lg, k.ra, k.ch0, k.ch1, k.cnt, k.run, k.tcmp, k.r1
            w, q0, q1, z = (r1[:, i, :] for i in range(2, 6))
            done(nc.vector.tensor_tensor(cnt[:].rearrange("p e i -> p i e"), ch0[:], ch1[:], ALU.add))
            done(nc.vector.tensor_tensor_scan(run[:].rearrange("p e i -> p (e i)"),
                                              cst[:, C_RMASK:C_PRIO], cnt[:].rearrange("p e i -> p (e i)"),
                                              0.0, ALU.mult, ALU.add))
            nc.vector.tensor_copy(small[:, 0, :], run[:, :, TT - 1]).then_inc(sem(f"count_ready{l}"), 1)
            v.wait_ge(sem(f"count_sums{l}"), 1)
            done(nc.vector.tensor_copy(small[:, 1, :], psum[:, 7, 0:EXPERTS]))
            done(nc.vector.tensor_scalar(smalli[:], psum[:, 7, EXPERTS:2 * EXPERTS], float(P - 1), None, ALU.add))
            done(nc.vector.tensor_scalar(smalli[:], smalli[:], 7, None, ALU.logical_shift_right))
            done(nc.vector.tensor_copy(small[:, 2, :], smalli[:]))
            done(nc.vector.tensor_tensor_scan(small[:, 3, :], cst[:, C_ONES:C_ONES + EXPERTS], small[:, 2, :],
                                              0.0, ALU.mult, ALU.add))
            done(nc.vector.tensor_tensor(small[:, 4, :], small[:, 3, :], small[:, 2, :], ALU.subtract))
            done(nc.vector.tensor_scalar(small[:, 4, :], small[:, 4, :], float(P), -1.0, ALU.mult, ALU.add))
            done(nc.vector.tensor_tensor(small[:, 4, :], small[:, 4, :], small[:, 1, :], ALU.add))
            done(nc.vector.tensor_tensor(run[:], run[:], small[:, 4, :].unsqueeze(2).to_broadcast([P, EXPERTS, TT]),
                                         ALU.add))
            run_v = run[:].rearrange("p e i -> p i e")
            for k, ch in enumerate((ch0, ch1)):
                done(nc.vector.tensor_tensor(ra[:], run_v, ch[:], ALU.mult))
                done(nc.vector.tensor_reduce(r1[:, 6 + k, :], ra[:], AX, ALU.add))
            done(nc.vector.tensor_copy(slot_i[:], r1[:, 6:8, :]))
            if l == 0:
                done(nc.vector.tensor_copy(rows[:, :, D], cst[:, C_TOK2:C_PART]))
            nc.vector.tensor_copy(rows[:, :, D + 1], r1[:, 6, :]).then_inc(sem(f"slots_ready{l}"), 1)
            iota = cst[:, C_IOTA:C_HEAD].unsqueeze(2).to_broadcast([P, SLOT_TILES, EXPERTS])
            ends = small[:, 3, :].unsqueeze(1).to_broadcast([P, SLOT_TILES, EXPERTS])
            done(nc.vector.tensor_tensor(tcmp[:], iota, ends, ALU.is_ge))
            ended = cnt[:].rearrange("p e i -> p (e i)")[:, 0:SLOT_TILES]
            done(nc.vector.tensor_reduce(ended, tcmp[:], AX, ALU.add))
            done(nc.vector.tensor_scalar(tile_expert[:], ended, float(EXPERTS - 1), None, ALU.min))
            if l == 0:
                v.wait_ge(sem("gate_exp0"), 1)
                done(nc.vector.tensor_scalar(z, q1, 1.0, None, ALU.add))
                done(nc.vector.reciprocal(gate_wt[:, 0, :], z))
                done(nc.vector.tensor_tensor(gate_wt[:, 1, :], q1, gate_wt[:, 0, :], ALU.mult))
            else:
                v.wait_ge(sem("gate_exp1"), 2)
                done(nc.vector.tensor_reduce(z, lg[:], AX, ALU.add))
                done(nc.vector.reciprocal(q0, z))
                done(nc.vector.tensor_tensor(q1, q1, q0, ALU.mult))
                done(nc.vector.tensor_tensor(z, q0, q1, ALU.add))
                done(nc.vector.tensor_scalar(z, z, 1e-9, None, ALU.add))
                done(nc.vector.reciprocal(w, z))
                done(nc.vector.tensor_tensor(gate_wt[:, 0, :], q0, w, ALU.mult))
                done(nc.vector.tensor_tensor(gate_wt[:, 1, :], q1, w, ALU.mult))

        LOOP_FROM = 16
        LOOP_TURNS = (SLOT_TILES - LOOP_FROM) // 8

        def mixture_steps(eng, step):
            for s in range(LOOP_FROM):
                step(s, None, s % 8)
            with eng.Fori(0, 8 * LOOP_TURNS - 7, 8) as dyn:
                for c in range(8):
                    step(LOOP_FROM + c, dyn, c)
            for s in range(LOOP_FROM + 8 * LOOP_TURNS, SLOT_TILES + 3):
                step(s, None, s % 8)

        def mixture_vector(v, l):
            b = tb[l]

            def step(s, dyn, c):
                def w(name, count, per=1):
                    v.wait_ge(sem(name), count if dyn is None else dyn * per + count)
                if s < SLOT_TILES:
                    w(f"gh_ready{l}", s + 1)
                    nc.vector.tensor_tensor(b.gl[:, c % 2, :], psum[:, 0, 0:P], b.gh[:, c % 2, :].bitcast(F32),
                                            ALU.subtract).then_inc(sem(f"gl_ready{l}"), 1)
                if l == 0 and 1 <= s <= SLOT_TILES:
                    t = (c - 1) % 2
                    w("silu_ready0", s)
                    w("h_ready0", 2 * s, 2)
                    if s >= 3:
                        w("aT_in0", s - 2)
                    nc.vector.tensor_tensor(b.act[:, t, :], b.s1[:, t, :], psum[:, 3 + t, :],
                                            ALU.mult).then_inc(sem("act_ready0"), 1)
                if s < SLOT_TILES:
                    if s >= OUTS:
                        count = 16 * (s // OUTS) + slot_uses(l, c)
                        v.wait_ge(sem(f"row_out_{c}"), count if dyn is None else dyn * 2 + count)
                    slot_id = cst[:, C_PART + s:C_PART + s + 1] if dyn is None else \
                        cst[:, bass.ds(dyn + (C_PART + s), 1)]
                    nc.vector.tensor_scalar(destf[:, c:c + 1], slot_id, b.xg[:, c % 8, D + 1:D + 2],
                                            b.xg[:, c % 8, D:D + 1], ALU.not_equal, ALU.add).then_inc(
                                                sem(f"dest_ready{l}"), 1)
            mixture_steps(v, step)

        def first_choice_vector(v, l, c):
            v.wait_ge(sem(f"back_{c}"), 16 * (l + 1))
            for i in range(TPC * c, TPC * (c + 1)):
                last = nc.vector.scalar_tensor_tensor(xres[:, i, :], yback[l][:, i, 0, :],
                                                      gate_wt[:, 0, i:i + 1], xres[:, i, :], ALU.mult, ALU.add)
            last.then_inc(sem(f"first_added{l}"), 1)

        @block.vector
        def _(v):
            done = chain(v, "vector_step")
            nc.vector.memset(pad_rows[:, 0:D], 0.0).then_inc(sem("pad_ready"), 1)
            v.wait_ge(sem("pad_ready"), 1)
            nc.vector.memset(pad_rows[:, D:ROW], SKIP).then_inc(sem("pad_ready"), 1)

            def leave(first, end):
                for T in range(first * TPC + 1, end * TPC, 2):
                    v.wait_ge(sem("qkv_done"), T + 1)
                    qkv_out(nc.vector.tensor_copy, T).then_inc(sem("qkv_vec"), 1)

            for c in range(2):
                v.wait_ge(sem(f"x_in{c}"), 16)
                moments(v, 0, c, done)
            v.wait_ge(sem("lora_prod"), 1)
            done(nc.vector.scalar_tensor_tensor(wraw[:, 0:3 * D], psum[:, 6, 0:3 * D], 1.0 / LORA_RANK,
                                                wraw[:, 0:3 * D], ALU.mult, ALU.add))
            nc.vector.scalar_tensor_tensor(wo_sb[:], psum[:, 6, 3 * D:4 * D], 1.0 / LORA_RANK,
                                           wo_raw[:], ALU.mult, ALU.add).then_inc(sem("w_ready"), 1)
            norm_vector(v, 0, 0, done)
            v.wait_ge(sem("x_in2"), 16)
            moments(v, 0, 2, done)
            norm_vector(v, 0, 1, done)
            v.wait_ge(sem("wh_ready"), 1)
            nc.vector.tensor_tensor(wl[:], wraw[:], wh[:].bitcast(F32), ALU.subtract).then_inc(sem("wl_ready"), 1)
            lo_vector(v, 0, 0)
            lo_vector(v, 0, 1)
            v.wait_ge(sem("x_in3"), 16)
            moments(v, 0, 3, done)
            norm_vector(v, 0, 2, done)
            lo_vector(v, 0, 2)
            lo_vector(v, 0, 3)
            leave(0, 2)
            norm_vector(v, 0, 3, done)
            lo_vector(v, 0, 4)
            lo_vector(v, 0, 5)
            leave(2, 4)
            lo_vector(v, 0, 6)
            lo_vector(v, 0, 7)
            leave(4, NCH)
            nc.vector.tensor_copy(ident_b[:], ident)
            nc.vector.tensor_copy(ones_b[:], cst[:, C_ONES:C_ONES + P])
            nc.vector.tensor_copy(mask_b[:], cst[:, C_MASK:C_MASK + P]).then_inc(sem("bf_consts"), 1)
            v.wait_ge(sem("qkv_sca"), TT // 2)
            v.wait_ge(sem("qkv_vec"), TT // 2)
            choices_vector(v, 0, 0, TT, done)
            router_vector(v, 0, done)
            v.wait_ge(sem("maxima_empty"), 1)

            def body(n, turn):
                cn = Count(n, turn)
                for u, w in ring_units(n):
                    bank = cn.all % RING
                    idx = cn.all + 1
                    cn.add(w)
                    if w[0] not in by_vector:
                        continue
                    wait(v, "ring_full", idx, PER_ALL, turn)
                    if w[0] == "A":
                        _, i, jt = w
                        nc.vector.reduce_max(mpart[:, :, i, jt], psum[:, bank, :].rearrange("p (j k) -> p j k", j=HPG),
                                             AX).then_inc(sem("ring_vec"), 1)
                    else:
                        output_unit(v, n - w[1], turn, w[1], bank)
                        if n == NIT - 1:
                            (weights_hi_lo if w[1] == 1 else weights_hi)()
                if n + 1 < NIT:
                    par = (n + 1) % 2
                    wait(v, "ring_vec", cn.vec, PER_VEC, turn)
                    step_a(v, nc.vector.tensor_reduce(mall[:], mpart[:], AX, ALU.max), n, turn, 1)
                    step_a(v, nc.vector.tensor_scalar(negm[:], mall[:], -1.0, None, ALU.mult), n, turn, 2)
                    step_a(v, nc.vector.tensor_copy(negh[:], negm[:]), n, turn, 3)
                    cols = tq[par][:].rearrange("p (t j) r -> p j t r", j=HPG)
                    nc.vector.tensor_copy(cols[:, :, :, 24], negh[:].bitcast(F32))
                    nc.vector.tensor_tensor(cols[:, :, :, 25], negm[:], negh[:].bitcast(F32),
                                            ALU.subtract).then_inc(sem("m_ready"), 1)

            def mixture0_part(t, n):
                return t[:, 4 * FF * (n % 2):4 * FF * (n % 2 + 1)]

            def weights_hi_lo():
                for n in range(2):
                    v.wait_ge(sem(f"w_in0_{n}"), 16)
                    nc.vector.tensor_copy(mixture0_part(W1h, n), wst[n][:]).then_inc(sem("w_hi0"), 1)
                for n in range(2):
                    v.wait_ge(sem("w_hi0"), n + 1)
                    nc.vector.tensor_tensor(mixture0_part(W1l, n), wst[n][:], mixture0_part(W1h, n).bitcast(F32),
                                            ALU.subtract).then_inc(sem("w_split0"), 1)

            def weights_hi():
                v.wait_ge(sem("b_full"), NB * (NIT - 1))
                for n in (2, 3):
                    v.wait_ge(sem(f"w_in0_{n}"), 16)
                    nc.vector.tensor_copy(mixture0_part(W3h, n), wst[n % 2][:]).then_inc(sem("w_hi0"), 1)

            def step_a(v, ins, n, turn, k):
                ins.then_inc(sem("max_step"), 1)
                wait(v, "max_step", 3 * (n + 1) + k, 3, turn)

            def output_unit(v, n, turn, half, bank):
                src = psum[:, bank, :].rearrange("p (t j r) -> p t j r", t=TPC, j=HPG)
                nc.vector.reciprocal(recip[:, half], src[:, :, :, HD]).then_inc(sem("recip_step"), 1)
                wait(v, "recip_step", 2 * n + half + 1, 2, turn)
                off = (2 * n + half) * CHUNK // 4
                if turn is None:
                    dst = Vn[:, n, half * TPC:(half + 1) * TPC, :]
                else:
                    flat = Vn[:].rearrange("p n t r -> p (n t r)")
                    dst = flat[:, bass.ds(turn * (TPB * HPG * HD) + off, TPC * HPG * HD)].rearrange(
                        "p (t r) -> p t r", t=TPC)
                nc.vector.tensor_tensor(dst.rearrange("p t (j d) -> p t j d", j=HPG), src[:, :, :, 0:HD],
                                        recip[:, half].unsqueeze(3).to_broadcast([P, TPC, HPG, HD]),
                                        ALU.mult).then_inc(sem("ring_vec"), 1)

            attention_iterations(v, body)
            r_all, r_vec, _ = ring_before(NIT)
            v.wait_ge(sem("ring_full"), r_all + 1)
            output_unit(v, NIT - 1, None, 1, r_all % RING)
            v.wait_ge(sem("ring_vec"), r_vec + 1)
            v.wait_ge(sem("pv_done"), NGROUPED * NIT)
            for c in range(NCH):
                b, i = divmod(TPC * c, TPB)
                nc.vector.tensor_copy(cx[:, TPC * c:TPC * (c + 1), :].rearrange("p t (g r) -> p t g r", g=GROUPS),
                                      Vn[:, b::BATCH, i:i + TPC, :].rearrange("p g t r -> p t g r")).then_inc(
                                          sem("cx_ready"), 1)
            v.wait_ge(sem("b_full"), NB * NIT)
            for c in range(NCH):
                v.wait_ge(sem("proj_done"), c + 1)
                nc.vector.tensor_tensor(xres[:, TPC * c:TPC * (c + 1), :], xres[:, TPC * c:TPC * (c + 1), :],
                                        psum[:, 4 + c % 2, :].rearrange("p (t d) -> p t d", t=TPC),
                                        ALU.add).then_inc(sem("proj_added"), 1)
                if c % 2 == 0:
                    n, half = 2 + c // 4, slice(c // 2 % 2 * 2 * FF, (c // 2 % 2 + 1) * 2 * FF)
                    v.wait_ge(sem("w_hi0"), n + 1)
                    nc.vector.tensor_tensor(mixture0_part(W3l, n)[:, half], wst[n % 2][:, half],
                                            mixture0_part(W3h, n)[:, half].bitcast(F32),
                                            ALU.subtract).then_inc(sem("w_split0"), 1)
            mixture_vector(v, 0)
            v.wait_ge(sem("proj_added"), NCH)
            def first_choices(c):
                first_choice_vector(v, 0, 2 * c)
                first_choice_vector(v, 0, 2 * c + 1)

            def combined_moments(c):
                v.wait_ge(sem("combined0"), 2 * c + 2)
                moments(v, 1, c, done)

            first_choices(0)
            first_choices(1)
            combined_moments(0)
            v.wait_ge(sem("gwh_ready"), 1)
            nc.vector.tensor_tensor(gwl[:], gw_sb[:], gwh[:].bitcast(F32), ALU.subtract).then_inc(sem("gwl_ready"), 1)
            first_choices(2)
            norm_vector(v, 1, 0, done)
            combined_moments(1)
            first_choices(3)
            norm_vector(v, 1, 1, done)
            combined_moments(2)
            lo_vector(v, 1, 0)
            lo_vector(v, 1, 1)
            norm_vector(v, 1, 2, done)
            combined_moments(3)
            lo_vector(v, 1, 2)
            lo_vector(v, 1, 3)
            norm_vector(v, 1, 3, done)
            for c in range(4, NCH):
                lo_vector(v, 1, c)
            v.wait_ge(sem("logits1"), NCH // 2)
            choices_vector(v, 1, 0, TT // 2, done)
            v.wait_ge(sem("rnn_hi"), 1)
            nc.vector.tensor_tensor(rwl[:], rw[:], rwh[:].bitcast(F32), ALU.subtract).then_inc(sem("rnn_lo"), 1)
            nc.vector.tensor_scalar(rnn_bh[:], rnn_bias[:, 2 * RC:3 * RC], 0.5, None, ALU.add).then_inc(
                sem("rnn_bh_ready"), 1)
            v.wait_ge(sem("logits1"), NCH)
            choices_vector(v, 1, TT // 2, TT, done)
            router_vector(v, 1, done)
            v.wait_ge(sem("rnn_bh_ready"), 1)
            for m in range(RC * NCH):
                c, k = m // RC, m % RC
                v.wait_ge(sem("sig_ready"), 3 * (m + 1))
                nc.vector.scalar_tensor_tensor(gg[:, m % 2, :], psum[:, 3 * (m % 2) + 2, :], rnn_bh[:, k:k + 1],
                                               gs[:, m % 2, :], ALU.add, ALU.max).then_inc(sem("g_ready"), 1)
                v.wait_ge(sem("g_ready"), m + 1)
                done(nc.vector.tensor_tensor(gv[:, m % 2, :], gg[:, m % 2, :], gi[:, m % 2, :], ALU.mult))
                start = c * CHUNK
                first = 0.5 if start % SEQ == 0 else hT[:, k, start - 1:start]
                if start % SEQ:
                    v.wait_ge(sem("scan_done"), m - RC + 1)
                nc.vector.tensor_tensor_scan(hT[:, k, start:start + CHUNK], gf[:, m % 2, :], gv[:, m % 2, :],
                                             first, ALU.mult, ALU.add).then_inc(sem("scan_done"), 1)
            v.wait_ge(sem("v_hi"), 1)
            nc.vector.tensor_tensor(V1l[:], vraw[:], V1h[:].bitcast(F32), ALU.subtract).then_inc(sem("v_split"), 1)
            for c in range(NCH):
                v.wait_ge(sem("rnn_out"), c + 1)
                nc.vector.tensor_tensor(xres[:, TPC * c:TPC * (c + 1), :], xres[:, TPC * c:TPC * (c + 1), :],
                                        psum[:, 6 + c % 2, :].rearrange("p (t d) -> p t d", t=TPC),
                                        ALU.add).then_inc(sem("rnn_added"), 1)
            mixture_vector(v, 1)
            v.wait_ge(sem("rnn_added"), NCH)
            for c in range(NCH):
                first_choice_vector(v, 1, c)

        def root_scalar(a, l, c):
            a.wait_ge(sem(f"var_ready{l}"), c + 1)
            nc.scalar.activation(sd[:, c % 2], rt[:, c % 2], ACT.Sqrt).then_inc(sem(f"sd_ready{l}"), 1)

        def norm_scalar(a, l, c):
            a.wait_ge(sem(f"rs_ready{l}"), c + 1)
            for i in range(TPC, NT):
                last = nc.scalar.activation(rows[:, NT * c + i, 0:D], xres[:, NT * c + i, :], ACT.Identity,
                                            bias=nm[:, c % 2, i:i + 1], scale=rs[:, c % 2, i:i + 1])
            last.then_inc(sem(f"xn_sca{l}"), 1)

        def hi_scalar(a, l, c):
            a.wait_ge(sem(f"xT_done{l}"), c + 1)
            nc.scalar.copy(xh[:, c * CHUNK:(c + 1) * CHUNK], psum[:, c % 2, :]).then_inc(sem(f"xh_ready{l}"), 1)

        def weigh_scalar(a, l, c):
            a.wait_ge(sem(f"back_{c}"), 16 * (l + 1))
            for i in range(TPC * c, TPC * (c + 1)):
                last = nc.scalar.activation(yback[l][:, i, 1, :], yback[l][:, i, 1, :], ACT.Copy,
                                            scale=gate_wt[:, 1, i:i + 1])
            last.then_inc(sem(f"weighed{l}"), 1)

        def mixture_scalar(a, l):
            b = tb[l]

            def step(s, dyn, c):
                def w(name, count, per=1):
                    a.wait_ge(sem(name), count if dyn is None else dyn * per + count)
                if s < SLOT_TILES:
                    w(f"gT_done{l}", s + 1)
                    if s >= 2:
                        w(f"h_ready{l}", (2 if l == 0 else 1) * (s - 1), 2 if l == 0 else 1)
                    nc.scalar.copy(b.gh[:, c % 2, :], psum[:, 0, 0:P]).then_inc(sem(f"gh_ready{l}"), 1)
                if 1 <= s <= SLOT_TILES:
                    t = (c - 1) % 2
                    if l == 0:
                        w("h_ready0", 2 * s - 1, 2)
                        if s >= 3:
                            w("act_ready0", s - 2)
                        nc.scalar.activation(b.s1[:, t, :], psum[:, 1 + t, :], ACT.Silu).then_inc(
                            sem("silu_ready0"), 1)
                    else:
                        w("h_ready1", s)
                        if s >= 3:
                            w("aT_in1", s - 2)
                        nc.scalar.activation(b.act[:, t, :], psum[:, 1 + t, :], ACT.Gelu).then_inc(sem("act_ready1"), 1)
                if 2 <= s < SLOT_TILES + 2:
                    w(f"aT_in{l}", s - 1)
                    if s >= 4:
                        w(f"y_ready{l}", s - 3)
                    nc.scalar.copy(b.aT[:, c % 2, :], psum[:, 5 + c % 2, :]).then_inc(sem(f"aT_ready{l}"), 1)
                if s >= 3:
                    w(f"y_ready{l}", s - 2)
                    if s - 3 >= OUTS:
                        o = (c - 3) % OUTS
                        count = 16 * ((s - 3) // OUTS) + slot_uses(l, o)
                        a.wait_ge(sem(f"row_out_{o}"), count if dyn is None else dyn * 2 + count)
                    nc.scalar.copy(b.yo[:, (c - 3) % OUTS, :], psum[:, 7, 0:D]).then_inc(sem(f"yo_ready{l}"), 1)
            mixture_steps(a, step)

        @block.scalar
        def _(a):
            a.dma_start(wraw[:], w_cat).then_inc(sem("w_in"), 16)
            a.dma_start(la[0:LORA_RANK, :], lora_a).then_inc(sem("w_in"), 16)
            a.dma_start(lb[0:LORA_RANK, :], lora_b).then_inc(sem("w_in"), 16)
            a.dma_start(wo_raw[:], wo_t).then_inc(sem("w_in"), 16)
            a.dma_start(gw_sb[:], gate_w).then_inc(sem("gw_in"), 16)
            a.dma_start(gbias[:], gate_b.partition_broadcast(P)).then_inc(sem("gw_in"), 16)
            a.dma_start(bias_c[0:EXPERTS, 0:FF], b1).then_inc(sem("bias_in"), 16)
            a.dma_start(bias_c[0:EXPERTS, FF:NB1], b2).then_inc(sem("bias_in"), 16)
            def leave(first, end):
                for T in range(first * TPC, end * TPC, 2):
                    a.wait_ge(sem("qkv_done"), T + 1)
                    qkv_out(nc.scalar.copy, T).then_inc(sem("qkv_sca"), 1)

            root_scalar(a, 0, 0)
            norm_scalar(a, 0, 0)
            a.wait_ge(sem("w_ready"), 1)
            nc.scalar.copy(wh[:], wraw[:]).then_inc(sem("wh_ready"), 1)
            root_scalar(a, 0, 1)
            hi_scalar(a, 0, 0)
            hi_scalar(a, 0, 1)
            norm_scalar(a, 0, 1)
            root_scalar(a, 0, 2)
            hi_scalar(a, 0, 2)
            hi_scalar(a, 0, 3)
            leave(0, 2)
            norm_scalar(a, 0, 2)
            root_scalar(a, 0, 3)
            hi_scalar(a, 0, 4)
            hi_scalar(a, 0, 5)
            leave(2, 4)
            norm_scalar(a, 0, 3)
            hi_scalar(a, 0, 6)
            hi_scalar(a, 0, 7)
            leave(4, NCH)
            a.wait_ge(sem("gate_diff0"), 1)
            nc.scalar.activation(rout[0].r1[:, 4, :], rout[0].r1[:, 3, :], ACT.Exp).then_inc(sem("gate_exp0"), 1)

            def heads(n, turn, a_):
                if turn is None:
                    return QK[:, a_, n, :, :]
                flat = QK[:].rearrange("p a n x d -> p (a n x d)")
                size = TPB * HPG * HD
                return flat[:, bass.ds(turn * size + (a_ * NIT + n) * size, size)].rearrange(
                    "p (x d) -> p x d", d=HD)

            def build_hi(n, turn):
                for a_, t in ((0, tq), (1, tk)):
                    nc.scalar.copy(t[n % 2][:, :, 0:HD].bitcast(F32R), heads(n, turn, a_)).then_inc(
                        sem("tok_hi"), 1)

            def stack_unit(n, turn, w, bank, idx):
                wait(a, "ring_full", idx, PER_ALL, turn)
                kind, half = w[0], w[1]
                r = slice(half * CHUNK, (half + 1) * CHUNK)
                if kind == "k":
                    m = n + 2 if half == 0 else n + 1
                    if m >= 2:
                        wait(a, "b_full", NB * (m - 2) + (32 if half == 0 else NB), NB, turn)
                    for j in range(HPG):
                        last = nc.scalar.activation(kz[m % 2][:, j, r], psum[:, bank, :], ACT.Copy,
                                                    scale=cst[:, C_HEAD + j:C_HEAD + j + 1])
                elif kind == "q":
                    last = nc.scalar.copy(qs[n % 2][:, r], psum[:, bank, :])
                else:
                    if n >= 1:
                        wait(a, "b_full", NB * n, NB, turn)
                    last = nc.scalar.copy(qm[(n + 1) % 2][:, r], psum[:, bank, :])
                last.then_inc(sem("ring_sca"), 1)

            a.wait_ge(sem("stacks_zeroed"), 1)
            build_hi(0, None)
            a.wait_ge(sem("bz_in"), 16)
            for k, (_, w) in enumerate(FRONT):
                stack_unit(-2, None, w, k % RING, k + 1)

            def body(n, turn):
                cn = Count(n, turn)
                mine = {}
                for u, w in ring_units(n):
                    if w[0] not in by_vector:
                        mine.setdefault(u, []).append((w, cn.all % RING, cn.all + 1))
                    cn.add(w)
                for u in range(NB):
                    if n >= 0:
                        g, j = divmod(u, HPG)
                        wait(a, "b_full", NB * n + u + 1, NB, turn)
                        if n > 0 or g >= 4:
                            wait(a, "pv_done", NGROUPED * n + g - 3, NGROUPED, turn)
                        _, width, skip = b_columns(g)
                        bank = 4 + (NB * n + u) % SCORES
                        nc.scalar.activation(pT[:, (g % 4) * HPG + j, 0:width], psum[:, bank, skip:skip + width],
                                             ACT.Exp, scale=HD ** -0.5).then_inc(sem("exp_done"), 1)
                    if u == 3 and n >= 1:
                        take_outputs(n - 1, turn, 1)
                    if u == 20 and n >= 0:
                        take_outputs(n, turn, 0)
                    if u == 12 and n + 2 < NIT:
                        if n >= 0:
                            wait(a, "ring_full", all_upto(n - 1, ("m", 1)), PER_ALL, turn)
                        build_hi(n + 2, turn)
                    for w, bank, idx in mine.get(u, ()):
                        stack_unit(n, turn, w, bank, idx)

            def take_outputs(n, turn, half):
                wait(a, "pv_done", NGROUPED * n + (4 if half == 0 else NGROUPED), NGROUPED, turn)
                if n >= 1:
                    wait(a, "ring_full", all_upto(n - 1 + half, ("o", half)), PER_ALL, turn)
                nc.scalar.copy(oT[:, half * CHUNK:(half + 1) * CHUNK], psum[:, OUT, :]).then_inc(
                    sem("o_taken"), 1)

            attention_iterations(a, body)
            take_outputs(NIT - 1, None, 1)
            for c in range(NCH):
                a.wait_ge(sem("cT_done"), c + 1)
                if c >= 2:
                    a.wait_ge(sem("proj_done"), c - 1)
                nc.scalar.copy(cT[:, c % 2, :], psum[:, 2 + c % 2, :]).then_inc(sem("cT_ready"), 1)
            mixture_scalar(a, 0)
            def weigh(c):
                weigh_scalar(a, 0, 2 * c)
                weigh_scalar(a, 0, 2 * c + 1)

            def logits_out(c):
                a.wait_ge(sem("logitsT"), c + 1)
                if c >= 4:
                    a.wait_ge(sem("logits1"), c - 3)
                nc.scalar.copy(lgT[0:EXPERTS, c % 4, :], psum[0:EXPERTS, 2 + c % 4, :]).then_inc(
                    sem("logitsT_out"), 1)

            a.wait_ge(sem("gw_in"), 32)
            nc.scalar.copy(gwh[:], gw_sb[:]).then_inc(sem("gwh_ready"), 1)
            weigh(0)
            weigh(1)
            root_scalar(a, 1, 0)
            norm_scalar(a, 1, 0)
            weigh(2)
            root_scalar(a, 1, 1)
            hi_scalar(a, 1, 0)
            hi_scalar(a, 1, 1)
            norm_scalar(a, 1, 1)
            weigh(3)
            root_scalar(a, 1, 2)
            hi_scalar(a, 1, 2)
            hi_scalar(a, 1, 3)
            logits_out(0)
            logits_out(1)
            norm_scalar(a, 1, 2)
            root_scalar(a, 1, 3)
            hi_scalar(a, 1, 4)
            hi_scalar(a, 1, 5)
            norm_scalar(a, 1, 3)
            logits_out(2)
            logits_out(3)
            hi_scalar(a, 1, 6)
            hi_scalar(a, 1, 7)
            for c in range(4, NCH):
                logits_out(c)
            a.wait_ge(sem("rnn_in"), 48)
            nc.scalar.copy(rwh[:], rw[:]).then_inc(sem("rnn_hi"), 1)
            a.wait_ge(sem("v_in"), 16)
            nc.scalar.copy(V1h[:], vraw[:]).then_inc(sem("v_hi"), 1)
            a.wait_ge(sem("gate_diff1"), 4)
            nc.scalar.activation(rout[1].r1[:, 4, :], rout[1].r1[:, 3, :], ACT.Exp).then_inc(sem("gate_exp1"), 1)
            nc.scalar.activation(rout[1].lg[:], rout[1].lg[:], ACT.Exp).then_inc(sem("gate_exp1"), 1)
            for m in range(RC * NCH):
                k = m % RC
                a.wait_ge(sem("rnn_mm"), m + 1)
                if m >= 2:
                    a.wait_ge(sem("scan_done"), m - 1)
                for g, dst in ((0, gf), (1, gi), (2, gs)):
                    nc.scalar.activation(dst[:, m % 2, :], psum[:, 3 * (m % 2) + g, :], ACT.Sigmoid,
                                         bias=rnn_bias[:, g * RC + k:g * RC + k + 1]).then_inc(sem("sig_ready"), 1)
            mixture_scalar(a, 1)
            for c in range(NCH):
                weigh_scalar(a, 1, c)

        def split_product(dst, lh, ll, rh, rl, first=True):
            nc.tensor.matmul(dst, lh, rh, start=first, stop=False)
            nc.tensor.matmul(dst, ll, rh, start=False, stop=False)
            return nc.tensor.matmul(dst, lh, rl, start=False, stop=True)

        def transposes_tensor(pe, l, c):
            pe.wait_ge(sem(f"xn_vec{l}" if c % 2 == 0 else f"xn_sca{l}"), c // 2 + 1)
            if c >= 2:
                pe.wait_ge(sem(f"xl_ready{l}"), c - 1)
            for t in range(TPC):
                last = nc.tensor.transpose(psum[:, c % 2, t * P:(t + 1) * P], rows[:, TPC * c + t, 0:D], ident)
            last.then_inc(sem(f"xT_done{l}"), 1)

        def counts_tensor(pe, l):
            pe.wait_ge(sem(f"count_ready{l}"), 1)
            nc.tensor.matmul(psum[:, 7, 0:EXPERTS], cst[:, C_TRI:C_TRI + P], small[:, 0, :], start=True, stop=True)
            nc.tensor.matmul(psum[:, 7, EXPERTS:2 * EXPERTS], cst[:, C_ONES:C_ONES + P], small[:, 0, :],
                             start=True, stop=True).then_inc(sem(f"count_sums{l}"), 1)

        def mixture_tensor(pe, l):
            b = tb[l]
            W2x = W2s if l == 0 else V2s

            held = {}

            def expert(t, dyn):
                if dyn is None:
                    first, end = t // 8 * 8, min(t // 8 * 8 + 8, SLOT_TILES)
                    if held.get("rows") != "static":
                        held.clear()
                    held["rows"] = "static"
                    where = tile_expert[0:1, first:end]
                else:
                    first, end = LOOP_FROM - 4, LOOP_FROM + 7
                    if held.get("rows") != "loop":
                        held.clear()
                    held["rows"] = "loop"
                    where = tile_expert[0:1, bass.ds(dyn + first, end - first)]
                if t not in held:
                    _, values = nc.values_load_multi_w_load_instructions(
                        where, engines=[mybir.EngineType.PE], min_val=0, max_val=EXPERTS - 1,
                        skip_runtime_bounds_check_because="tile_expert is clamped to the experts on the chip")
                    held.update({first + k: x for k, x in enumerate(values)})
                return held[t]

            def step(s, dyn, c):
                def w(name, count, per=1):
                    pe.wait_ge(sem(name), count if dyn is None else dyn * per + count)
                if s < SLOT_TILES:
                    count = 16 * (s // 8 + 1) + slot_uses(l, c)
                    pe.wait_ge(sem(f"row_in_{c}"), count if dyn is None else dyn * 2 + count)
                    if s >= 1:
                        w(f"gl_ready{l}", s)
                    nc.tensor.transpose(psum[:, 0, 0:P], b.xg[:, c % 8, 0:D], ident).then_inc(sem(f"gT_done{l}"), 1)
                if 1 <= s <= SLOT_TILES:
                    t = (c - 1) % 2
                    w(f"gl_ready{l}", s)
                    cols = bass.ds(expert(s - 1, dyn) * FF, FF)
                    if s >= 3:
                        w("silu_ready0" if l == 0 else "act_ready1", s - 2)
                    pairs = ((W1h, W1l, 1), (W3h, W3l, 3)) if l == 0 else ((V1h, V1l, 1),)
                    for h, lo, bank in pairs:
                        if bank == 3 and s >= 3:
                            w("act_ready0", s - 2)
                        if l == 1:
                            nc.tensor.matmul(psum[:, bank + t, :], ones_b[:], bz[:, cols], start=True, stop=False)
                        split_product(psum[:, bank + t, :], b.gh[:, t, :], b.gl[:, t, :], h[:, cols],
                                      lo[:, cols], first=(l == 0)).then_inc(sem(f"h_ready{l}"), 1)
                if 2 <= s < SLOT_TILES + 2:
                    t = c % 2
                    w(f"act_ready{l}", s - 1)
                    if s >= 4:
                        w(f"aT_ready{l}", s - 3)
                    for k in range(FC):
                        last = nc.tensor.transpose(psum[:, 5 + t, k * P:(k + 1) * P],
                                                   b.act[:, t, k * P:(k + 1) * P], ident)
                    last.then_inc(sem(f"aT_in{l}"), 1)
                if s >= 3:
                    t = (c - 3) % 2
                    e = expert(s - 3, dyn)
                    w(f"aT_ready{l}", s - 2)
                    if s >= 4:
                        w(f"yo_ready{l}", s - 3)
                    if l == 1:
                        nc.tensor.matmul(psum[:, 7, 0:D], ones_b[:], bz[:, bass.ds(e * D + EXPERTS * FF, D)],
                                         start=True, stop=False)
                    for k in range(FC):
                        last = nc.tensor.matmul(psum[:, 7, 0:D], b.aT[:, t, k * P:(k + 1) * P],
                                                W2x[:, bass.ds(e * (FC * D) + k * D, D)],
                                                start=(k == 0 and l == 0), stop=(k == FC - 1))
                    last.then_inc(sem(f"y_ready{l}"), 1)
            mixture_steps(pe, step)

        @block.tensor
        def _(pe):
            pe.wait_ge(sem("const_in"), 16)
            pe.wait_ge(sem("w_in"), 64)
            for k in range(4):
                last = nc.tensor.matmul(psum[:, 6, k * D:(k + 1) * D], la[0:LORA_RANK, k * D:(k + 1) * D],
                                        lb[0:LORA_RANK, k * D:(k + 1) * D], start=True, stop=True)
            last.then_inc(sem("lora_prod"), 1)
            def project(first, end):
                for T in range(first * TPC, end * TPC):
                    if T % TPC == 0:
                        pe.wait_ge(sem("xl_ready0"), T // TPC + 1)
                    if T >= 4:
                        pe.wait_ge(sem("qkv_sca" if T % 2 == 0 else "qkv_vec"), T // 2 - 1)
                    t = slice(T * P, (T + 1) * P)
                    split_product(psum[:, 2 + T % 4, 0:NW], xh[:, t], xl[:, t], wh[:], wl[:]).then_inc(
                        sem("qkv_done"), 1)

            for c in range(4):
                transposes_tensor(pe, 0, c)
            pe.wait_ge(sem("wl_ready"), 1)
            project(0, 2)
            transposes_tensor(pe, 0, 4)
            transposes_tensor(pe, 0, 5)
            project(2, 4)
            transposes_tensor(pe, 0, 6)
            transposes_tensor(pe, 0, 7)
            project(4, NCH)
            counts_tensor(pe, 0)

            def ring_fill(n, turn, w, cn):
                bank = cn.all % RING
                if len(cn.hist) >= RING:
                    vec, count = cn.hist[-RING]
                    if vec:
                        wait(pe, "ring_vec", count, PER_VEC, turn)
                    else:
                        wait(pe, "ring_sca", count, PER_SCA, turn)
                cn.add(w)
                if w[0] == "A":
                    _, i, jt = w
                    m = n + 1
                    if (i, jt) == (0, 0):
                        count = upto(m - 2, ("q", 1)) if m - 2 >= -1 else len(FRONT)
                        wait(pe, "ring_sca", count, PER_SCA, turn)
                    if (i, jt) == (TPB // 2, TPB // 2):
                        wait(pe, "ring_sca", upto(n, ("k", 1)), PER_SCA, turn)
                    last = nc.tensor.matmul(psum[:, bank, :], qs[m % 2][:, i * P:(i + 1) * P],
                                            kz[m % 2][:, :, jt * P:(jt + 1) * P], start=True, stop=(i != jt))
                    if i == jt:
                        last = nc.tensor.matmul(psum[:, bank, :], ident_b[:],
                                                mask_b[:].unsqueeze(1).to_broadcast([P, HPG, P]),
                                                start=False, stop=True)
                    return last
                half = w[1]
                if w[0] == "o":
                    wait(pe, "o_taken", 2 * n + 1 - half, 2, turn)
                    src = oT[:]
                elif w[0] == "k":
                    m = n + 2 if half == 0 else n + 1
                    wait(pe, "tok_ready", m + 1, 1, turn)
                    src = tk[m % 2][:].rearrange("p x r -> p (x r)")
                elif w[0] == "q":
                    wait(pe, "tok_ready", n + 3, 1, turn)
                    src = tq[n % 2][:].rearrange("p x r -> p (x r)")
                else:
                    wait(pe, "m_ready", n + 2, 1, turn)
                    src = tq[(n + 1) % 2][:].rearrange("p x r -> p (x r)")
                for t in range(TPC):
                    c0 = (half * TPC + t) * P
                    last = nc.tensor.transpose(psum[:, bank, t * P:(t + 1) * P], src[:, c0:c0 + P], ident)
                return last

            def pv(n, turn, g):
                h, jt = GROUPED[g]
                if g in DIAG:
                    wait(pe, "diag_done", HPG * (len(DIAG) * n + DIAG.index(g) + 1), HPG * len(DIAG), turn)
                else:
                    wait(pe, "exp_done", NB * n + HPG * (g + 1), NB, turn)
                if g == 0:
                    wait(pe, "v_ready", n + 1, 1, turn)
                if jt == 0 and (n >= 1 or h == 1):
                    wait(pe, "o_taken", 2 * n + h, 2, turn)
                q0, width, _ = b_columns(g)
                o = q0 - CHUNK * h
                for j in range(HPG):
                    last = nc.tensor.matmul(psum[32 * j:32 * j + 32, OUT, o:CHUNK], Vs[n % 2][:, jt, j, :],
                                            pT[:, (g % 4) * HPG + j, 0:width],
                                            start=(jt == 0), stop=(g in (3, NGROUPED - 1)))
                last.then_inc(sem("pv_done"), 1)

            def body(n, turn):
                cn = Count(n, turn)
                fills = {}
                for u, w in ring_units(n):
                    fills.setdefault(u, []).append(w)
                for u in range(NB):
                    if n >= 0:
                        g, j = divmod(u, HPG)
                        if u == 0:
                            wait(pe, "ring_sca", upto(n - 1, ("m", 1)), PER_SCA, turn)
                        if not (n == 0 and u < SCORES):
                            wait(pe, "exp_done", NB * n + u + 1 - SCORES, NB, turn)
                        jt = GROUPED[g][1]
                        q0, width, skip = b_columns(g)
                        nc.tensor.matmul(psum[:, 4 + (NB * n + u) % SCORES, 0:width + skip],
                                         kz[n % 2][:, j, jt * P:(jt + 1) * P],
                                         qm[n % 2][:, q0 - skip:q0 + width],
                                         start=True, stop=True).then_inc(sem("b_full"), 1)
                    if u == 1 and n >= 1:
                        pv(n - 1, turn, NGROUPED - 1)
                    if n >= 0 and u % HPG == HPG - 1 and u > HPG:
                        pv(n, turn, u // HPG - 1)
                    for w in fills.get(u, ()):
                        ring_fill_signal(n, turn, w, cn)

            def ring_fill_signal(n, turn, w, cn):
                last = ring_fill(n, turn, w, cn)
                last.then_inc(sem("ring_full"), 1)

            cf = Count(-1, None)
            cf.all, cf.vec, cf.sca, cf.hist = 0, 0, 0, []
            for _, w in FRONT:
                ring_fill_signal(-2, None, w, cf)
            attention_iterations(pe, body)
            pv(NIT - 1, None, NGROUPED - 1)
            ce = Count(NIT, None)
            for _, w in BACK:
                ring_fill_signal(NIT, None, w, ce)

            pe.wait_ge(sem("exp_done"), NB * NIT)
            for c in range(NCH + 1):
                if c < NCH:
                    if c >= 2:
                        pe.wait_ge(sem("cT_ready"), c - 1)
                    pe.wait_ge(sem("cx_ready"), c + 1)
                    for t in range(TPC):
                        last = nc.tensor.transpose(psum[:, 2 + c % 2, t * P:(t + 1) * P], cx[:, TPC * c + t, :],
                                                   ident)
                    last.then_inc(sem("cT_done"), 1)
                if c >= 1:
                    k = c - 1
                    pe.wait_ge(sem("cT_ready"), k + 1)
                    if k >= 2:
                        pe.wait_ge(sem("proj_added"), k - 1)
                    for t in range(TPC):
                        last = nc.tensor.matmul(psum[:, 4 + k % 2, t * P:(t + 1) * P],
                                                cT[:, k % 2, t * P:(t + 1) * P], wo_sb[:], start=True, stop=True)
                    last.then_inc(sem("proj_done"), 1)
            pe.wait_ge(sem("w_split0"), 2 + NCH // 2)
            pe.wait_ge(sem("w2_in0"), 16)
            pe.wait_ge(sem("proj_added"), NCH)
            mixture_tensor(pe, 0)

            def logits(c):
                pe.wait_ge(sem("xl_ready1"), c + 1)
                if c >= 4:
                    pe.wait_ge(sem("logitsT_out"), c - 3)
                t = slice(c * CHUNK, (c + 1) * CHUNK)
                split_product(psum[0:EXPERTS, 2 + c % 4, :], gwh[:], gwl[:], xh[:, t], xl[:, t]).then_inc(
                    sem("logitsT"), 1)

            def logits_back(c):
                pe.wait_ge(sem("logitsT_out"), c + 1)
                for t in range(TPC):
                    T = TPC * c + t
                    last = nc.tensor.transpose(logits_at(T, T + 1),
                                               lgT[0:EXPERTS, c % 4, t * P:(t + 1) * P], ident[0:EXPERTS, 0:EXPERTS])
                last.then_inc(sem("logits1"), 1)

            for c in range(4):
                transposes_tensor(pe, 1, c)
            pe.wait_ge(sem("gwl_ready"), 1)
            logits(0)
            logits(1)
            transposes_tensor(pe, 1, 4)
            transposes_tensor(pe, 1, 5)
            logits_back(0)
            logits_back(1)
            logits(2)
            logits(3)
            transposes_tensor(pe, 1, 6)
            transposes_tensor(pe, 1, 7)
            for c in range(4, NCH):
                logits_back(c - 2)
                logits(c)
            logits_back(NCH - 2)
            logits_back(NCH - 1)
            counts_tensor(pe, 1)
            pe.wait_ge(sem("rnn_lo"), 1)
            for m in range(RC * NCH):
                c, k = m // RC, m % RC
                if m >= 2:
                    pe.wait_ge(sem("g_ready"), m - 1)
                    pe.wait_ge(sem("sig_ready"), 3 * (m - 1))
                xr = slice(c * CHUNK, (c + 1) * CHUNK)
                for g in range(3):
                    wr = slice(g * RNN_E + k * P, g * RNN_E + (k + 1) * P)
                    last = split_product(psum[:, 3 * (m % 2) + g, :], rwh[:, wr], rwl[:, wr], xh[:, xr], xl[:, xr])
                last.then_inc(sem("rnn_mm"), 1)
            for c in range(NCH):
                pe.wait_ge(sem("scan_done"), RC * (c + 1))
                if c >= 2:
                    pe.wait_ge(sem("rnn_added"), c - 1)
                for t in range(TPC):
                    T = TPC * c + t
                    for k in range(RC):
                        last = nc.tensor.matmul(psum[:, 6 + c % 2, t * D:(t + 1) * D], hT[:, k, T * P:(T + 1) * P],
                                                rwd[:, k, :], start=(k == 0), stop=(k == RC - 1))
                last.then_inc(sem("rnn_out"), 1)
            pe.wait_ge(sem("v_split"), 1)
            pe.wait_ge(sem("v2_in"), 16)
            pe.wait_ge(sem("bz_in"), 16)
            pe.wait_ge(sem("rnn_added"), NCH)
            mixture_tensor(pe, 1)

        def scatter_rows(g, l, first=0, end=TT):
            if first == 0:
                g.wait_ge(sem(f"slots_ready{l}"), 1)
                g.wait_ge(sem("pads_in"), 32)
            for i in range(first, end):
                for k in range(TOPK):
                    g.indirect_dma_start(xs[l], bass.IndirectOffsetOnAxis(ap=slot_i[:, k, i:i + 1], axis=0),
                                         rows[:, i, :], None).then_inc(sem(f"rows_sorted{l}"), 16)

        def second_choices_gpsimd(g, l):
            for c in range(NCH):
                tiles = slice(TPC * c, TPC * (c + 1))
                g.wait_ge(sem(f"first_added{l}"), c + 1)
                g.wait_ge(sem(f"weighed{l}"), c + 1)
                nc.gpsimd.tensor_tensor(xres[:, tiles, :], xres[:, tiles, :], yback[l][:, tiles, 1, :],
                                        ALU.add).then_inc(sem(f"combined{l}"), 1)

        def mixture_gpsimd(g, l):
            b = tb[l]

            def step(s, dyn, c):
                if s < 3:
                    return
                t = (c - 3) % OUTS
                g.wait_ge(sem(f"yo_ready{l}"), s - 2 if dyn is None else dyn + (s - 2))
                g.wait_ge(sem(f"dest_ready{l}"), s - 2 if dyn is None else dyn + (s - 2))
                if dyn is not None:
                    g.sem_inc(sem("pool_waited"), 1)
                g.indirect_dma_start(yc[l], bass.IndirectOffsetOnAxis(ap=destf[:, t:t + 1], axis=0),
                                     b.yo[:, t, :], None, bounds_check=TOPK * TOKENS - 1,
                                     oob_is_err=False).then_inc(sem(f"row_out_{t}"), 16)
            mixture_steps(g, step)

        @block.gpsimd
        def _(g_):
            def wait_alone(name, count, per, turn):
                wait(g_, name, count, per, turn)
                if turn is not None:
                    g_.sem_inc(sem("pool_waited"), 1)

            def heads(n, turn, a_):
                if turn is None:
                    return QK[:, a_, n, :, :]
                flat = QK[:].rearrange("p a n x d -> p (a n x d)")
                size = TPB * HPG * HD
                return flat[:, bass.ds(turn * size + (a_ * NIT + n) * size, size)].rearrange(
                    "p (x d) -> p x d", d=HD)

            def build(n, turn):
                par = n % 2
                wait_alone("tok_hi", 2 * n + 2, 2, turn)
                q, k = tq[par], tk[par]
                nc.gpsimd.tensor_tensor(q[:, :, 8:16], heads(n, turn, 0), q[:, :, 0:8], ALU.subtract)
                nc.gpsimd.tensor_copy(q[:, :, 16:24], q[:, :, 0:8])
                nc.gpsimd.memset(q[:, :, 24:26], 0.0)
                nc.gpsimd.tensor_copy(k[:, :, 8:16], k[:, :, 0:8])
                nc.gpsimd.tensor_tensor(k[:, :, 16:24], heads(n, turn, 1), k[:, :, 0:8],
                                        ALU.subtract).then_inc(sem("tok_ready"), 1)

            def values(n, turn):
                if n >= 2:
                    wait_alone("pv_done", NGROUPED * (n - 1), NGROUPED, turn)
                if turn is None:
                    src = Vn[:, n, :, :]
                else:
                    size = TPB * HPG * HD
                    src = Vn[:].rearrange("p n t r -> p (n t r)")[:, bass.ds(turn * size + n * size, size)].rearrange(
                        "p (t r) -> p t r", t=TPB)
                nc.gpsimd.tensor_copy(Vs[n % 2][:, :, :, 0:HD], src.rearrange("p t (j d) -> p t j d", j=HPG)).then_inc(
                    sem("v_ready"), 1)

            def body(n, turn):
                for u in range(NB):
                    g, j = divmod(u, HPG)
                    if n >= 0 and g in DIAG:
                        wait_alone("exp_done", NB * n + u + 1, NB, turn)
                        blk = pT[:, (g % 4) * HPG + j, 0:P]
                        nc.gpsimd.affine_select(out=blk, in_=blk, compare_op=ALU.is_ge, fill=0.0, base=0,
                                                pattern=[[1, P]], channel_multiplier=-1).then_inc(
                                                    sem("diag_done"), 1)
                    if u == 5 and n + 1 < NIT:
                        values(n + 1, turn)
                    if u == 16 and n + 2 < NIT:
                        build(n + 2, turn)
                    if turn is None and u % 4 == 2 and u >= 6:
                        if sorted_[0] < TT:
                            scatter_rows(g_, 0, sorted_[0], sorted_[0] + 1)
                            sorted_[0] += 1

            for i in range(2):
                nc.gpsimd.memset(tq[i][:], 0.0)
                nc.gpsimd.memset(tk[i][:], 0.0).then_inc(sem("stack_fill"), 1)
                nc.gpsimd.memset(Vs[i][:], 0.0).then_inc(sem("stack_fill"), 1)
            g_.wait_ge(sem("stack_fill"), 4)
            for i in range(2):
                nc.gpsimd.memset(tk[i][:, :, 24:26], 1.0)
                last = nc.gpsimd.memset(Vs[i][:, :, :, HD:HD + 1], 1.0)
            last.then_inc(sem("stacks_zeroed"), 1)
            nc.gpsimd.memset(mpart[:], -BIG).then_inc(sem("maxima_empty"), 1)
            nc.gpsimd.memset(bz[:], 0.0).then_inc(sem("bz_zeroed"), 1)
            g_.wait_ge(sem("bias_in"), 32)
            e8 = slice(0, EXPERTS)
            steps = [(bias_p[e8, 0, :], bias_c[e8, :], None), (bias_r[e8, 0, :], bias_c[e8, :], bias_p[e8, 0, :]),
                     (bias_p[e8, 1, :], bias_r[e8, 0, :], None),
                     (bias_r[e8, 1, :], bias_r[e8, 0, :], bias_p[e8, 1, :]),
                     (bias_p[e8, 2, :], bias_r[e8, 1, :], None)]
            for k, (dst, src, part) in enumerate(steps):
                if k:
                    g_.wait_ge(sem("bias_split"), k)
                ins = nc.gpsimd.tensor_copy(dst, src) if part is None else \
                    nc.gpsimd.tensor_tensor(dst, src, part, ALU.subtract)
                ins.then_inc(sem("bias_split"), 1)
            sorted_ = [0]
            build(0, None)
            attention_iterations(g_, body)
            scatter_rows(g_, 0, sorted_[0], TT)
            mixture_gpsimd(g_, 0)
            second_choices_gpsimd(g_, 0)
            scatter_rows(g_, 1)
            mixture_gpsimd(g_, 1)
            second_choices_gpsimd(g_, 1)


def kernel(**inputs):
    import concourse.bacc as bacc
    from concourse import mybir as mb
    from concourse.bass_utils import run_bass_kernel_spmd

    f = {k: np.asarray(v) for k, v in inputs.items()}

    def cat(*xs):
        return np.ascontiguousarray(np.concatenate(xs, axis=1))

    A = "L0_attn_"
    arrays = {
        "x": f[A + "x"], "consts": constants(),
        "w_cat": cat(*(f[A + "w" + n].T for n in "qkv"), f["L0_ffn_Wr"]),
        "lora_a": cat(*(f[A + "a" + n] for n in "qkvo")),
        "lora_b": cat(*(f[A + "b" + n].T for n in "qkvo")),
        "wo_t": f[A + "wo"].T,
        "W1": f["L0_ffn_W1"], "W2": f["L0_ffn_W2"], "W3": f["L0_ffn_W3"],
        "rnn_w": f["L1_attn_W"].T, "rnn_b": f["L1_attn_b"].reshape(-1, P).T, "rnn_wd": f["L1_attn_Wd"].T,
        "gate_w": f["L1_ffn_gate_w"], "gate_b": f["L1_ffn_gate_b"], "w1": f["L1_ffn_w1"], "b1": f["L1_ffn_b1"],
        "w2": f["L1_ffn_w2"], "b2": f["L1_ffn_b2"],
    }
    nc = bacc.Bacc("TRN2", target_bir_lowering=False, num_devices=1)
    feed, args = {}, []
    for name, a in arrays.items():
        a = np.ascontiguousarray(a)
        feed[f"in_{name}"] = a
        args.append(nc.dram_tensor(f"in_{name}", a.shape, mb.dt.from_np(a.dtype), kind="ExternalInput").ap())
    args.append(nc.dram_tensor("out_x", f[A + "x"].shape, mb.dt.from_np(f[A + "x"].dtype),
                               kind="ExternalOutput").ap())
    program(nc, *args)
    r = run_bass_kernel_spmd(nc, [feed], core_ids=[0])
    return r.results[0]["out_x"]
```
